# Optimizing a Trainium2 kernel written in Bass

```python
import numpy as np
import jax
import jax.numpy as jnp

def _softmax(x, axis=-1):
    return jax.nn.softmax(x, axis=axis)

def _gelu(x):
    return jax.nn.gelu(x, approximate=True)

def _silu(x):
    return jax.nn.silu(x)

def _sigmoid(x):
    return jax.nn.sigmoid(x)

def _layernorm(x, axis=-1, eps=1e-05):
    m = jnp.mean(x, axis=axis, keepdims=True)
    v = jnp.var(x, axis=axis, keepdims=True)
    return (x - m) / jnp.sqrt(v + eps)

def _scatter_add(tgt, idx, src, axis=0):
    return tgt.at[idx].add(src)

def _segment_sum(src, seg, n):
    return jax.ops.segment_sum(src, seg, n)
kernel_name = 'mk_gnn_resnorm_d4_gnn_r32_19e8a1'

def setup_inputs(seed: int=0):
    np.random.seed(seed)
    _w = jnp.asarray

    def _rec_inputs():
        import jax
        import jax.numpy as jnp
        _gk = jax.random.key(seed)
        x = -0.000202 + 1 * jax.random.normal(jax.random.fold_in(_gk, 1), (3125, 64), jnp.float32)
        src = jax.random.randint(jax.random.fold_in(_gk, 2), (100000,), 0, 3125, jnp.int32)
        dst = jnp.minimum((3125 * jax.random.uniform(jax.random.fold_in(_gk, 3), (100000,)) ** 2.0).astype(jnp.int32), 99999)
        _o = jnp.argsort(dst, stable=True)
        src = src[_o]
        dst = dst[_o]
        edge_attr_64 = 0.000189758 + 1.00013 * jax.random.normal(jax.random.fold_in(_gk, 12), (100000, 64), jnp.float32)
        edge_type_8 = jax.random.randint(jax.random.fold_in(_gk, 14), (100000,), 0, 8, jnp.int32)
        return (x, src, dst, edge_attr_64, edge_type_8)
    x, src, dst, edge_attr_64, edge_type_8 = _rec_inputs()

    def _L0_gnn_setup():
        import jax, jax.numpy as jnp
        import numpy as np
        N = 3125
        E = 50000
        H = 64
        key = jax.random.key(seed)
        k1, k2, k3, k4, k5 = jax.random.split(key, 5)
        x = jax.random.normal(k1, (N, H), dtype=jnp.float32)
        src = jax.random.randint(k2, (E,), 0, N, dtype=jnp.int32)
        off = jax.random.randint(k3, (E,), 1, N, dtype=jnp.int32)
        dst = (src + off) % N
        edge_index = jnp.stack([src, dst])
        w_i = jax.random.normal(k4, (H,), dtype=jnp.float32) / np.sqrt(H)
        w_j = jax.random.normal(k5, (H,), dtype=jnp.float32) / np.sqrt(H)
        return {'x': x, 'edge_index': edge_index, 'w_i': w_i, 'w_j': w_j}
    _L0_gnn_all = _L0_gnn_setup()
    _L0_gnn_in = {k: v for k, v in _L0_gnn_all.items() if k in ('w_i', 'w_j')}
    del _L0_gnn_all

    def _L1_gnn_setup():
        import jax, jax.numpy as jnp
        import numpy as np
        N, E, D_IN, D_H, D_OUT = (3125, 50000, 64, 64, 64)

        def _lin_params(key, d_out, d_in):
            k1, k2 = jax.random.split(key)
            s = 1.0 / np.sqrt(d_in)
            W = jax.random.uniform(k1, (d_out, d_in), jnp.float32, -s, s)
            b = jax.random.uniform(k2, (d_out,), jnp.float32, -s, s)
            return (W, b)

        def transformer_conv(x, src, dst, Wq, bq, Wk, bk, Wv, bv, Ws, bs):
            n = x.shape[0]
            q = x @ Wq.T + bq
            k = x @ Wk.T + bk
            v = x @ Wv.T + bv
            scale = 1.0 / np.sqrt(q.shape[-1])
            score = jnp.sum(q[dst] * k[src], axis=-1) * scale
            m = jax.lax.stop_gradient(jax.ops.segment_max(score, dst, num_segments=n))
            e = jnp.exp(score - m[dst])
            denom = jax.ops.segment_sum(e, dst, num_segments=n)
            alpha = e / denom[dst]
            out = jax.ops.segment_sum(alpha[:, None] * v[src], dst, num_segments=n)
            return out + (x @ Ws.T + bs)
        key = jax.random.key(seed)
        ks = jax.random.split(key, 10)
        x = jax.random.normal(ks[0], (N, D_IN), jnp.float32)
        edge_index = jax.random.randint(ks[1], (2, E), 0, N, jnp.int64)
        Wq1, bq1 = _lin_params(ks[2], D_H, D_IN)
        Wk1, bk1 = _lin_params(ks[3], D_H, D_IN)
        Wv1, bv1 = _lin_params(ks[4], D_H, D_IN)
        Ws1, bs1 = _lin_params(ks[5], D_H, D_IN)
        Wq2, bq2 = _lin_params(ks[6], D_OUT, D_H)
        Wk2, bk2 = _lin_params(ks[7], D_OUT, D_H)
        Wv2, bv2 = _lin_params(ks[8], D_OUT, D_H)
        Ws2, bs2 = _lin_params(ks[9], D_OUT, D_H)
        return dict(x=x, edge_index=edge_index, Wq1=Wq1, bq1=bq1, Wk1=Wk1, bk1=bk1, Wv1=Wv1, bv1=bv1, Ws1=Ws1, bs1=bs1, Wq2=Wq2, bq2=bq2, Wk2=Wk2, bk2=bk2, Wv2=Wv2, bv2=bv2, Ws2=Ws2, bs2=bs2)
    _L1_gnn_all = _L1_gnn_setup()
    _L1_gnn_in = {k: v for k, v in _L1_gnn_all.items() if k in ('Wq1', 'bq1', 'Wk1', 'bk1', 'Wv1', 'bv1', 'Ws1', 'bs1', 'Wq2', 'bq2', 'Wk2', 'bk2', 'Wv2', 'bv2', 'Ws2', 'bs2')}
    del _L1_gnn_all

    def _L2_gnn_setup():
        import jax, jax.numpy as jnp
        import numpy as np
        N = 50000
        E = 25000
        D_IN = 64
        D_OUT = 64
        HEADS = 8
        C = D_OUT // HEADS

        def segment_softmax(scores, seg, num_segments):
            m = jax.ops.segment_max(scores, seg, num_segments=num_segments)
            ex = jnp.exp(scores - m[seg])
            s = jax.ops.segment_sum(ex, seg, num_segments=num_segments)
            return ex / s[seg]
        key = jax.random.key(seed)
        ks = jax.random.split(key, 12)
        scale = 1.0 / np.sqrt(D_IN)
        x = jax.random.normal(ks[0], (N, D_IN), dtype=jnp.float32)
        edge_index = jax.random.randint(ks[1], (2, E), 0, N, dtype=jnp.int64)
        edge_attr = jax.random.normal(ks[2], (E, D_IN), dtype=jnp.float32)
        Wq = jax.random.normal(ks[3], (D_IN, HEADS * C), dtype=jnp.float32) * scale
        bq = jnp.zeros((HEADS * C,), dtype=jnp.float32)
        Wk = jax.random.normal(ks[4], (D_IN, HEADS * C), dtype=jnp.float32) * scale
        bk = jnp.zeros((HEADS * C,), dtype=jnp.float32)
        Wv = jax.random.normal(ks[5], (D_IN, HEADS * C), dtype=jnp.float32) * scale
        bv = jnp.zeros((HEADS * C,), dtype=jnp.float32)
        Ws = jax.random.normal(ks[6], (D_IN, HEADS * C), dtype=jnp.float32) * scale
        bs = jnp.zeros((HEADS * C,), dtype=jnp.float32)
        return {'x': x, 'edge_index': edge_index, 'edge_attr': edge_attr, 'Wq': Wq, 'bq': bq, 'Wk': Wk, 'bk': bk, 'Wv': Wv, 'bv': bv, 'Ws': Ws, 'bs': bs}
    _L2_gnn_all = _L2_gnn_setup()
    _L2_gnn_in = {k: v for k, v in _L2_gnn_all.items() if k in ('Wq', 'bq', 'Wk', 'bk', 'Wv', 'bv', 'Ws', 'bs')}
    del _L2_gnn_all

    def _L3_gnn_setup():
        import jax, jax.numpy as jnp
        import numpy as np
        C = 0.01
        EPS = 1e-06
        MIN_NORM = 1e-10
        N_NODES = 50000
        N_EDGES = 12500
        IN_FEAT = 64
        OUT_FEAT = 64
        NUM_RELS = 8
        NUM_HEADS = 4
        SQRT_C = np.sqrt(C).astype(np.float32)

        def project_to_ball(x, c=C):
            norm = jnp.maximum(jnp.linalg.norm(x, axis=-1, keepdims=True), MIN_NORM)
            maxnorm = (1.0 - 1e-05) / np.sqrt(c)
            return jnp.where(norm > maxnorm, x * (maxnorm / norm), x)

        def log_map_zero(x, c=C):
            norm = jnp.maximum(jnp.linalg.norm(x, axis=-1, keepdims=True), MIN_NORM)
            t = jnp.clip(np.sqrt(c) * norm, MIN_NORM, 1.0 - 1e-05)
            return jnp.arctanh(t) * x / t

        def exp_map_zero(v, c=C):
            norm = jnp.maximum(jnp.linalg.norm(v, axis=-1, keepdims=True), MIN_NORM)
            t = np.sqrt(c) * norm
            return jnp.tanh(t) * v / t

        def mobius_add(x, y, c=C):
            xy = jnp.sum(x * y, axis=-1, keepdims=True)
            x2 = jnp.sum(x * x, axis=-1, keepdims=True)
            y2 = jnp.sum(y * y, axis=-1, keepdims=True)
            num = (1.0 + 2.0 * c * xy + c * y2) * x + (1.0 - c * x2) * y
            den = 1.0 + 2.0 * c * xy + c ** 2 * x2 * y2
            return num / jnp.maximum(den, MIN_NORM)

        def leaky_relu(x, slope=0.2):
            return jnp.where(x > 0, x, slope * x)
        key = jax.random.key(seed)
        k1, k2, k3, k4, k5, k6, k7 = jax.random.split(key, 7)
        h = jax.random.normal(k1, (N_NODES, IN_FEAT), dtype=jnp.float32) * 0.5
        h = project_to_ball(h)
        rel_weight = jax.random.normal(k2, (NUM_RELS, NUM_HEADS, IN_FEAT, OUT_FEAT), dtype=jnp.float32) * 0.125
        attn_vec = jax.random.normal(k3, (NUM_RELS, NUM_HEADS, OUT_FEAT), dtype=jnp.float32) * 0.125
        rel_emb = jax.random.normal(k4, (NUM_RELS, IN_FEAT), dtype=jnp.float32) * 0.1
        src = jax.random.randint(k5, (N_EDGES,), 0, N_NODES, dtype=jnp.int32)
        dst = jax.random.randint(k6, (N_EDGES,), 0, N_NODES, dtype=jnp.int32)
        etype = jax.random.randint(k7, (N_EDGES,), 0, NUM_RELS, dtype=jnp.int32)
        return {'h_hyper': h, 'rel_weight': rel_weight, 'attn_vec': attn_vec, 'rel_emb': rel_emb, 'src': src, 'dst': dst, 'etype': etype}
    _L3_gnn_all = _L3_gnn_setup()
    _L3_gnn_in = {k: v for k, v in _L3_gnn_all.items() if k in ('rel_weight', 'attn_vec', 'rel_emb')}
    del _L3_gnn_all
    return {'x': x, 'src': src, 'dst': dst, 'edge_attr_64': edge_attr_64, 'edge_type_8': edge_type_8, 'L0_gnn_w_i': _L0_gnn_in['w_i'], 'L0_gnn_w_j': _L0_gnn_in['w_j'], 'L1_gnn_Wq1': _L1_gnn_in['Wq1'], 'L1_gnn_bq1': _L1_gnn_in['bq1'], 'L1_gnn_Wk1': _L1_gnn_in['Wk1'], 'L1_gnn_bk1': _L1_gnn_in['bk1'], 'L1_gnn_Wv1': _L1_gnn_in['Wv1'], 'L1_gnn_bv1': _L1_gnn_in['bv1'], 'L1_gnn_Ws1': _L1_gnn_in['Ws1'], 'L1_gnn_bs1': _L1_gnn_in['bs1'], 'L1_gnn_Wq2': _L1_gnn_in['Wq2'], 'L1_gnn_bq2': _L1_gnn_in['bq2'], 'L1_gnn_Wk2': _L1_gnn_in['Wk2'], 'L1_gnn_bk2': _L1_gnn_in['bk2'], 'L1_gnn_Wv2': _L1_gnn_in['Wv2'], 'L1_gnn_bv2': _L1_gnn_in['bv2'], 'L1_gnn_Ws2': _L1_gnn_in['Ws2'], 'L1_gnn_bs2': _L1_gnn_in['bs2'], 'L2_gnn_Wq': _L2_gnn_in['Wq'], 'L2_gnn_bq': _L2_gnn_in['bq'], 'L2_gnn_Wk': _L2_gnn_in['Wk'], 'L2_gnn_bk': _L2_gnn_in['bk'], 'L2_gnn_Wv': _L2_gnn_in['Wv'], 'L2_gnn_bv': _L2_gnn_in['bv'], 'L2_gnn_Ws': _L2_gnn_in['Ws'], 'L2_gnn_bs': _L2_gnn_in['bs'], 'L3_gnn_rel_weight': _L3_gnn_in['rel_weight'], 'L3_gnn_attn_vec': _L3_gnn_in['attn_vec'], 'L3_gnn_rel_emb': _L3_gnn_in['rel_emb']}

def reference(x, src, dst, edge_attr_64, edge_type_8, L0_gnn_w_i, L0_gnn_w_j, L1_gnn_Wq1, L1_gnn_bq1, L1_gnn_Wk1, L1_gnn_bk1, L1_gnn_Wv1, L1_gnn_bv1, L1_gnn_Ws1, L1_gnn_bs1, L1_gnn_Wq2, L1_gnn_bq2, L1_gnn_Wk2, L1_gnn_bk2, L1_gnn_Wv2, L1_gnn_bv2, L1_gnn_Ws2, L1_gnn_bs2, L2_gnn_Wq, L2_gnn_bq, L2_gnn_Wk, L2_gnn_bk, L2_gnn_Wv, L2_gnn_bv, L2_gnn_Ws, L2_gnn_bs, L3_gnn_rel_weight, L3_gnn_attn_vec, L3_gnn_rel_emb):
    import jax
    import jax.numpy as jnp

    def _L0_gnn_ref(x, edge_index, w_i, w_j):
        import jax, jax.numpy as jnp
        import numpy as np
        N = 3125
        E = 50000
        H = 64
        n = x.shape[0]
        loops = jnp.arange(n, dtype=edge_index.dtype)
        src = jnp.concatenate([edge_index[0], loops])
        dst = jnp.concatenate([edge_index[1], loops])
        s_i = x @ w_i
        s_j = x @ w_j
        e = jax.nn.leaky_relu(s_i[dst] + s_j[src], 0.01)
        e_max = jax.ops.segment_max(e, dst, num_segments=n)
        e_exp = jnp.exp(e - e_max[dst])
        denom = jax.ops.segment_sum(e_exp, dst, num_segments=n)
        alpha = e_exp / denom[dst]
        out = jax.ops.segment_sum(alpha[:, None] * x[src], dst, num_segments=n)
        return jax.nn.relu(out)

    def _L1_gnn_ref(x, edge_index, Wq1, bq1, Wk1, bk1, Wv1, bv1, Ws1, bs1, Wq2, bq2, Wk2, bk2, Wv2, bv2, Ws2, bs2):
        import jax, jax.numpy as jnp
        import numpy as np
        N, E, D_IN, D_H, D_OUT = (3125, 50000, 64, 64, 64)

        def _lin_params(key, d_out, d_in):
            k1, k2 = jax.random.split(key)
            s = 1.0 / np.sqrt(d_in)
            W = jax.random.uniform(k1, (d_out, d_in), jnp.float32, -s, s)
            b = jax.random.uniform(k2, (d_out,), jnp.float32, -s, s)
            return (W, b)

        def transformer_conv(x, src, dst, Wq, bq, Wk, bk, Wv, bv, Ws, bs):
            n = x.shape[0]
            q = x @ Wq.T + bq
            k = x @ Wk.T + bk
            v = x @ Wv.T + bv
            scale = 1.0 / np.sqrt(q.shape[-1])
            score = jnp.sum(q[dst] * k[src], axis=-1) * scale
            m = jax.lax.stop_gradient(jax.ops.segment_max(score, dst, num_segments=n))
            e = jnp.exp(score - m[dst])
            denom = jax.ops.segment_sum(e, dst, num_segments=n)
            alpha = e / denom[dst]
            out = jax.ops.segment_sum(alpha[:, None] * v[src], dst, num_segments=n)
            return out + (x @ Ws.T + bs)
        src, dst = (edge_index[0], edge_index[1])
        h = transformer_conv(x, src, dst, Wq1, bq1, Wk1, bk1, Wv1, bv1, Ws1, bs1)
        h = jax.nn.relu(h)
        h = transformer_conv(h, src, dst, Wq2, bq2, Wk2, bk2, Wv2, bv2, Ws2, bs2)
        return h

    def _L2_gnn_ref(x, edge_index, edge_attr, Wq, bq, Wk, bk, Wv, bv, Ws, bs):
        import jax, jax.numpy as jnp
        import numpy as np
        N = 50000
        E = 25000
        D_IN = 64
        D_OUT = 64
        HEADS = 8
        C = D_OUT // HEADS

        def segment_softmax(scores, seg, num_segments):
            m = jax.ops.segment_max(scores, seg, num_segments=num_segments)
            ex = jnp.exp(scores - m[seg])
            s = jax.ops.segment_sum(ex, seg, num_segments=num_segments)
            return ex / s[seg]
        n = x.shape[0]
        q = (x @ Wq + bq).reshape(n, HEADS, C)
        k = (x @ Wk + bk).reshape(n, HEADS, C)
        v = (x @ Wv + bv).reshape(n, HEADS, C)
        src = edge_index[0]
        dst = edge_index[1]
        inv_sqrt_c = np.float32(1.0 / np.sqrt(C))
        alpha = jnp.einsum('ehc,ehc->eh', q[dst], k[src]) * inv_sqrt_c
        alpha = segment_softmax(alpha, dst, n)
        agg = jax.ops.segment_sum(alpha[:, :, None] * v[src], dst, num_segments=n)
        return agg.reshape(n, HEADS * C) + (x @ Ws + bs)

    def _L3_gnn_ref(h_hyper, rel_weight, attn_vec, rel_emb, src, dst, etype):
        import jax, jax.numpy as jnp
        import numpy as np
        C = 0.01
        EPS = 1e-06
        MIN_NORM = 1e-10
        N_NODES = 50000
        N_EDGES = 12500
        IN_FEAT = 64
        OUT_FEAT = 64
        NUM_RELS = 8
        NUM_HEADS = 4
        SQRT_C = np.sqrt(C).astype(np.float32)

        def project_to_ball(x, c=C):
            norm = jnp.maximum(jnp.linalg.norm(x, axis=-1, keepdims=True), MIN_NORM)
            maxnorm = (1.0 - 1e-05) / np.sqrt(c)
            return jnp.where(norm > maxnorm, x * (maxnorm / norm), x)

        def log_map_zero(x, c=C):
            norm = jnp.maximum(jnp.linalg.norm(x, axis=-1, keepdims=True), MIN_NORM)
            t = jnp.clip(np.sqrt(c) * norm, MIN_NORM, 1.0 - 1e-05)
            return jnp.arctanh(t) * x / t

        def exp_map_zero(v, c=C):
            norm = jnp.maximum(jnp.linalg.norm(v, axis=-1, keepdims=True), MIN_NORM)
            t = np.sqrt(c) * norm
            return jnp.tanh(t) * v / t

        def mobius_add(x, y, c=C):
            xy = jnp.sum(x * y, axis=-1, keepdims=True)
            x2 = jnp.sum(x * x, axis=-1, keepdims=True)
            y2 = jnp.sum(y * y, axis=-1, keepdims=True)
            num = (1.0 + 2.0 * c * xy + c * y2) * x + (1.0 - c * x2) * y
            den = 1.0 + 2.0 * c * xy + c ** 2 * x2 * y2
            return num / jnp.maximum(den, MIN_NORM)

        def leaky_relu(x, slope=0.2):
            return jnp.where(x > 0, x, slope * x)
        E = src.shape[0]
        N = h_hyper.shape[0]
        R, H, din, dh = rel_weight.shape
        h_t = log_map_zero(h_hyper)
        h_src_t = h_t[src]
        msg_t = jnp.zeros((E, H, dh), dtype=h_hyper.dtype)
        for r in range(R):
            xr = jnp.where((etype == r)[:, None], h_src_t, 0.0)
            msg_t = msg_t + jnp.einsum('ei,hio->eho', xr, rel_weight[r])
        msg_h = exp_map_zero(msg_t)
        diff = mobius_add(h_hyper[src], -h_hyper[dst])
        diff_t = log_map_zero(diff)
        av = attn_vec[etype]
        score = leaky_relu(jnp.einsum('ed,ehd->eh', diff_t, av))
        m = jax.ops.segment_max(score, dst, num_segments=N)
        ex = jnp.exp(score - m[dst])
        denom = jax.ops.segment_sum(ex, dst, num_segments=N)
        alpha = ex / denom[dst]
        nsq = jnp.sum(msg_h * msg_h, axis=-1)
        lam = 2.0 / (1.0 - C * nsq + EPS)
        w = alpha * lam
        num = jax.ops.segment_sum(w[..., None] * msg_h, dst, num_segments=N)
        den = jax.ops.segment_sum(w, dst, num_segments=N) + EPS
        mid = project_to_ball(num / den[..., None])
        agg_t = jnp.mean(log_map_zero(mid), axis=1)
        h_new = exp_map_zero(agg_t)
        return h_new
    edge_index = jnp.stack([src, dst])
    x = _layernorm(x + _L0_gnn_ref(x, edge_index, L0_gnn_w_i, L0_gnn_w_j), axis=-1)
    x = _layernorm(x + _L1_gnn_ref(x, edge_index, L1_gnn_Wq1, L1_gnn_bq1, L1_gnn_Wk1, L1_gnn_bk1, L1_gnn_Wv1, L1_gnn_bv1, L1_gnn_Ws1, L1_gnn_bs1, L1_gnn_Wq2, L1_gnn_bq2, L1_gnn_Wk2, L1_gnn_bk2, L1_gnn_Wv2, L1_gnn_bv2, L1_gnn_Ws2, L1_gnn_bs2), axis=-1)
    x = _layernorm(x + _L2_gnn_ref(x, edge_index, edge_attr_64, L2_gnn_Wq, L2_gnn_bq, L2_gnn_Wk, L2_gnn_bk, L2_gnn_Wv, L2_gnn_bv, L2_gnn_Ws, L2_gnn_bs), axis=-1)
    x = _layernorm(x + _L3_gnn_ref(x, L3_gnn_rel_weight, L3_gnn_attn_vec, L3_gnn_rel_emb, src, dst, edge_type_8), axis=-1)
    return x

_drawn_inputs = setup_inputs


def setup_inputs(seed=0):
    import zlib

    import numpy as np

    out = dict(_drawn_inputs(seed))
    spreads = {'L2_gnn_bq': (0.0, 0.469),
     'L2_gnn_bk': (0.0, 0.8),
     'L2_gnn_bv': (0.0, 0.1),
     'L2_gnn_bs': (0.0, 0.1)}
    factors = {'L1_gnn_Wq1': 2.813,
     'L1_gnn_bq1': 8.0,
     'L1_gnn_Wk1': 2.809,
     'L1_gnn_bk1': 8.0,
     'L1_gnn_Wq2': 8.0,
     'L1_gnn_bq2': 8.0,
     'L1_gnn_Wk2': 8.0,
     'L1_gnn_bk2': 8.0}
    for name, (base, spread) in spreads.items():
        noise = np.random.default_rng([zlib.crc32(name.encode()), seed]).standard_normal(out[name].shape)
        drawn = base * np.exp(spread * noise) if base else spread * noise
        out[name] = jnp.asarray(drawn.astype(out[name].dtype))
    for name, factor in factors.items():
        out[name] = (out[name] * factor).astype(out[name].dtype)
    return out
```

```python
from contextlib import ExitStack

import numpy as np
import concourse.bass as bass
from concourse import mybir

F32 = mybir.dt.float32
I32 = mybir.dt.int32
ALU = mybir.AluOpType
ACT = mybir.ActivationFunctionType
AX = mybir.AxisListType

P = 128
N, D, E = 3125, 64, 100000
NB = -(-N // P)
NFULL = N // P
NREST = N - NFULL * P
NPAD = NB * P
G = 4
VE = G * P
U = 4
V = (E + NB * (VE - 1)) // VE
V = -(-V // U) * U
RUN = -(-V * G // P)
T = RUN * P
SL = RUN * P
EC, ER = E // P, E % P
BIG = 1.0e30
EPS = 1e-5


class Steps:

    def __init__(self, eng, sem, n=0):
        self.eng, self.sem, self.n, self.turn = eng, sem, n, None

    def __call__(self, ins):
        ins.then_inc(self.sem, 1)
        self.n += 1
        self.eng.wait_ge(self.sem, self.at())

    def at(self):
        if self.turn is None:
            return self.n
        i, base, per = self.turn
        return i * per + self.n

    def enter(self, i, per):
        self.turn = (i, self.n, per)

    def leave(self, turns):
        i, base, per = self.turn
        assert self.n - base == per, (self.n - base, per)
        self.turn = None
        self.n = base + per * turns


def rows(dram, width):
    return dram.rearrange("(b p) w -> p b w", p=P)


def build(nc, io):
    ctx = ExitStack()
    with ctx:
        m = Memory(nc, ctx)
        setup(nc, io, m)
        prep0(nc, io, m)
        pass_a(nc, io, m, 0)
        soft(nc, io, m, 0)
        pass_b(nc, io, m, 0)
        finish0(nc, io, m)
        prep_linear(nc, io, m, 1)
        pass_a(nc, io, m, 1)
        soft(nc, io, m, 1)
        pass_b(nc, io, m, 1)
        finish_linear(nc, io, m, 1)
        prep_linear(nc, io, m, 2)
        pass_a(nc, io, m, 2)
        soft(nc, io, m, 2)
        pass_b(nc, io, m, 2)
        finish_linear(nc, io, m, 2)
        prep_linear(nc, io, m, 3)
        pass_a(nc, io, m, 3)
        soft(nc, io, m, 3)
        pass_b(nc, io, m, 3)
        finish_linear(nc, io, m, 3)
        prep4(nc, io, m)
        pass_a(nc, io, m, 4)
        score4(nc, io, m)
        soft(nc, io, m, 4)
        pass_b(nc, io, m, 4)
        finish4(nc, io, m)


class Conv:

    def __init__(self, heads, block, row, spread, raw, extra=0):
        self.H, self.B, self.W, self.Q, self.R, self.X = heads, block, row, spread, raw, extra
        self.PW = heads * block


R_, H3 = 8, 4
B3 = D + 2
CONVS = [Conv(1, D + 1, D + 2, 1, 1, extra=2),
         Conv(1, D + 1, 2 * D + 1, D, 1),
         Conv(1, D + 1, 2 * D + 1, D, 1),
         Conv(8, D // 8 + 1, 8 * 9 + D, D, 8),
         Conv(H3, B3, H3 * B3 + D + 1 + H3 + R_ * H3, D + R_ * H3 + 1, 11)]


class Memory:

    def __init__(self, nc, ctx):
        def sb(name, shape, dt=F32):
            return ctx.enter_context(nc.sbuf_tensor(name, shape, dt))

        def dram(name, shape, dt=F32):
            return nc.dram_tensor(name, shape, dt, kind="Internal").ap()

        self.nc = nc
        self.sems = [[ctx.enter_context(nc.semaphore(f"bank{k}_{j}")) for j in range(24)] for k in range(2)]
        self.stages = 0
        self.gathered = [[ctx.enter_context(nc.semaphore(f"gathered{l}_{s}")) for s in range(U)] for l in range(5)]
        self.bank = [ctx.enter_context(nc.psum_tensor(f"bank{i}", [P, 512], F32)) for i in range(6)]
        self.wide = ctx.enter_context(nc.psum_tensor("wide", [P, 1024], F32))
        self.ident = sb("ident", [P, P])
        self.ones = sb("ones", [P, P])
        self.iota_p = sb("iota_p", [P, 1])
        self.iota_f = sb("iota_f", [P, P])
        self.visit_bucket = sb("visit_bucket", [1, V], I32)
        self.dl = sb("dl", [P, T])
        self.src_t = sb("src_t", [P, T], I32)
        self.s8_t = sb("s8_t", [P, T], I32)
        self.cut_f = sb("cut_f", [P, SL])
        self.cut_b = sb("cut_b", [P, SL])
        self.end = sb("end", [P, SL])
        self.row_cut = sb("row_cut", [8, 2, P])
        self.x = sb("x", [P, NB, D])
        self.h = sb("h", [P, NB, D])
        self.extra = sb("extra", [P, T, 2])
        self.skip = sb("skip", [P, NB, D])
        self.acc = sb("acc", [P, NB + 1, H3 * B3])
        self.spread = sb("spread", [P, NB + 1, D + R_ * H3 + 1])
        self.raw = sb("raw", [P, T * 11])
        self.wt = sb("wt", [P, T * 8])
        self.flat_dl = dram("flat_dl", [T * P])
        self.table = [dram(f"table{l}", [NPAD * (R_ if l == 4 else 1), c.W]) for l, c in enumerate(CONVS)]
        self.spill = [dram(f"spill{l}", [V, P, G * c.PW]) for l, c in enumerate(CONVS)]


    def stage_sems(self):
        mine, other = self.sems[self.stages % 2], self.sems[1 - self.stages % 2]
        if self.stages:
            lo = min(s.num for s in other)
            assert max(s.num for s in other) == lo + len(other) - 1
            self.nc.sync.sem_clear(range(lo, lo + len(other)))
        self.stages += 1
        left = list(mine)
        return lambda name: left.pop(0)


def setup(nc, io, m):
    ctx = ExitStack()
    with ctx:
        def sb(name, shape, dt=F32):
            return ctx.enter_context(nc.sbuf_tensor("st_" + name, shape, dt))

        sem = m.stage_sems()

        def dram(name, shape, dt=F32):
            return nc.dram_tensor(name, shape, dt, kind="Internal").ap()

        VH = (V + 1) // 2
        dst_i, src_i, typ_i = (sb(n, [P, EC + 1], I32) for n in ("dst_i", "src_i", "typ_i"))
        dst_f, junk = sb("dst_f", [P, EC + 1]), sb("junk", [P, EC + 1])
        s8_i = sb("s8_i", [P, EC + 1], I32)
        cnt = sb("cnt", [P, NB + 1])
        row = sb("row", [1, 12, NB + 1])
        rowi = sb("rowi", [1, 2, NB + 1], I32)
        col = sb("col", [NB, 2])
        iota_i = sb("iota_i", [P, 256], I32)
        iota_pi = sb("iota_pi", [P, 1], I32)
        iota_v = sb("iota_v", [NB, V])
        iota_vc = sb("iota_vc", [VH, 2])
        past = sb("past", [NB, V])
        e0 = sb("e0", [VH, 4])
        e0_i = sb("e0_i", [VH, 2], I32)
        bv = sb("bv", [P, V])
        pad = sb("pad", [1, 3, VE], I32)
        gat = [[sb(f"gat{a}{h}", [VH, VE], I32) for h in range(2)] for a in range(3)]
        tail = sb("tail", [T - V * G, 3, P], I32)
        scan_i = [sb(f"scan_i{a}", [P, SL], I32) for a in range(3)]
        part = [m.raw[:, k * T:(k + 1) * T] for k in range(10)]
        scan_f, (dst_t, key_t, ok, key_s, prev_s, next_s, dl_s) = part[0:3], part[3:10]
        edge2 = sb("edge2", [1, 2])
        rc = sb("rc", [P, 2, 8])
        lin = [dram(f"lin{a}", [E + VE], I32) for a in range(3)]
        flat = [dram(f"flat{a}", [T * P], I32) for a in range(3)]
        flat_key = dram("flat_key", [T * P + 2])

        loaded, pool_step, consts = sem("loaded"), sem("pool_step"), sem("consts")
        dve_step, dve_done, pe_done = sem("dve_step"), sem("dve_done"), sem("pe_done")
        stored, gathered, flat_in, key_io, turned = (sem("stored"), ctx.enter_context(nc.semaphore("gathered")), sem("flat_in"),
                                                     sem("key_io"), sem("turned"))
        flat_out, x_in = sem("flat_out"), sem("x_in")
        block = ctx.enter_context(nc.Block())

        def edges(a):
            return a[0:P * EC].rearrange("(p c) -> p c", p=P), a[P * EC:E].rearrange("(p c) -> p c", c=1)

        @block.sync
        def _(sp):
            for tile, name in ((dst_i, "dst"), (src_i, "src"), (typ_i, "edge_type_8")):
                body, rest = edges(io[name])
                sp.dma_start(tile[:, 0:EC], body).then_inc(loaded, 16)
                sp.dma_start(tile[0:ER, EC:EC + 1], rest).then_inc(loaded, 16)
            xin = io["x"]
            sp.wait_ge(dve_done, 1)
            sp.dma_start(m.x[:, 0:NFULL, :], xin[0:NFULL * P, :].rearrange("(b p) d -> p b d", p=P)).then_inc(x_in, 16)
            sp.dma_start(m.x[0:NREST, NFULL, :], xin[NFULL * P:N, :]).then_inc(x_in, 16)
            sp.wait_ge(dve_done, 2)
            for a, tile in enumerate((dst_i, src_i, s8_i)):
                body, rest = edges(lin[a][0:E])
                sp.dma_start(body, tile[:, 0:EC]).then_inc(stored, 16)
                sp.dma_start(rest, tile[0:ER, EC:EC + 1]).then_inc(stored, 16)
                sp.dma_start(lin[a][E:E + VE].rearrange("(o w) -> o w", o=1), pad[:, a, :]).then_inc(stored, 16)
                sp.dma_start(flat[a][V * VE:T * P].rearrange("(t p) -> t p", p=P), tail[:, a, :]).then_inc(flat_out, 16)
            sp.wait_ge(gathered, 96)
            for a in range(3):
                for h in range(2):
                    n = min(VH, V - h * VH)
                    sp.dma_start(flat[a][h * VH * VE:(h * VH + n) * VE].rearrange("(v e) -> v e", e=VE),
                                 gat[a][h][0:n, :]).then_inc(flat_out, 16)
            sp.wait_ge(flat_out, 16 * 9)
            for a in range(3):
                sp.dma_start(scan_i[a][:, :], flat[a].rearrange("(p e) -> p e", p=P)).then_inc(flat_in, 16)
            sp.wait_ge(dve_done, 5)
            sp.dma_start(flat_key[1:1 + T * P].rearrange("(p e) -> p e", p=P), key_s[:, :]).then_inc(key_io, 16)
            sp.dma_start(flat_key[0:1].rearrange("(o w) -> o w", o=1), edge2[:, 0:1]).then_inc(key_io, 16)
            sp.dma_start(flat_key[T * P + 1:T * P + 2].rearrange("(o w) -> o w", o=1), edge2[:, 1:2]).then_inc(key_io, 16)
            sp.dma_start(m.flat_dl.rearrange("(p e) -> p e", p=P), dl_s[:, :]).then_inc(key_io, 16)
            sp.wait_ge(key_io, 64)
            sp.dma_start(prev_s[:, :], flat_key[0:T * P].rearrange("(p e) -> p e", p=P)).then_inc(key_io, 16)
            sp.dma_start(next_s[:, :], flat_key[2:T * P + 2].rearrange("(p e) -> p e", p=P)).then_inc(key_io, 16)

        @block.gpsimd
        def _(pool):
            step = Steps(pool, pool_step)
            step(pool.memset(m.ident[:, :], 0.0))
            step(pool.affine_select(out=m.ident[:, :], in_=m.ident[:, :], compare_op=ALU.not_equal, fill=1.0,
                                    base=0, pattern=[[-1, P]], channel_multiplier=1))
            step(pool.iota(iota_i[:, :], [[1, 256]], base=0, channel_multiplier=0))
            pool.memset(m.ones[:, :], 1.0).then_inc(consts, 1)
            pool.iota(iota_pi[:, :], [[0, 1]], base=0, channel_multiplier=1).then_inc(consts, 1)
            pool.wait_ge(dve_done, 3)
            pool.wait_ge(stored, 16 * 9)
            for a in range(3):
                for h in range(2):
                    n = min(VH, V - h * VH)
                    pool.indirect_dma_start(gat[a][h][0:n, :], None, lin[a].rearrange("(n o) -> n o", o=1),
                                            bass.IndirectOffsetOnAxis(ap=e0_i[0:n, h:h + 1], axis=0)).then_inc(gathered, 16)

        @block.vector
        def _(dve):
            step = Steps(dve, dve_step)
            step(dve.memset(m.x[:, :, :], 0.0))
            dve.nop(nofuse=True).then_inc(dve_done, 1)
            step(dve.memset(pad[:, 0, :], NPAD))
            step(dve.memset(pad[:, 1:3, :], 0))
            step(dve.memset(tail[:, 0, :], NPAD))
            step(dve.memset(tail[:, 1:3, :], 0))
            step(dve.memset(edge2[:, :], -1000.0))
            step(dve.memset(cnt[:, :], 0.0))
            step(dve.memset(dst_f[:, :], 1.0e9))
            dve.wait_ge(loaded, 16 * 6)
            step(dve.tensor_scalar(s8_i[:, 0:EC], src_i[:, 0:EC], float(R_), None, ALU.mult))
            step(dve.tensor_scalar(s8_i[0:ER, EC:EC + 1], src_i[0:ER, EC:EC + 1], float(R_), None, ALU.mult))
            step(dve.tensor_tensor(s8_i[:, 0:EC], s8_i[:, 0:EC], typ_i[:, 0:EC], ALU.add))
            step(dve.tensor_tensor(s8_i[0:ER, EC:EC + 1], s8_i[0:ER, EC:EC + 1], typ_i[0:ER, EC:EC + 1], ALU.add))
            dve.nop(nofuse=True).then_inc(dve_done, 1)
            step(dve.tensor_copy(dst_f[:, 0:EC], dst_i[:, 0:EC]))
            step(dve.tensor_copy(dst_f[0:ER, EC:EC + 1], dst_i[0:ER, EC:EC + 1]))
            for b in range(1, NB + 1):
                step(dve.tensor_scalar(junk[:, :], dst_f[:, :], float(P * b), 0.0, ALU.is_lt, ALU.add,
                                       accum_out=cnt[:, b:b + 1]))
            dve.wait_ge(consts, 2)
            step(dve.tensor_copy(m.iota_p[:, :], iota_pi[:, :]))
            step(dve.tensor_copy(m.iota_f[:, :], iota_i[:, 0:P]))
            step(dve.tensor_copy(iota_v[:, :], iota_i[0:NB, 0:V]))
            dve.nop(nofuse=True).then_inc(turned, 1)
            dve.wait_ge(pe_done, 1)
            start, n, nv, vs, g, dg = (row[:, k, :] for k in range(6))
            step(dve.tensor_copy(start, m.bank[0][0:1, 0:NB + 1]))
            step(dve.tensor_tensor(n[:, 0:NB], start[:, 1:NB + 1], start[:, 0:NB], ALU.subtract))
            step(dve.tensor_scalar(rowi[:, 0, 0:NB], n[:, 0:NB], float(VE - 1), None, ALU.add))
            step(dve.tensor_scalar(rowi[:, 1, 0:NB], rowi[:, 0, 0:NB], VE.bit_length() - 1, None, ALU.arith_shift_right))
            step(dve.tensor_copy(nv[:, 0:NB], rowi[:, 1, 0:NB]))
            step(dve.memset(vs[:, 0:1], 0.0))
            step(dve.tensor_tensor_scan(vs[:, 1:NB + 1], m.ones[0:1, 0:NB], nv[:, 0:NB], 0.0, ALU.mult, ALU.add))
            step(dve.scalar_tensor_tensor(g, vs, float(-VE), start, ALU.mult, ALU.add))
            step(dve.tensor_tensor(dg[:, 0:NB], g[:, 1:NB + 1], g[:, 0:NB], ALU.subtract))
            dve.nop(nofuse=True).then_inc(turned, 1)
            dve.wait_ge(pe_done, 2)
            step(dve.tensor_copy(col[:, :], m.bank[1][0:NB, 0:2]))
            step(dve.tensor_scalar(past[:, :], iota_v[:, :], col[:, 0:1], None, ALU.is_ge))
            dve.nop(nofuse=True).then_inc(turned, 1)
            dve.wait_ge(pe_done, 3)
            step(dve.tensor_copy(bv[:, :], m.bank[2][:, 0:V]))
            step(dve.tensor_copy(m.visit_bucket[:, :], bv[0:1, :]))
            step(dve.tensor_copy(iota_vc[:, 0:1], m.iota_p[0:VH, :]))
            step(dve.tensor_scalar(iota_vc[:, 1:2], m.iota_p[0:VH, :], float(VH), None, ALU.add))
            step(dve.tensor_copy(e0[:, 0:2], m.bank[3][0:VH, 0:2]))
            step(dve.scalar_tensor_tensor(e0[:, 2:4], iota_vc[:, :], float(VE), e0[:, 0:2], ALU.mult, ALU.add))
            step(dve.tensor_scalar(e0_i[:, :], e0[:, 2:4], float(E), 0.0, ALU.min, ALU.max))
            dve.nop(nofuse=True).then_inc(dve_done, 1)
            dve.wait_ge(flat_in, 48)
            for a in range(3):
                step(dve.tensor_copy(scan_f[a][:, :], scan_i[a][:, :]))
            dve.nop(nofuse=True).then_inc(turned, 1)
            outs = (dst_t, m.src_t, m.s8_t)
            for a in range(3):
                dve.wait_ge(pe_done, 4 + a)
                step(dve.tensor_copy(outs[a][:, :].rearrange("p (i k) -> p k i", k=RUN),
                                     m.wide[:, 0:SL].rearrange("p (k i) -> p k i", k=RUN)))
                dve.nop(nofuse=True).then_inc(turned, 1)
            step(dve.memset(m.dl[:, :], float(P)))
            step(dve.scalar_tensor_tensor(
                m.dl[:, 0:V * G].rearrange("p (v g) -> p v g", g=G),
                bv[:, :].unsqueeze(2).to_broadcast([P, V, G]), float(-P),
                dst_t[:, 0:V * G].rearrange("p (v g) -> p v g", g=G), ALU.mult, ALU.add))
            step(dve.tensor_scalar(ok[:, :], m.dl[:, :], float(P), None, ALU.is_lt))
            step(dve.scalar_tensor_tensor(m.dl[:, :], m.dl[:, :], 1.0, ok[:, :], ALU.add, ALU.mult))
            step(dve.tensor_scalar(m.dl[:, :], m.dl[:, :], -1.0, None, ALU.add))
            step(dve.tensor_copy(key_t[:, :], m.dl[:, :]))
            step(dve.scalar_tensor_tensor(
                key_t[:, 0:V * G].rearrange("p (v g) -> p v g", g=G),
                bv[:, :].unsqueeze(2).to_broadcast([P, V, G]), float(P + 2),
                m.dl[:, 0:V * G].rearrange("p (v g) -> p v g", g=G), ALU.mult, ALU.add))
            dve.nop(nofuse=True).then_inc(dve_done, 1)
            for k, o in enumerate((key_s, dl_s)):
                dve.wait_ge(pe_done, 7 + k)
                step(dve.tensor_copy(o[:, :], m.wide[:, 0:SL]))
                dve.nop(nofuse=True).then_inc(turned, 1)
            dve.nop(nofuse=True).then_inc(dve_done, 1)
            dve.wait_ge(key_io, 96)
            step(dve.tensor_tensor(m.cut_f[:, :], key_s[:, :], prev_s[:, :], ALU.not_equal))
            step(dve.tensor_tensor(m.end[:, :], key_s[:, :], next_s[:, :], ALU.not_equal))
            step(dve.tensor_scalar(m.cut_f[:, :], m.cut_f[:, :], -BIG, None, ALU.mult))
            step(dve.tensor_scalar(m.cut_b[:, :], m.end[:, :], -BIG, None, ALU.mult))
            for k, cut in enumerate((m.cut_f, m.cut_b)):
                step(dve.tensor_reduce(rc[:, k, 0:1], cut[:, :], AX.X, ALU.min))
                step(dve.tensor_copy(rc[:, k, 1:8], rc[:, k, 0:1].to_broadcast([P, 7])))
            dve.nop(nofuse=True).then_inc(turned, 1)
            dve.wait_ge(pe_done, 9)
            step(dve.tensor_copy(m.row_cut[:, :, :], m.bank[4][0:8, 0:2 * P].rearrange("h (k p) -> h k p", k=2)))
            dve.wait_ge(x_in, 32)

        @block.tensor
        def _(pe):
            pe.wait_ge(turned, 1)
            pe.matmul(m.bank[0][0:1, 0:NB + 1], m.ones[:, 0:1], cnt[:, :], start=True, stop=True).then_inc(pe_done, 1)
            pe.wait_ge(turned, 2)
            pe.matmul(m.bank[1][0:NB, 0:1], row[:, 3, 1:NB + 1], m.ones[0:1, 0:1], start=True, stop=True)
            pe.matmul(m.bank[1][0:NB, 1:2], row[:, 5, 0:NB], m.ones[0:1, 0:1], start=True, stop=True).then_inc(pe_done, 1)
            pe.wait_ge(turned, 3)
            pe.matmul(m.bank[2][:, 0:V], m.ones[0:NB, :], past[:, :], start=True, stop=True)
            for h in range(2):
                n = min(VH, V - h * VH)
                mm = pe.matmul(m.bank[3][0:n, h:h + 1], past[:, h * VH:h * VH + n], col[:, 1:2], start=True, stop=True)
            mm.then_inc(pe_done, 1)
            pe.wait_ge(turned, 4)
            for a in range(3):
                if a:
                    pe.wait_ge(turned, 4 + a)
                turn_blocks(pe, m, [scan_f[a][:, k * P:(k + 1) * P] for k in range(RUN)]).then_inc(pe_done, 1)
            pe.wait_ge(dve_done, 4)
            for k, t in enumerate((key_t, m.dl)):
                pe.wait_ge(turned, 7 + k)
                turn_blocks(pe, m, [t[:, :].rearrange("p (i k) -> p k i", k=RUN)[:, j, :] for j in range(RUN)])\
                    .then_inc(pe_done, 1)
            pe.wait_ge(turned, 10)
            for k in range(2):
                mm = pe.transpose(m.bank[4][0:8, k * P:(k + 1) * P], rc[:, k, :], m.ident[:, :])
            mm.then_inc(pe_done, 1)


def turn_blocks(pe, m, blocks):
    for k, b in enumerate(blocks):
        at = k * P
        ins = pe.transpose(m.wide[:, at:at + P], b, m.ident[:, :])
    return ins


def prep0(nc, io, m):
    c = CONVS[0]
    with ExitStack() as ctx:
        sb = lambda n, s, dt=F32: ctx.enter_context(nc.sbuf_tensor("p0_" + n, s, dt))
        sem = m.stage_sems()
        w = sb("w", [P, 2, D])
        tb = sb("tb", [P, NB, c.W])
        prod = sb("prod", [P, NB, D])
        w_in, step_sem, made, out_sem = sem("w_in"), sem("step"), sem("made"), sem("out")
        block = ctx.enter_context(nc.Block())

        @block.sync
        def _(sp):
            sp.dma_start(w[:, :, :], io["wij"].rearrange("(o k) d -> o k d", o=1).to_broadcast([P, 2, D])).then_inc(w_in, 16)
            sp.wait_ge(made, 1)
            sp.dma_start(rows(m.table[0], c.W), tb[:, :, :]).then_inc(out_sem, 16)
            sp.wait_ge(out_sem, 16)

        @block.vector
        def _(dve):
            step = Steps(dve, step_sem)
            step(dve.memset(m.spread[:, :, 0:1], 0.0))
            step(dve.tensor_copy(tb[:, :, 0:D], m.x[:, :, :]))
            step(dve.memset(tb[:, :, D:D + 1], 1.0))
            dve.wait_ge(w_in, 16)
            for k, out in enumerate((m.spread[:, 0:NB, 0:1], tb[:, :, D + 1:D + 2])):
                step(dve.tensor_tensor(prod[:, :, :], m.x[:, :, :], w[:, k:k + 1, :].to_broadcast([P, NB, D]), ALU.mult))
                step(dve.tensor_reduce(out, prod[:, :, :], AX.X, ALU.add))
            dve.nop(nofuse=True).then_inc(made, 1)


def prep_linear(nc, io, m, l):
    c = CONVS[l]
    inp = m.h if l == 2 else m.x
    with ExitStack() as ctx:
        sb = lambda n, s, dt=F32: ctx.enter_context(nc.sbuf_tensor(f"pl{l}_" + n, s, dt))
        sem = m.stage_sems()
        w = sb("w", [D + 1, 4 * D])
        xt = sb("xt", [D + 1, 2, P])
        tb = sb("tb", [P, NB, c.W])
        w_in, ready, turned, moved = sem("w_in"), sem("ready"), sem("turned"), sem("moved")
        product, taken_d, taken_a, out_sem = sem("product"), sem("taken_d"), sem("taken_a"), sem("out")
        block = ctx.enter_context(nc.Block())
        vb = D // c.H
        payload = tb[:, :, 0:c.PW].rearrange("p b (h v) -> p b h v", h=c.H)

        @block.sync
        def _(sp):
            sp.dma_start(w[:, :], io[f"W{l}"]).then_inc(w_in, 16)
            sp.wait_ge(taken_d, NB)
            sp.wait_ge(taken_a, NB)
            sp.dma_start(rows(m.table[l], c.W), tb[:, :, :]).then_inc(out_sem, 16)
            sp.wait_ge(out_sem, 16)

        @block.gpsimd
        def _(pool):
            step = Steps(pool, ready)
            step(pool.memset(xt[D:D + 1, :, :], 1.0))
            step(pool.memset(payload[:, :, :, vb:vb + 1], 1.0))
            step(pool.memset(m.spread[:, NB:NB + 1, :], 0.0))

        @block.tensor
        def _(pe):
            pe.wait_ge(w_in, 16)
            pe.wait_ge(ready, 3)
            for b in range(NB + 1):
                if b < NB:
                    if b >= 2:
                        pe.wait_ge(moved, b - 1)
                    pe.transpose(m.bank[b % 2][0:D, 0:P], inp[:, b, :], m.ident[:, :]).then_inc(turned, 1)
                if b >= 1:
                    k = b - 1
                    pe.wait_ge(moved, k + 1)
                    if k >= 2:
                        pe.wait_ge(taken_d, k - 1)
                        pe.wait_ge(taken_a, k - 1)
                    pe.matmul(m.bank[2 + k % 2][:, 0:4 * D], xt[:, k % 2, :], w[:, :], start=True, stop=True)\
                        .then_inc(product, 1)

        @block.scalar
        def _(act):
            for b in range(NB + 1):
                if b < NB:
                    act.wait_ge(turned, b + 1)
                    if b >= 2:
                        act.wait_ge(product, b - 1)
                    act.copy(xt[0:D, b % 2, :], m.bank[b % 2][0:D, 0:P]).then_inc(moved, 1)
                if b >= 1:
                    k = b - 1
                    act.wait_ge(product, k + 1)
                    act.copy(payload[:, k, :, 0:vb],
                             m.bank[2 + k % 2][:, 2 * D:3 * D].rearrange("p (h v) -> p h v", h=c.H)).then_inc(taken_a, 1)

        @block.vector
        def _(dve):
            dve.wait_ge(ready, 3)
            for b in range(NB):
                dve.wait_ge(taken_a, b + 1)
                bank = m.bank[2 + b % 2]
                dve.tensor_copy(m.spread[:, b, 0:D], bank[:, 0:D])
                dve.tensor_copy(tb[:, b, c.PW:c.W], bank[:, D:2 * D])
                dve.tensor_copy(m.skip[:, b, :], bank[:, 3 * D:4 * D]).then_inc(taken_d, 1)


def pass_a(nc, io, m, l):
    c = CONVS[l]
    W, Q, R, PW = c.W, c.Q, c.R, c.PW
    TURNS = V // U
    idx = m.s8_t if l == 4 else m.src_t
    raw = m.raw[:, 0:T * R]
    with ExitStack() as ctx:
        sb = lambda n, s, dt=F32: ctx.enter_context(nc.sbuf_tensor(f"a{l}_" + n, s, dt))
        sem = m.stage_sems()
        stage = sb("stage", [P, U, G], I32)
        g = sb("g", [P, U, G, W])
        dlrow = sb("dlrow", [1, U, VE])
        oh = sb("oh", [P, 2, VE])
        prod = sb("prod", [P, G, D])
        prod2 = sb("prod2", [P, G, R_ * H3])
        staged, gathered = sem("staged"), m.gathered[l]
        row_in, spilled = [sem(f"row_in{s}") for s in range(U)], [sem(f"spilled{s}") for s in range(U)]
        widened, onehot, spread, scored, score_step = (sem("widened"), sem("onehot"), sem("spread"), sem("scored"),
                                                       sem("score_step"))
        copied = sem("copied")
        padded = sem("padded")
        block = ctx.enter_context(nc.Block())

        def flat_row(v):
            return m.flat_dl[bass.ds(v * VE, VE)].rearrange("(o w) -> o w", o=1)

        @block.scalar
        def _(act):
            def copy_indices(v, s):
                act.copy(stage[:, s, :], idx[:, bass.ds(v * G, G)]).then_inc(staged, 1)

            def take_sides(i, s):
                v = i * U + s
                act.wait_ge(scored, v + 1)
                out = raw[:, bass.ds(v * (G * R), G * R)].rearrange("p (g r) -> p g r", r=R)
                bank = m.bank[2 + s % 2][:, 0:G * Q].rearrange("p (g q) -> p g q", q=Q)
                act.copy(out[:, :, 1:2], bank[:, :, Q - 1:Q])
                act.copy(out[:, :, 6:11], g[:, s, :, PW + D:PW + D + 5]).then_inc(copied, 1)

            for s in range(U):
                copy_indices(s, s)

            def turn(i, last):
                for s in range(U):
                    if not last:
                        act.wait_ge(gathered[s], (i + 1) * (16 * G))
                        copy_indices((i + 1) * U + s, s)
                    if l == 4:
                        take_sides(i, s)
            with act.Fori(0, TURNS - 1) as i:
                turn(i, False)
            turn(TURNS - 1, True)

        @block.gpsimd
        def _(pool):
            if V * G < T:
                pool.memset(raw[:, V * G * R:T * R], 0.0).then_inc(padded, 1)

            def turn(i, first):
                for s in range(U):
                    pool.wait_ge(staged, i * U + s + 1)
                    pool.nop(nofuse=True)
                    if not first:
                        pool.wait_ge(scored, i * U + (s + 1 - U))
                        pool.nop(nofuse=True)
                        if l == 4:
                            pool.wait_ge(copied, i * U + (s + 1 - U))
                            pool.nop(nofuse=True)
                        pool.wait_ge(spilled[s], i * 16)
                        pool.nop(nofuse=True)
                    for j in range(G):
                        pool.indirect_dma_start(g[:, s, j, :], None, m.table[l],
                                                bass.IndirectOffsetOnAxis(ap=stage[:, s, j:j + 1], axis=0))\
                            .then_inc(gathered[s], 16)
            turn(0, True)
            with pool.Fori(1, TURNS) as i:
                turn(i, False)
            pool.wait_ge(padded, 1)

        @block.sync
        def _(sp):
            for s in range(U):
                sp.dma_start(dlrow[:, s, :], flat_row(s)).then_inc(row_in[s], 16)

            def turn(i, last):
                for s in range(U):
                    v = i * U + s
                    if not last:
                        sp.wait_ge(widened, v + 1)
                        sp.dma_start(dlrow[:, s, :], flat_row(v + U)).then_inc(row_in[s], 16)
                    sp.wait_ge(gathered[s], (i + 1) * (16 * G))
                    sp.dma_start(m.spill[l][bass.ds(v, 1), :, :].rearrange("o p (g w) -> (o p) g w", w=PW),
                                 g[:, s, :, 0:PW]).then_inc(spilled[s], 16)
            with sp.Fori(0, TURNS - 1) as i:
                turn(i, False)
            turn(TURNS - 1, True)
            for s in range(U):
                sp.wait_ge(spilled[s], 16 * TURNS)

        @block.tensor
        def _(pe):
            def widen(i, s, first):
                pe.wait_ge(row_in[s % U], (i + s // U) * 16 + 16)
                if not (first and s < 2):
                    pe.wait_ge(onehot, i * U + s - 1)
                pe.matmul(m.bank[s % 2][:, :], m.ones[0:1, :], dlrow[:, s % U, :], start=True, stop=True)\
                    .then_inc(widened, 1)

            def turn(i, first, last):
                for s in range(U):
                    if not (last and s == U - 1):
                        widen(i, s + 1, first)
                    v = i * U + s
                    b = pe.value_load(m.visit_bucket[0:1, bass.ds(v, 1)], min_val=0, max_val=NB)
                    pe.wait_ge(onehot, v + 1)
                    if not (first and s < 2):
                        pe.wait_ge(scored, v - 1)
                        if l == 4:
                            pe.wait_ge(copied, v - 1)
                    for j in range(G):
                        mm = pe.matmul(m.bank[2 + s % 2][:, j * Q:(j + 1) * Q], oh[:, s % 2, j * P:(j + 1) * P],
                                       m.spread[:, bass.ds(b, 1), 0:Q], start=True, stop=True)
                    mm.then_inc(spread, 1)
            widen(0, 0, True)
            turn(0, True, False)
            with pe.Fori(1, TURNS - 1) as i:
                turn(i, False, False)
            turn(TURNS - 1, False, True)

        @block.vector
        def _(dve):
            def compare(i, s, first):
                dve.wait_ge(widened, i * U + s + 1)
                if not (first and s < 2):
                    dve.wait_ge(spread, i * U + s - 1)
                dve.tensor_scalar(oh[:, s % 2, :], m.bank[s % 2][:, :], m.iota_p[:, 0:1], None, ALU.is_equal)\
                    .then_inc(onehot, 1)

            def score(i, s, step):
                v = i * U + s
                dve.wait_ge(spread, v + 1)
                dve.wait_ge(gathered[s], (i + 1) * (16 * G))
                bank = m.bank[2 + s % 2][:, 0:G * Q].rearrange("p (g q) -> p g q", q=Q)
                out = raw[:, bass.ds(v * (G * R), G * R)].rearrange("p (g r) -> p g r", r=R)
                if l == 0:
                    dve.tensor_tensor(out, bank, g[:, s, :, W - 1:W], ALU.add).then_inc(scored, 1)
                    return
                if l == 4:
                    step(dve.tensor_tensor(prod2[:, :, :], bank[:, :, D:D + R_ * H3], g[:, s, :, W - R_ * H3:W], ALU.mult))
                    step(dve.tensor_reduce(out[:, :, 2:6], prod2[:, :, :].rearrange("p g (r h) -> p g h r", h=H3), AX.X, ALU.add))
                step(dve.tensor_tensor(prod[:, :, :], bank[:, :, 0:D], g[:, s, :, PW:PW + D], ALU.mult))
                if l == 3:
                    dve.tensor_reduce(out, prod[:, :, :].rearrange("p g (h c) -> p g h c", h=c.H), AX.X, ALU.add)\
                        .then_inc(scored, 1)
                else:
                    dve.tensor_reduce(out[:, :, 0:1], prod[:, :, :], AX.X, ALU.add).then_inc(scored, 1)
                dve.wait_ge(scored, v + 1)

            step = Steps(dve, score_step)

            def turn(i, first, last):
                for s in range(U):
                    if not (last and s == U - 1):
                        compare(i, s + 1, first)
                    score(i, s, step)
            per = U * {0: 0, 4: 3}.get(l, 1)
            compare(0, 0, True)
            turn(0, True, False)
            with dve.Fori(1, TURNS - 1) as i:
                step.enter(i - 1, per)
                turn(i, False, False)
            step.leave(TURNS - 2)
            turn(TURNS - 1, False, True)


def soft(nc, io, m, l):
    c = CONVS[l]
    H = c.H
    scale = {0: 1.0, 1: float(D) ** -0.5, 2: float(D) ** -0.5, 3: float(D // 8) ** -0.5, 4: 1.0}[l]
    raw = (m.wt if l == 4 else m.raw)[:, 0:T * H].rearrange("p (t h) -> p t h", h=H)
    wt = m.wt[:, 0:T * H].rearrange("p (t h) -> p t h", h=H)
    with ExitStack() as ctx:
        sb = lambda n, s, dt=F32: ctx.enter_context(nc.sbuf_tensor(f"s{l}_" + n, s, dt))
        sem = m.stage_sems()
        S = sb("S", [P, H, SL])
        f, b = sb("f", [P, SL]), sb("b", [P, SL])
        ex = sb("ex", [P, 3 if l == 0 else 1, SL])
        last = sb("last", [P, 2, H])
        lrow = sb("lrow", [H, 2, P])
        crow = sb("crow", [H, 2, P + 1])
        carry = sb("carry", [P, 2, H])
        turned, scanned_in, step_sem, ready = sem("turned"), sem("scan_in"), sem("step"), sem("ready")
        carried, shifted, weighed, back, back_out = (sem("carried"), sem("shifted"), sem("weighed"), sem("back"),
                                                     sem("back_out"))
        block = ctx.enter_context(nc.Block())
        NBACK = H + (2 if l == 0 else 0)

        @block.tensor
        def _(pe):
            if l == 0:
                pe.wait_ge(ready, 1)
            for h in range(H):
                if h:
                    pe.wait_ge(scanned_in, h)
                col = raw[:, :, h].rearrange("p (i k) -> p k i", k=RUN)
                turn_blocks(pe, m, [col[:, k, :] for k in range(RUN)]).then_inc(turned, 1)
            pe.wait_ge(carried, 1)
            for k in range(2):
                mm = pe.transpose(m.bank[0][0:H, k * P:(k + 1) * P], last[:, k, :], m.ident[:, :])
            mm.then_inc(turned, 1)
            pe.wait_ge(carried, 2)
            for k in range(2):
                mm = pe.transpose(m.bank[1][:, k * H:(k + 1) * H], crow[:, k, k:k + P], m.ident[0:H, 0:H])
            mm.then_inc(turned, 1)
            for n in range(NBACK):
                pe.wait_ge(weighed, n + 1)
                if n:
                    pe.wait_ge(back_out, n)
                turn_blocks(pe, m, [ex[:, n if l == 0 else 0, k * P:(k + 1) * P] for k in range(RUN)]).then_inc(back, 1)

        @block.scalar
        def _(act):
            for h in range(H):
                act.wait_ge(turned, h + 1)
                act.copy(S[:, h, :], m.wide[:, 0:SL]).then_inc(scanned_in, 1)
            for n in range(NBACK):
                if n < H:
                    act.wait_ge(shifted, n + 1)
                    if n:
                        act.wait_ge(back, n)
                    act.activation(ex[:, 0, :], S[:, n, :], ACT.Exp, scale=scale).then_inc(weighed, 1)
                else:
                    if n == H:
                        act.wait_ge(ready, 2)
                    act.nop(nofuse=True).then_inc(weighed, 1)
                act.wait_ge(back, n + 1)
                out = wt[:, :, n] if n < H else m.extra[:, :, n - H]
                act.copy(out.rearrange("p (i k) -> p k i", k=RUN),
                         m.wide[:, 0:SL].rearrange("p (k i) -> p k i", k=RUN)).then_inc(back_out, 1)

        @block.vector
        def _(dve):
            step = Steps(dve, step_sem)
            if l == 0:
                step(dve.scalar_tensor_tensor(m.raw[:, 0:T], m.raw[:, 0:T], 0.01, m.raw[:, 0:T], ALU.mult, ALU.max))
                dve.nop(nofuse=True).then_inc(ready, 1)
            for h in range(H):
                dve.wait_ge(scanned_in, h + 1)
                step(dve.tensor_tensor_scan(f[:, :], m.cut_f[:, :], S[:, h, :], -BIG, ALU.add, ALU.max))
                step(dve.tensor_tensor_scan(b[:, ::-1], m.cut_b[:, ::-1], S[:, h, ::-1], -BIG, ALU.add, ALU.max))
                step(dve.tensor_copy(last[:, 0, h:h + 1], f[:, SL - 1:SL]))
                step(dve.tensor_copy(last[:, 1, h:h + 1], b[:, 0:1]))
            dve.nop(nofuse=True).then_inc(carried, 1)
            dve.wait_ge(turned, H + 1)
            step(dve.tensor_copy(lrow[:, :, :], m.bank[0][0:H, 0:2 * P].rearrange("h (k p) -> h k p", k=2)))
            step(dve.memset(crow[:, :, :], -BIG))
            step(dve.tensor_tensor_scan(crow[:, 0, 1:P + 1], m.row_cut[0:H, 0, :], lrow[:, 0, :], -BIG, ALU.add, ALU.max))
            step(dve.tensor_tensor_scan(crow[:, 1, P - 1::-1], m.row_cut[0:H, 1, ::-1], lrow[:, 1, ::-1], -BIG,
                                        ALU.add, ALU.max))
            dve.nop(nofuse=True).then_inc(carried, 1)
            dve.wait_ge(turned, H + 2)
            step(dve.tensor_copy(carry[:, :, :], m.bank[1][:, 0:2 * H].rearrange("p (k h) -> p k h", k=2)))
            for h in range(H):
                step(dve.tensor_tensor_scan(f[:, :], m.cut_f[:, :], S[:, h, :], carry[:, 0, h:h + 1], ALU.add, ALU.max))
                step(dve.tensor_tensor_scan(b[:, ::-1], m.cut_b[:, ::-1], S[:, h, ::-1], carry[:, 1, h:h + 1],
                                            ALU.add, ALU.max))
                step(dve.tensor_tensor(f[:, :], f[:, :], b[:, :], ALU.max))
                step(dve.tensor_tensor(S[:, h, :], S[:, h, :], f[:, :], ALU.subtract))
                dve.nop(nofuse=True).then_inc(shifted, 1)
            if l == 0:
                step(dve.tensor_tensor(ex[:, 1, :], f[:, :], m.end[:, :], ALU.mult))
                step(dve.tensor_copy(ex[:, 2, :], m.end[:, :]))
                dve.nop(nofuse=True).then_inc(ready, 1)


def pass_b(nc, io, m, l):
    c = CONVS[l]
    H, B, PW, X = c.H, c.B, c.PW, c.X
    AW = PW + X
    TURNS = V // U
    with ExitStack() as ctx:
        sb = lambda n, s, dt=F32: ctx.enter_context(nc.sbuf_tensor(f"b{l}_" + n, s, dt))
        sem = m.stage_sems()
        pay = sb("pay", [P, U, G * PW])
        oh = sb("oh", [P, 2, G, P])
        wp = sb("wp", [P, 2, G, AW])
        pay_in = [sem(f"pay_in{s}") for s in range(U)]
        cleared, weighted, summed, added, sides = (sem("cleared"), sem("weighted"), sem("summed"), sem("added"),
                                                   sem("sides"))
        block = ctx.enter_context(nc.Block())

        @block.sync
        def _(sp):
            def load(v, s):
                sp.dma_start(pay[:, s, :], m.spill[l][bass.ds(v, 1), :, :].rearrange("o p w -> (o p) w"))\
                    .then_inc(pay_in[s], 16)
            for s in range(U):
                load(s, s)
            with sp.Fori(0, TURNS - 1) as i:
                for s in range(U):
                    sp.wait_ge(weighted, i * U + s + 1)
                    load((i + 1) * U + s, s)

        @block.gpsimd
        def _(pool):
            pool.memset(m.acc[:, :, 0:AW], 0.0).then_inc(cleared, 1)

        @block.scalar
        def _(act):
            if l == 0:
                def copy_sides(i, s, first):
                    v = i * U + s
                    if not (first and s < 2):
                        act.wait_ge(summed, v - 1)
                    act.copy(wp[:, s % 2, :, PW:AW], m.extra[:, bass.ds(v * G, G), :]).then_inc(sides, 1)
                for s in range(U):
                    copy_sides(0, s, True)
                with act.Fori(1, TURNS) as i:
                    for s in range(U):
                        copy_sides(i, s, False)

        @block.tensor
        def _(pe):
            def turn(i, first):
                for s in range(U):
                    v = i * U + s
                    pe.wait_ge(weighted, v + 1)
                    if l == 0:
                        pe.wait_ge(sides, v + 1)
                    if not (first and s < 2):
                        pe.wait_ge(added, v - 1)
                    for j in range(G):
                        mm = pe.matmul(m.bank[s % 2][:, 0:AW], oh[:, s % 2, j, :], wp[:, s % 2, j, :],
                                       start=(j == 0), stop=(j == G - 1))
                    mm.then_inc(summed, 1)
            turn(0, True)
            with pe.Fori(1, TURNS) as i:
                turn(i, False)

        @block.vector
        def _(dve):
            def weigh(i, s, first):
                v = i * U + s
                if not (first and s < 2):
                    dve.wait_ge(summed, v - 1)
                dve.tensor_tensor(oh[:, s % 2, :, :], m.iota_f[:, :].unsqueeze(1).to_broadcast([P, G, P]),
                                  m.dl[:, bass.ds(v * G, G)].unsqueeze(2).to_broadcast([P, G, P]), ALU.is_equal)
                dve.wait_ge(pay_in[s], (i + 1) * 16)
                w = m.wt[:, bass.ds(v * (G * H), G * H)].unsqueeze(2).to_broadcast([P, G * H, B])
                out = wp[:, s % 2, :, 0:PW]
                if X:
                    out = out.rearrange("p g (h b) -> p (g h) b", h=1) if H == 1 else out
                else:
                    out = wp[:, s % 2, :, :].rearrange("p g (h b) -> p (g h) b", h=H)
                dve.tensor_tensor(out, pay[:, s, :].rearrange("p (g b) -> p g b", b=B), w, ALU.mult).then_inc(weighted, 1)

            def add(i, s):
                v = i * U + s
                b = dve.value_load(m.visit_bucket[0:1, bass.ds(v, 1)], min_val=0, max_val=NB)
                dve.wait_ge(summed, v + 1)
                acc = m.acc[:, bass.ds(b, 1), 0:AW]
                dve.tensor_tensor(acc, acc, m.bank[s % 2][:, 0:AW].unsqueeze(1), ALU.add).then_inc(added, 1)
                dve.wait_ge(added, v + 1)

            dve.wait_ge(cleared, 1)
            weigh(0, 0, True)
            for s in range(U - 1):
                weigh(0, s + 1, True)
                add(0, s)
            with dve.Fori(1, TURNS) as i:
                for s in range(U):
                    weigh(i, s, False)
                    if s:
                        add(i, s - 1)
                    else:
                        add(i - 1, U - 1)
            add(TURNS - 1, U - 1)


def layer_norm(dve, step, m, y, sq, st, ask, answered):
    mean, var, rstd = (st[:, k, :].unsqueeze(2) for k in range(3))
    step(dve.tensor_reduce(mean, y[:, :, :], AX.X, ALU.add))
    step(dve.tensor_scalar(mean, mean, 1.0 / D, None, ALU.mult))
    step(dve.tensor_tensor(y[:, :, :], y[:, :, :], mean.to_broadcast([P, NB, D]), ALU.subtract))
    step(dve.tensor_tensor(sq[:, :, :], y[:, :, :], y[:, :, :], ALU.mult))
    step(dve.tensor_reduce(var, sq[:, :, :], AX.X, ALU.add))
    step(dve.tensor_scalar(var, var, 1.0 / D, EPS, ALU.mult, ALU.add))
    dve.nop(nofuse=True).then_inc(ask, 1)
    dve.wait_ge(*answered)
    step(dve.reciprocal(rstd, var))
    step(dve.tensor_tensor(m.x[:, :, :], y[:, :, :], rstd.to_broadcast([P, NB, D]), ALU.mult))


def finish0(nc, io, m):
    with ExitStack() as ctx:
        sb = lambda n, s, dt=F32: ctx.enter_context(nc.sbuf_tensor("f0_" + n, s, dt))
        sem = m.stage_sems()
        y, sq = sb("y", [P, NB, D]), sb("sq", [P, NB, D])
        w, sj, pr = sb("w", [P, D]), sb("sj", [P, NB]), sb("pr", [P, NB, D])
        st = sb("st", [P, 12, NB])
        w_in, step_sem, ask, ans = sem("w_in"), sem("step"), sem("ask"), sem("answered")
        block = ctx.enter_context(nc.Block())

        @block.sync
        def _(sp):
            sp.dma_start(w[:, :], io["wij"][1:2, :].to_broadcast([P, D])).then_inc(w_in, 16)

        @block.scalar
        def _(act):
            act.wait_ge(ask, 1)
            act.activation(st[:, 6:8, :], st[:, 4:6, :], ACT.Exp).then_inc(ans, 1)
            act.wait_ge(ask, 2)
            act.activation(st[:, 1, :], st[:, 1, :], ACT.Sqrt).then_inc(ans, 1)

        @block.vector
        def _(dve):
            step = Steps(dve, step_sem)
            dve.wait_ge(w_in, 16)
            acc = m.acc[:, 0:NB, :]
            own, most, top = st[:, 8, :], st[:, 9, :], st[:, 10, :]
            step(dve.tensor_tensor(pr[:, :, :], m.x[:, :, :], w[:, :].unsqueeze(1).to_broadcast([P, NB, D]), ALU.mult))
            step(dve.tensor_reduce(own.unsqueeze(2), pr[:, :, :], AX.X, ALU.add))
            step(dve.tensor_tensor(own, own, m.spread[:, 0:NB, 0], ALU.add))
            step(dve.scalar_tensor_tensor(own, own, 0.01, own, ALU.mult, ALU.max))
            step(dve.tensor_scalar(most, acc[:, :, D + 2], BIG, -BIG, ALU.mult, ALU.add))
            step(dve.tensor_tensor(most, most, acc[:, :, D + 1], ALU.add))
            step(dve.tensor_tensor(top, most, own, ALU.max))
            step(dve.tensor_tensor(st[:, 4, :], most, top, ALU.subtract))
            step(dve.tensor_tensor(st[:, 5, :], own, top, ALU.subtract))
            step(dve.tensor_scalar(st[:, 4:6, :], st[:, 4:6, :], -200.0, None, ALU.max))
            dve.nop(nofuse=True).then_inc(ask, 1)
            dve.wait_ge(ans, 1)
            fac, one = st[:, 6, :], st[:, 7, :]
            den = st[:, 11, :]
            step(dve.tensor_tensor(den, acc[:, :, D], fac, ALU.mult))
            step(dve.tensor_tensor(den, den, one, ALU.add))
            step(dve.reciprocal(den, den))
            step(dve.tensor_tensor(fac, fac, den, ALU.mult))
            step(dve.tensor_tensor(one, one, den, ALU.mult))
            step(dve.tensor_tensor(y[:, :, :], acc[:, :, 0:D], fac.unsqueeze(2).to_broadcast([P, NB, D]), ALU.mult))
            step(dve.tensor_tensor(sq[:, :, :], m.x[:, :, :], one.unsqueeze(2).to_broadcast([P, NB, D]), ALU.mult))
            step(dve.tensor_tensor(y[:, :, :], y[:, :, :], sq[:, :, :], ALU.add))
            step(dve.scalar_tensor_tensor(y[:, :, :], y[:, :, :], 0.0, m.x[:, :, :], ALU.max, ALU.add))
            layer_norm(dve, step, m, y, sq, st, ask, (ans, 2))


def finish_linear(nc, io, m, l):
    c = CONVS[l]
    H, B = c.H, c.B
    with ExitStack() as ctx:
        sb = lambda n, s, dt=F32: ctx.enter_context(nc.sbuf_tensor(f"f{l}_" + n, s, dt))
        sem = m.stage_sems()
        y, sq = sb("y", [P, NB, D]), sb("sq", [P, NB, D])
        st, den = sb("st", [P, 3, NB]), sb("den", [P, NB, H])
        step_sem, ask, ans = sem("step"), sem("ask"), sem("answered")
        block = ctx.enter_context(nc.Block())

        @block.scalar
        def _(act):
            if l != 1:
                act.wait_ge(ask, 1)
                act.activation(st[:, 1, :], st[:, 1, :], ACT.Sqrt).then_inc(ans, 1)

        @block.vector
        def _(dve):
            step = Steps(dve, step_sem)
            acc = m.acc[:, 0:NB, 0:c.PW].rearrange("p n (h b) -> p n h b", h=H)
            step(dve.tensor_scalar(den[:, :, :], acc[:, :, :, B - 1], 1.0e-20, None, ALU.max))
            step(dve.reciprocal(den[:, :, :], den[:, :, :]))
            step(dve.tensor_tensor(y[:, :, :].rearrange("p n (h b) -> p n h b", h=H), acc[:, :, :, 0:B - 1],
                                   den[:, :, :].unsqueeze(3).to_broadcast([P, NB, H, B - 1]), ALU.mult))
            step(dve.tensor_tensor(y[:, :, :], y[:, :, :], m.skip[:, :, :], ALU.add))
            if l == 1:
                step(dve.tensor_scalar(m.h[:, :, :], y[:, :, :], 0.0, None, ALU.max))
                return
            step(dve.tensor_tensor(y[:, :, :], y[:, :, :], m.x[:, :, :], ALU.add))
            layer_norm(dve, step, m, y, sq, st, ask, (ans, 1))


ATANH_TERMS = [1.0 / (2 * k + 1) for k in range(9)]


def atanh_ratio(dve, step, t, lo, up, u, poly, out, ask, answered):
    dve.nop(nofuse=True).then_inc(ask, 1)
    step(dve.tensor_tensor(u, t, t, ALU.mult))
    step(dve.tensor_scalar(poly, u, ATANH_TERMS[-1], ATANH_TERMS[-2], ALU.mult, ALU.add))
    for a in ATANH_TERMS[-3::-1]:
        step(dve.tensor_tensor(poly, poly, u, ALU.mult))
        step(dve.tensor_scalar(poly, poly, a, None, ALU.add))
    dve.wait_ge(*answered)
    step(dve.tensor_tensor(up, up, lo, ALU.subtract))
    step(dve.reciprocal(lo, t))
    step(dve.scalar_tensor_tensor(up, up, 0.5, lo, ALU.mult, ALU.mult))
    step(dve.tensor_scalar(u, t, 0.25, None, ALU.is_lt))
    step(dve.tensor_tensor(poly, poly, up, ALU.subtract))
    step(dve.tensor_tensor(poly, poly, u, ALU.mult))
    step(dve.tensor_tensor(out, up, poly, ALU.add))


CURV, MIN_NORM, TOP = 0.01, 1e-10, 1.0 - 1e-5
ROOT_C = 0.1


def prep4(nc, io, m):
    c = CONVS[4]
    W, PW = c.W, c.PW
    RH = R_ * H3
    with ExitStack() as ctx:
        sb = lambda n, s, dt=F32: ctx.enter_context(nc.sbuf_tensor("p4_" + n, s, dt))
        sem = m.stage_sems()
        w, av = sb("w", [D, RH * D]), sb("av", [D, RH])
        ht = sb("ht", [P, NB, D])
        st = sb("st", [P, 8, NB])
        xt = sb("xt", [D, 2, P])
        rb = sb("rb", [P, 2, R_, W])
        sq = sb("sq", [P, 4, 512])
        ms = sb("ms", [P, 8, RH])
        ohr = sb("ohr", [P, RH * R_], I32)
        w_in, step_sem, ask, ans, ready = sem("w_in"), sem("step"), sem("ask"), sem("answered"), sem("ready")
        turned, moved, product, row_out = sem("turned"), sem("moved"), sem("product"), [sem("row_out0"), sem("row_out1")]
        rowed, squared, tanhed = sem("rowed"), sem("squared"), sem("tanhed")
        normed, made = sem("normed"), sem("made")
        block = ctx.enter_context(nc.Block())

        @block.sync
        def _(sp):
            sp.dma_start(w[:, :], io["Wrel"]).then_inc(w_in, 16)
            sp.dma_start(av[:, :], io["AV"]).then_inc(w_in, 16)
            tab = m.table[4].rearrange("(b p r) w -> b p (r w)", p=P, r=R_)
            for b in range(NB):
                sp.wait_ge(rowed, b + 1)
                sp.dma_start(tab[b], rb[:, b % 2, :, :].rearrange("p r w -> p (r w)")).then_inc(row_out[b % 2], 16)
            sp.wait_ge(row_out[0], 16 * ((NB + 1) // 2))
            sp.wait_ge(row_out[1], 16 * (NB // 2))

        @block.gpsimd
        def _(pool):
            step = Steps(pool, ready)
            step(pool.iota(ohr[:, :], [[-1, R_], [1, R_], [0, H3]], base=0, channel_multiplier=0))
            step(pool.memset(m.spread[:, NB:NB + 1, :], 0.0))

        @block.scalar
        def _(act):
            act.wait_ge(ask, 1)
            act.activation(st[:, 1, :], st[:, 0, :], ACT.Sqrt).then_inc(ans, 1)
            act.wait_ge(ask, 2)
            act.activation(st[:, 3, :], st[:, 2, :], ACT.Ln, bias=1.0)
            act.activation(st[:, 4, :], st[:, 2, :], ACT.Ln, bias=1.0, scale=-1.0).then_inc(ans, 1)
            for b in range(NB):
                act.wait_ge(turned, b + 1)
                act.copy(xt[:, 0, :], m.bank[0][0:D, 0:P])
                act.copy(xt[:, 1, :], m.bank[0][0:D, P:2 * P]).then_inc(moved, 1)
                act.wait_ge(product, b + 1)
                if b:
                    act.wait_ge(made, 2 * b - 1)
                for k in range(4):
                    ins = act.activation(sq[:, k, :], m.bank[2 + k][:, :], ACT.Square)
                ins.then_inc(squared, 1)
                act.wait_ge(made, 2 * b + 1)
                act.activation(ms[:, 1, :], ms[:, 0, :], ACT.Sqrt).then_inc(normed, 1)
                act.wait_ge(made, 2 * b + 2)
                act.activation(ms[:, 3, :], ms[:, 2, :], ACT.Tanh).then_inc(tanhed, 1)

        @block.tensor
        def _(pe):
            pe.wait_ge(w_in, 32)
            pe.wait_ge(ask, 3)
            for b in range(NB):
                if b:
                    pe.wait_ge(moved, b)
                pe.transpose(m.bank[0][0:D, 0:P], ht[:, b, :], m.ident[:, :])
                pe.transpose(m.bank[0][0:D, P:2 * P], m.x[:, b, :], m.ident[:, :]).then_inc(turned, 1)
                pe.wait_ge(moved, b + 1)
                if b:
                    pe.wait_ge(rowed, b)
                for k in range(4):
                    pe.matmul(m.bank[2 + k][:, :], xt[:, 0, :], w[:, k * 512:(k + 1) * 512], start=True, stop=True)
                pe.matmul(m.bank[1][:, 0:RH], xt[:, 1, :], av[:, :], start=True, stop=True).then_inc(product, 1)

        @block.vector
        def _(dve):
            step = Steps(dve, step_sem)
            n2, nrm, t, up, lo, u, poly, ratio = (st[:, k, :] for k in range(8))
            step(dve.tensor_tensor(ht[:, :, :], m.x[:, :, :], m.x[:, :, :], ALU.mult))
            step(dve.tensor_reduce(n2.unsqueeze(2), ht[:, :, :], AX.X, ALU.add))
            step(dve.tensor_copy(m.spread[:, 0:NB, D + RH], n2))
            step(dve.tensor_copy(m.spread[:, 0:NB, 0:D], m.x[:, :, :]))
            step(dve.tensor_scalar(n2, n2, 1e-30, None, ALU.max))
            dve.nop(nofuse=True).then_inc(ask, 1)
            dve.wait_ge(ans, 1)
            step(dve.tensor_scalar(nrm, nrm, MIN_NORM, None, ALU.max))
            step(dve.tensor_scalar(t, nrm, ROOT_C, MIN_NORM, ALU.mult, ALU.max))
            step(dve.tensor_scalar(t, t, TOP, None, ALU.min))
            atanh_ratio(dve, step, t, lo, up, u, poly, ratio, ask, (ans, 2))
            step(dve.tensor_tensor(ht[:, :, :], m.x[:, :, :], ratio.unsqueeze(2).to_broadcast([P, NB, D]), ALU.mult))
            dve.nop(nofuse=True).then_inc(ask, 1)
            dve.wait_ge(ready, 2)
            for s in range(2):
                step(dve.tensor_scalar(rb[:, s, :, W - RH:W], ohr[:, :].rearrange("p (r k) -> p r k", r=R_), 0.0, None,
                                       ALU.is_equal))
                blocks = rb[:, s, :, 0:PW].rearrange("p r (h k) -> p r h k", h=H3)
                step(dve.memset(blocks[:, :, :, B3 - 1:B3], 1.0))
            a = [ms[:, k, :] for k in range(8)]
            for b in range(NB):
                s = b % 2
                if b >= 2:
                    dve.wait_ge(row_out[s], 16 * (b // 2))
                blocks = rb[:, s, :, 0:PW].rearrange("p r (h k) -> p r h k", h=H3)
                step(dve.tensor_copy(rb[:, s, :, PW:PW + D], m.x[:, b:b + 1, :].to_broadcast([P, R_, D])))
                step(dve.tensor_copy(rb[:, s, :, PW + D:PW + D + 1],
                                     m.spread[:, b:b + 1, D + RH:D + RH + 1].to_broadcast([P, R_, 1])))
                dve.wait_ge(squared, b + 1)
                step(dve.tensor_reduce(a[0].unsqueeze(2), sq[:, :, :].rearrange("p k (q o) -> p (k q) o", o=D), AX.X, ALU.add))
                step(dve.tensor_scalar(a[7], a[0], 1e-30, None, ALU.max))
                step(dve.tensor_copy(a[0], a[7]))
                dve.nop(nofuse=True).then_inc(made, 1)
                step(dve.tensor_copy(m.spread[:, b, D:D + RH], m.bank[1][:, 0:RH]))
                step(dve.tensor_copy(rb[:, s, :, PW + D + 1:PW + D + 1 + H3],
                                     m.bank[1][:, 0:RH].rearrange("p (r h) -> p r h", h=H3)))
                dve.wait_ge(normed, b + 1)
                step(dve.tensor_scalar(a[2], a[1], MIN_NORM, ROOT_C, ALU.max, ALU.mult))
                dve.nop(nofuse=True).then_inc(made, 1)
                step(dve.reciprocal(a[4], a[2]))
                dve.wait_ge(tanhed, b + 1)
                step(dve.tensor_tensor(a[4], a[3], a[4], ALU.mult))
                step(dve.tensor_tensor(a[5], a[4], a[4], ALU.mult))
                step(dve.tensor_tensor(a[5], a[5], a[0], ALU.mult))
                step(dve.tensor_scalar(a[5], a[5], -CURV, 1.0, ALU.mult, ALU.add))
                step(dve.tensor_scalar(a[5], a[5], 1e-6, 0.5, ALU.add, ALU.mult))
                step(dve.reciprocal(a[6], a[5]))
                step(dve.tensor_tensor(a[4], a[4], a[6], ALU.mult))
                step(dve.tensor_copy(blocks[:, :, :, D], a[6].rearrange("p (r h) -> p r h", h=H3)))
                for k in range(4):
                    fac = a[4].rearrange("p (r h) -> p r h", h=H3)[:, 2 * k:2 * k + 2, :]
                    step(dve.tensor_tensor(blocks[:, 2 * k:2 * k + 2, :, 0:D],
                                           m.bank[2 + k][:, :].rearrange("p (r h o) -> p r h o", r=2, h=H3),
                                           fac.unsqueeze(3).to_broadcast([P, 2, H3, D]), ALU.mult))
                dve.nop(nofuse=True).then_inc(rowed, 1)


def score4(nc, io, m):
    with ExitStack() as ctx:
        sb = lambda n, s, dt=F32: ctx.enter_context(nc.sbuf_tensor("q4_" + n, s, dt))
        sem = m.stage_sems()
        v = [sb(f"v{k}", [P, T]) for k in range(10)]
        step_sem, ask, ans = sem("step"), sem("ask"), sem("answered")
        block = ctx.enter_context(nc.Block())

        @block.scalar
        def _(act):
            act.wait_ge(ask, 1)
            act.activation(v[4][:, :], v[3][:, :], ACT.Sqrt).then_inc(ans, 1)
            act.wait_ge(ask, 2)
            act.activation(v[5][:, :], v[4][:, :], ACT.Ln, bias=1.0)
            act.activation(v[6][:, :], v[4][:, :], ACT.Ln, bias=1.0, scale=-1.0).then_inc(ans, 1)

        @block.vector
        def _(dve):
            step = Steps(dve, step_sem)
            raw = m.raw[:, :].rearrange("p (t r) -> p t r", r=11)
            dot, y2, x2 = raw[:, :, 0], raw[:, :, 1], raw[:, :, 6]
            A, B, den, n2, t, up, lo, u, poly, f = (k[:, :] for k in v)
            stt, ts, tt = dve.scalar_tensor_tensor, dve.tensor_scalar, dve.tensor_tensor
            step(ts(f, dot, -2.0 * CURV, 1.0, ALU.mult, ALU.add))
            step(stt(A, y2, CURV, f, ALU.mult, ALU.add))
            step(ts(B, x2, -CURV, 1.0, ALU.mult, ALU.add))
            step(stt(den, x2, CURV * CURV, y2, ALU.mult, ALU.mult))
            step(tt(den, den, f, ALU.add))
            step(ts(den, den, MIN_NORM, None, ALU.max))
            step(dve.reciprocal(den, den))
            step(tt(A, A, den, ALU.mult))
            step(tt(B, B, den, ALU.mult))
            step(tt(n2, A, A, ALU.mult))
            step(tt(n2, n2, x2, ALU.mult))
            step(tt(u, A, B, ALU.mult))
            step(stt(u, u, -2.0, dot, ALU.mult, ALU.mult))
            step(tt(n2, n2, u, ALU.add))
            step(tt(u, B, B, ALU.mult))
            step(tt(u, u, y2, ALU.mult))
            step(tt(n2, n2, u, ALU.add))
            step(ts(n2, n2, 1e-30, None, ALU.max))
            dve.nop(nofuse=True).then_inc(ask, 1)
            dve.wait_ge(ans, 1)
            step(ts(t, t, MIN_NORM, ROOT_C, ALU.max, ALU.mult))
            step(ts(t, t, MIN_NORM, TOP, ALU.max, ALU.min))
            atanh_ratio(dve, step, t, lo, up, u, poly, f, ask, (ans, 2))
            step(tt(A, A, f, ALU.mult))
            step(tt(B, B, f, ALU.mult))
            out = m.wt[:, 0:T * H3].rearrange("p (t h) -> p t h", h=H3)
            for h in range(H3):
                step(tt(u, A, raw[:, :, 7 + h], ALU.mult))
                step(tt(poly, B, raw[:, :, 2 + h], ALU.mult))
                step(tt(u, u, poly, ALU.subtract))
                step(stt(out[:, :, h], u, 0.2, u, ALU.mult, ALU.max))


def finish4(nc, io, m):
    NH = NB * H3
    with ExitStack() as ctx:
        sb = lambda n, s, dt=F32: ctx.enter_context(nc.sbuf_tensor("f4_" + n, s, dt))
        sem = m.stage_sems()
        y, sq, st = sb("y", [P, NB, D]), sb("sq", [P, NB, D]), sb("st", [P, 8, NB])
        mid, a = sb("mid", [P, NH, D]), sb("a", [P, 11, NH])
        mq = m.raw[:, 0:NH * D].rearrange("p (n d) -> p n d", d=D)
        step_sem, ask, ans, out_sem = sem("step"), sem("ask"), sem("answered"), sem("out")
        block = ctx.enter_context(nc.Block())

        @block.scalar
        def _(act):
            act.wait_ge(ask, 1)
            act.activation(a[:, 3, :], a[:, 2, :], ACT.Sqrt).then_inc(ans, 1)
            act.wait_ge(ask, 2)
            act.activation(a[:, 6, :], a[:, 5, :], ACT.Ln, bias=1.0)
            act.activation(a[:, 7, :], a[:, 5, :], ACT.Ln, bias=1.0, scale=-1.0).then_inc(ans, 1)
            act.wait_ge(ask, 3)
            act.activation(st[:, 1, :], st[:, 0, :], ACT.Sqrt).then_inc(ans, 1)
            act.wait_ge(ask, 4)
            act.activation(st[:, 3, :], st[:, 2, :], ACT.Tanh).then_inc(ans, 1)
            act.wait_ge(ask, 5)
            act.activation(st[:, 1, :], st[:, 1, :], ACT.Sqrt).then_inc(ans, 1)

        @block.vector
        def _(dve):
            step = Steps(dve, step_sem)
            ts, tt = dve.tensor_scalar, dve.tensor_tensor
            acc = m.acc[:, 0:NB, :].rearrange("p n (h b) -> p (n h) b", h=H3)
            rz, den, n2, nrm, p, t, up, lo, u, poly, f = (a[:, k, :] for k in range(11))
            wide = lambda k: k.unsqueeze(2).to_broadcast([P, NH, D])
            step(ts(rz, acc[:, :, D + 1], 1e-20, None, ALU.max))
            step(dve.reciprocal(rz, rz))
            step(tt(den, acc[:, :, D], rz, ALU.mult))
            step(ts(den, den, 1e-6, None, ALU.add))
            step(dve.reciprocal(den, den))
            step(tt(rz, rz, den, ALU.mult))
            step(tt(mid[:, :, :], acc[:, :, 0:D], wide(rz), ALU.mult))
            step(tt(mq[:, :, :], mid[:, :, :], mid[:, :, :], ALU.mult))
            step(dve.tensor_reduce(n2.unsqueeze(2), mq[:, :, :], AX.X, ALU.add))
            step(ts(n2, n2, 1e-30, None, ALU.max))
            dve.nop(nofuse=True).then_inc(ask, 1)
            dve.wait_ge(ans, 1)
            step(ts(nrm, nrm, MIN_NORM, None, ALU.max))
            step(dve.reciprocal(p, nrm))
            step(ts(p, p, TOP / ROOT_C, 1.0, ALU.mult, ALU.min))
            step(tt(t, nrm, p, ALU.mult))
            step(ts(t, t, MIN_NORM, ROOT_C, ALU.max, ALU.mult))
            step(ts(t, t, MIN_NORM, TOP, ALU.max, ALU.min))
            atanh_ratio(dve, step, t, lo, up, u, poly, f, ask, (ans, 2))
            step(tt(f, f, p, ALU.mult))
            step(ts(f, f, 1.0 / H3, None, ALU.mult))
            step(tt(mid[:, :, :], mid[:, :, :], wide(f), ALU.mult))
            step(dve.tensor_reduce(y[:, :, :], mid[:, :, :].rearrange("p (n h) d -> p n d h", h=H3), AX.X, ALU.add))
            n2, nrm, t, th, f = (st[:, k, :] for k in range(5))
            step(tt(sq[:, :, :], y[:, :, :], y[:, :, :], ALU.mult))
            step(dve.tensor_reduce(n2.unsqueeze(2), sq[:, :, :], AX.X, ALU.add))
            step(ts(n2, n2, 1e-30, None, ALU.max))
            dve.nop(nofuse=True).then_inc(ask, 1)
            dve.wait_ge(ans, 3)
            step(ts(t, nrm, MIN_NORM, ROOT_C, ALU.max, ALU.mult))
            dve.nop(nofuse=True).then_inc(ask, 1)
            step(dve.reciprocal(f, t))
            dve.wait_ge(ans, 4)
            step(tt(f, th, f, ALU.mult))
            step(tt(y[:, :, :], y[:, :, :], f.unsqueeze(2).to_broadcast([P, NB, D]), ALU.mult))
            step(tt(y[:, :, :], y[:, :, :], m.x[:, :, :], ALU.add))
            layer_norm(dve, step, m, y, sq, st, ask, (ans, 5))
            dve.nop(nofuse=True).then_inc(ask, 1)

        @block.sync
        def _(sp):
            sp.wait_ge(ask, 6)
            out = io["out"]
            sp.dma_start(out[0:NFULL * P, :].rearrange("(b p) d -> p b d", p=P), m.x[:, 0:NFULL, :]).then_inc(out_sem, 16)
            sp.dma_start(out[NFULL * P:N, :], m.x[0:NREST, NFULL, :]).then_inc(out_sem, 16)
            sp.wait_ge(out_sem, 32)


def kernel(**inputs):
    import numpy as _np
    import concourse.bacc as _bacc
    from concourse import mybir as _mybir
    from concourse.bass_utils import run_bass_kernel_spmd as _run

    i = {k: _np.asarray(v) for k, v in inputs.items()}
    cat = _np.concatenate

    def packed(prefix, suffix, turned):
        w = [i[f"{prefix}_W{n}{suffix}"] for n in "qkvs"]
        b = [i[f"{prefix}_b{n}{suffix}"] for n in "qkvs"]
        return cat([cat([k.T if turned else k for k in w], axis=1), cat(b)[None, :]], axis=0)

    arrays = {
        "x": i["x"], "src": i["src"], "dst": i["dst"], "edge_type_8": i["edge_type_8"],
        "wij": _np.stack([i["L0_gnn_w_i"], i["L0_gnn_w_j"]]),
        "W1": packed("L1_gnn", "1", True), "W2": packed("L1_gnn", "2", True), "W3": packed("L2_gnn", "", False),
        "Wrel": i["L3_gnn_rel_weight"].transpose(2, 0, 1, 3).reshape(64, -1),
        "AV": i["L3_gnn_attn_vec"].transpose(2, 0, 1).reshape(64, -1),
    }
    arrays = {f"in_{k}": _np.ascontiguousarray(v) for k, v in arrays.items()}
    nc = _bacc.Bacc("TRN2", target_bir_lowering=False, num_devices=1)
    io = {k[3:]: nc.dram_tensor(k, v.shape, _mybir.dt.from_np(v.dtype), kind="ExternalInput").ap()
          for k, v in arrays.items()}
    io["out"] = nc.dram_tensor("out_x", (3125, 64), _mybir.dt.float32, kind="ExternalOutput").ap()
    build(nc, io)
    r = _run(nc, [arrays], core_ids=[0])
    return r.results[0]["out_x"]
```

```python
from contextlib import ExitStack

import numpy as np
import concourse.bass as bass
from concourse import mybir

F32 = mybir.dt.float32
BF16 = mybir.dt.bfloat16
I32 = mybir.dt.int32
ALU = mybir.AluOpType
ACT = mybir.ActivationFunctionType
AX = mybir.AxisListType

P = 128
N, D, E = 3125, 64, 100000
NB = -(-N // P)
NFULL = N // P
NREST = N - NFULL * P
NPAD = NB * P
GU = 2
UE = GU * P
TC = 64
UC = TC // GU
CH = -(-((E + NB * (UE - 1)) // UE) // UC)
UNITS = CH * UC
T = CH * TC
TB = -(-T // P)
EC, ER = E // P, E % P
BIG = 1.0e30
EPS = 1e-5


class Steps:

    def __init__(self, eng, sem):
        self.eng, self.sem, self.n, self.base, self.per = eng, sem, 0, 0, None

    def __call__(self, ins):
        ins.then_inc(self.sem, 1)
        self.n += 1
        self.eng.wait_ge(self.sem, self.base + self.n)

    def begin(self, i, per):
        assert self.per is None or self.n == self.per, (self.n, self.per)
        self.base, self.n, self.per = i * per, 0, per


def rows(dram, width):
    return dram.rearrange("(b p) w -> p b w", p=P)


def build(nc, io):
    ctx = ExitStack()
    with ctx:
        m = Memory(nc, ctx)
        setup(nc, io, m)
        prep0(nc, io, m)
        conv(nc, io, m, 0)
        finish0(nc, io, m)
        for l in (1, 2, 3):
            prep_linear(nc, io, m, l)
            conv(nc, io, m, l)
            finish_linear(nc, io, m, l)
        prep4(nc, io, m)
        conv(nc, io, m, 4)
        finish4(nc, io, m)


class Conv:

    def __init__(self, heads, block, row, spread, raw, extra=0, tiles=8, ring=4):
        self.G, self.ring = tiles, ring
        self.H, self.B, self.W, self.Q, self.R, self.X = heads, block, row, spread, raw, extra
        self.PW = heads * block
        self.HP = min(heads, 2)
        self.NS = heads // self.HP


R_, H3 = 8, 4
B3 = D + 2
CONVS = [Conv(1, D + 1, D + 2, 1, 1, extra=2),
         Conv(1, D + 1, 2 * D + 1, D, 1),
         Conv(1, D + 1, 2 * D + 1, D, 1),
         Conv(8, D // 8 + 1, 8 * 9 + D, D, 8),
         Conv(H3, B3, H3 * B3 + D + 1 + H3 + R_, D + R_ * H3 + 1, 11, tiles=4, ring=4)]


class Memory:

    def __init__(self, nc, ctx):
        def sb(name, shape, dt=F32):
            return ctx.enter_context(nc.sbuf_tensor(name, shape, dt))

        def dram(name, shape, dt=F32):
            return nc.dram_tensor(name, shape, dt, kind="Internal").ap()

        self.nc = nc
        self.sems = [[ctx.enter_context(nc.semaphore(f"bank{k}_{j}")) for j in range(40)] for k in range(2)]
        self.stages = 0
        self.gathered = [[ctx.enter_context(nc.semaphore(f"gathered{l}_{s}")) for s in range(CONVS[l].ring)] for l in range(5)]
        self.bank = [ctx.enter_context(nc.psum_tensor(f"bank{i}", [P, 512], F32)) for i in range(8)]
        self.ident = sb("ident", [P, P])
        self.ones = sb("ones", [P, P])
        self.iota_p = sb("iota_p", [P, 1])
        self.iota_f = sb("iota_f", [P, P])
        self.eye4 = sb("eye4", [4, 4, 2])
        self.unit_bucket = sb("unit_bucket", [1, UNITS], I32)
        self.dl = sb("dl", [P, T])
        self.src_t = sb("src_t", [P, T], I32)
        self.s8_t = sb("s8_t", [P, T], I32)
        self.cut_f = sb("cut_f", [P, CH, P])
        self.cut_b = sb("cut_b", [P, CH, P])
        self.row_cut = sb("row_cut", [4, 2, CH, TC])
        self.dl0 = sb("dl0", [4, CH])
        self.x = sb("x", [P, NB, D])
        self.skip = sb("skip", [P, NB, D])
        self.acc = sb("acc", [P, NB + 1, H3 * B3])
        self.spread = sb("spread", [P, NB + 1, D + R_ * H3 + 1])
        self.flat_dl = dram("flat_dl", [T * P], BF16)
        self.table = [dram(f"table{l}", [NPAD * (R_ if l == 4 else 1), c.W]) for l, c in enumerate(CONVS)]

    def stage_sems(self):
        mine, other = self.sems[self.stages % 2], self.sems[1 - self.stages % 2]
        if self.stages:
            lo = min(s.num for s in other)
            assert max(s.num for s in other) == lo + len(other) - 1
            self.nc.sync.sem_clear(range(lo, lo + len(other)))
        self.stages += 1
        left = list(mine)
        return lambda name: left.pop(0)


def setup(nc, io, m):
    ctx = ExitStack()
    with ctx:
        def sb(name, shape, dt=F32):
            return ctx.enter_context(nc.sbuf_tensor("st_" + name, shape, dt))

        sem = m.stage_sems()

        def dram(name, shape, dt=F32):
            return nc.dram_tensor(name, shape, dt, kind="Internal").ap()

        UQ = UNITS // 4
        dst_i, src_i, typ_i = (sb(n, [P, EC + 1], I32) for n in ("dst_i", "src_i", "typ_i"))
        dst_f, junk = sb("dst_f", [P, EC + 1]), sb("junk", [P, EC + 1])
        s8_i = sb("s8_i", [P, EC + 1], I32)
        cnt = sb("cnt", [P, NB + 1])
        row = sb("row", [1, 6, NB + 1])
        rowi = sb("rowi", [1, 2, NB + 1], I32)
        col = sb("col", [NB, 2])
        iota_i = sb("iota_i", [P, T], I32)
        iota_pi = sb("iota_pi", [P, 1], I32)
        iota_t = sb("iota_t", [NB, T])
        past = sb("past", [NB, T])
        e0 = sb("e0", [UQ, 12])
        e0_i = sb("e0_i", [UQ, 4], I32)
        bvt = sb("bvt", [P, TB])
        pad = sb("pad", [1, 3, UE], I32)
        gat = [[sb(f"gat{a}{h}", [UQ, UE], I32) for h in range(4)] for a in range(3)]
        nat_i = [sb(f"nat_i{a}", [P, TB, P], I32) for a in range(3)]
        nat_f = [sb(f"nat_f{a}", [P, TB, P]) for a in range(3)]
        ok, key = sb("ok", [P, TB, P]), sb("key", [P, TB, P])
        dl_b = sb("dl_b", [P, TB, P], BF16)
        own, prev, nxt = (sb(n, [P, CH, P]) for n in ("own", "prev", "nxt"))
        edge2 = sb("edge2", [1, 2])
        rc = sb("rc", [TC, 2, CH])
        rcw = sb("rcw", [TC, 2, CH, 4])
        lin = [dram(f"lin{a}", [E + UE], I32) for a in range(3)]
        flat = [dram(f"flat{a}", [T * P], I32) for a in range(3)]
        flat_key = dram("flat_key", [T * P + 2])

        loaded, x_in, pool_step, consts = sem("loaded"), sem("x_in"), sem("pool_step"), sem("consts")
        dve_step, stored, flat_out, flat_in = sem("dve_step"), sem("stored"), sem("flat_out"), sem("flat_in")
        key_out, key_in = sem("key_out"), sem("key_in")
        gathered = ctx.enter_context(nc.semaphore("gathered"))
        (x_zero, s8_made, e0_made, key_made, counted, rowed, past_made, floated, dl_made, cuts_made) = (
            sem(n) for n in ("x_zero", "s8_made", "e0_made", "key_made", "counted", "rowed", "past_made",
                             "floated", "dl_made", "cuts_made"))
        starts, cols, units, turned, cuts_turned = (sem(n) for n in ("starts", "cols", "units", "turned",
                                                                     "cuts_turned"))
        taken = sem("taken")
        block = ctx.enter_context(nc.Block())

        def edges(a):
            return a[0:P * EC].rearrange("(p c) -> p c", p=P), a[P * EC:E].rearrange("(p c) -> p c", c=1)

        def blocks(flat_array):
            full = T // P
            yield flat_array[0:full * P * P].rearrange("(k i e) -> i k e", i=P, e=P), P, slice(0, full)
            if T % P:
                yield flat_array[full * P * P:T * P].rearrange("(k i e) -> i k e", k=1, e=P), T % P, slice(full, full + 1)

        NPARTS = 1 + (T % P > 0)

        @block.sync
        def _(sp):
            for tile, name in ((dst_i, "dst"), (src_i, "src"), (typ_i, "edge_type_8")):
                body, rest = edges(io[name])
                sp.dma_start(tile[:, 0:EC], body).then_inc(loaded, 16)
                sp.dma_start(tile[0:ER, EC:EC + 1], rest).then_inc(loaded, 16)
            xin = io["x"]
            sp.wait_ge(x_zero, 1)
            sp.dma_start(m.x[:, 0:NFULL, :], xin[0:NFULL * P, :].rearrange("(b p) d -> p b d", p=P)).then_inc(x_in, 16)
            sp.dma_start(m.x[0:NREST, NFULL, :], xin[NFULL * P:N, :]).then_inc(x_in, 16)
            sp.wait_ge(s8_made, 1)
            for a, tile in enumerate((dst_i, src_i, s8_i)):
                body, rest = edges(lin[a][0:E])
                sp.dma_start(body, tile[:, 0:EC]).then_inc(stored, 16)
                sp.dma_start(rest, tile[0:ER, EC:EC + 1]).then_inc(stored, 16)
                sp.dma_start(lin[a][E:E + UE].rearrange("(o w) -> o w", o=1), pad[:, a, :]).then_inc(stored, 16)
            sp.wait_ge(gathered, 16 * 12)
            for a in range(3):
                for h in range(4):
                    sp.dma_start(flat[a][h * UQ * UE:(h + 1) * UQ * UE].rearrange("(v e) -> v e", e=UE),
                                 gat[a][h][:, :]).then_inc(flat_out, 16)
            sp.wait_ge(flat_out, 16 * 12)
            for a in range(3):
                for src, n, ks in blocks(flat[a]):
                    sp.dma_start(nat_i[a][0:n, ks, :], src).then_inc(flat_in, 16)
            sp.wait_ge(key_made, 1)
            for tile, array in ((key, flat_key[1:1 + T * P]), (dl_b, m.flat_dl)):
                for out, n, ks in blocks(array):
                    sp.dma_start(out, tile[0:n, ks, :]).then_inc(key_out, 16)
            sp.dma_start(flat_key[0:1].rearrange("(o w) -> o w", o=1), edge2[:, 0:1]).then_inc(key_out, 16)
            sp.dma_start(flat_key[T * P + 1:T * P + 2].rearrange("(o w) -> o w", o=1), edge2[:, 1:2]).then_inc(key_out, 16)
            sp.wait_ge(key_out, 16 * (2 * NPARTS + 2))
            for at, tile in enumerate((prev, own, nxt)):
                for half in range(2):
                    sp.dma_start(tile[half * TC:(half + 1) * TC, :, :],
                                 flat_key[at:at + T * P].rearrange("(c t e) -> t c e", t=TC, e=P)).then_inc(key_in, 16)

        @block.gpsimd
        def _(pool):
            step = Steps(pool, pool_step)
            step(pool.memset(m.ident[:, :], 0.0))
            step(pool.affine_select(out=m.ident[:, :], in_=m.ident[:, :], compare_op=ALU.not_equal, fill=1.0,
                                    base=0, pattern=[[-1, P]], channel_multiplier=1))
            step(pool.memset(m.eye4[:, :, :], 0.0))
            step(pool.affine_select(out=m.eye4[:, :, :], in_=m.eye4[:, :, :], compare_op=ALU.not_equal, fill=1.0,
                                    base=0, pattern=[[-1, 4], [0, 2]], channel_multiplier=1))
            step(pool.iota(iota_i[:, :], [[1, T]], base=0, channel_multiplier=0))
            pool.memset(m.ones[:, :], 1.0).then_inc(consts, 1)
            pool.iota(iota_pi[:, :], [[0, 1]], base=0, channel_multiplier=1).then_inc(consts, 1)
            pool.wait_ge(e0_made, 1)
            pool.wait_ge(stored, 16 * 9)
            for a in range(3):
                for h in range(4):
                    pool.indirect_dma_start(gat[a][h][:, :], None, lin[a].rearrange("(n o) -> n o", o=1),
                                            bass.IndirectOffsetOnAxis(ap=e0_i[:, h:h + 1], axis=0)).then_inc(gathered, 16)

        @block.vector
        def _(dve):
            step = Steps(dve, dve_step)

            def tell(sem):
                dve.nop(nofuse=True).then_inc(sem, 1)

            step(dve.memset(m.x[:, :, :], 0.0))
            tell(x_zero)
            step(dve.memset(pad[:, 0, :], NPAD))
            step(dve.memset(pad[:, 1:3, :], 0))
            step(dve.memset(edge2[:, :], -1000.0))
            step(dve.memset(cnt[:, :], 0.0))
            step(dve.memset(dst_f[:, :], 1.0e9))
            dve.wait_ge(loaded, 16 * 6)
            step(dve.tensor_scalar(s8_i[:, 0:EC], src_i[:, 0:EC], float(R_), None, ALU.mult))
            step(dve.tensor_scalar(s8_i[0:ER, EC:EC + 1], src_i[0:ER, EC:EC + 1], float(R_), None, ALU.mult))
            step(dve.tensor_tensor(s8_i[:, 0:EC], s8_i[:, 0:EC], typ_i[:, 0:EC], ALU.add))
            step(dve.tensor_tensor(s8_i[0:ER, EC:EC + 1], s8_i[0:ER, EC:EC + 1], typ_i[0:ER, EC:EC + 1], ALU.add))
            tell(s8_made)
            step(dve.tensor_copy(dst_f[:, 0:EC], dst_i[:, 0:EC]))
            step(dve.tensor_copy(dst_f[0:ER, EC:EC + 1], dst_i[0:ER, EC:EC + 1]))
            for b in range(1, NB + 1):
                step(dve.tensor_scalar(junk[:, :], dst_f[:, :], float(P * b), 0.0, ALU.is_lt, ALU.add,
                                       accum_out=cnt[:, b:b + 1]))
            dve.wait_ge(consts, 2)
            step(dve.tensor_copy(m.iota_p[:, :], iota_pi[:, :]))
            step(dve.tensor_copy(m.iota_f[:, :], iota_i[:, 0:P]))
            step(dve.tensor_copy(iota_t[:, :], iota_i[0:NB, :]))
            tell(counted)
            dve.wait_ge(starts, 1)
            start, n, nu, us, g, dg = (row[:, k, :] for k in range(6))
            step(dve.tensor_copy(start, m.bank[0][0:1, 0:NB + 1]))
            step(dve.tensor_tensor(n[:, 0:NB], start[:, 1:NB + 1], start[:, 0:NB], ALU.subtract))
            step(dve.tensor_scalar(rowi[:, 0, 0:NB], n[:, 0:NB], float(UE - 1), None, ALU.add))
            step(dve.tensor_scalar(rowi[:, 1, 0:NB], rowi[:, 0, 0:NB], UE.bit_length() - 1, None, ALU.arith_shift_right))
            step(dve.tensor_copy(nu[:, 0:NB], rowi[:, 1, 0:NB]))
            step(dve.memset(us[:, 0:1], 0.0))
            step(dve.tensor_tensor_scan(us[:, 1:NB + 1], m.ones[0:1, 0:NB], nu[:, 0:NB], 0.0, ALU.mult, ALU.add))
            step(dve.scalar_tensor_tensor(g, us, float(-UE), start, ALU.mult, ALU.add))
            step(dve.tensor_tensor(dg[:, 0:NB], g[:, 1:NB + 1], g[:, 0:NB], ALU.subtract))
            step(dve.tensor_scalar(us, us, float(GU), None, ALU.mult))
            tell(rowed)
            dve.wait_ge(cols, 1)
            step(dve.tensor_copy(col[:, :], m.bank[1][0:NB, 0:2]))
            step(dve.tensor_scalar(past[:, :], iota_t[:, :], col[:, 0:1], None, ALU.is_ge))
            tell(past_made)
            dve.wait_ge(units, 1)
            step(dve.tensor_copy(m.unit_bucket[:, :], m.bank[2][0:1, 0:UNITS]))
            step(dve.tensor_copy(e0[:, 0:4], m.bank[3][0:UQ, 0:4]))
            for h in range(4):
                step(dve.tensor_scalar(e0[:, 4 + h:5 + h], m.iota_p[0:UQ, :], float(h * UQ), float(UE), ALU.add, ALU.mult))
            step(dve.tensor_tensor(e0[:, 8:12], e0[:, 0:4], e0[:, 4:8], ALU.add))
            step(dve.tensor_scalar(e0_i[:, :], e0[:, 8:12], float(E), 0.0, ALU.min, ALU.max))
            tell(e0_made)
            step(dve.tensor_copy(bvt[:, :], m.bank[4][:, 0:TB]))
            if T % P:
                for a in range(3):
                    step(dve.memset(nat_f[a][:, TB - 1, :], 0.0))
            dve.wait_ge(flat_in, 16 * 3 * NPARTS)
            for a in range(3):
                for _, n, ks in blocks(flat[a]):
                    step(dve.tensor_copy(nat_f[a][0:n, ks, :], nat_i[a][0:n, ks, :]))
            dst_n = nat_f[0][:, :, :]
            wide = bvt[:, :].unsqueeze(2).to_broadcast([P, TB, P])
            step(dve.scalar_tensor_tensor(dst_n, wide, float(-P), dst_n, ALU.mult, ALU.add))
            step(dve.tensor_scalar(ok[:, :, :], dst_n, float(P), None, ALU.is_lt))
            step(dve.scalar_tensor_tensor(dst_n, dst_n, 1.0, ok[:, :, :], ALU.add, ALU.mult))
            step(dve.tensor_scalar(dst_n, dst_n, -1.0, None, ALU.add))
            tell(floated)
            step(dve.scalar_tensor_tensor(key[:, :, :], wide, float(P + 2), dst_n, ALU.mult, ALU.add))
            step(dve.tensor_copy(dl_b[:, :, :], dst_n))
            tell(key_made)
            outs = (m.dl, m.src_t, m.s8_t)
            for a in range(3):
                dve.wait_ge(turned, a + 1)
                at = 4 * (a % 2)
                step(dve.tensor_copy(outs[a][:, 0:512], m.bank[at][:, :]))
                step(dve.tensor_copy(outs[a][:, 512:T], m.bank[at + 1][:, 0:T - 512]))
                tell(taken)
            tell(dl_made)
            dve.wait_ge(key_in, 16 * 6)
            for k, (cut, other) in enumerate(((m.cut_f, prev), (m.cut_b, nxt))):
                out = cut[:, :, ::-1] if k else cut[:, :, :]
                step(dve.tensor_tensor(out, own[:, :, :], other[:, :, :], ALU.not_equal))
                step(dve.tensor_scalar(cut[:, :, :], cut[:, :, :], -BIG, None, ALU.mult))
                step(dve.tensor_reduce(rc[:, k, :].unsqueeze(2), cut[0:TC, :, :], AX.X, ALU.min))
            step(dve.tensor_copy(rcw[:, :, :, :], rc[:, :, :].unsqueeze(3).to_broadcast([TC, 2, CH, 4])))
            tell(cuts_made)
            dve.wait_ge(cuts_turned, 1)
            step(dve.tensor_copy(m.dl0[:, :], m.bank[6][0:4, 0:CH]))
            for k in range(2):
                for h in range(2):
                    n = min(8, CH - 8 * h)
                    step(dve.tensor_copy(m.row_cut[:, k, 8 * h:8 * h + n, ::(-1 if k else 1)],
                                         m.bank[2 * k + h][0:4, 0:n * TC].rearrange("s (c t) -> s c t", t=TC)))
            dve.wait_ge(x_in, 32)

        @block.tensor
        def _(pe):
            pe.wait_ge(counted, 1)
            pe.matmul(m.bank[0][0:1, 0:NB + 1], m.ones[:, 0:1], cnt[:, :], start=True, stop=True).then_inc(starts, 1)
            pe.wait_ge(rowed, 1)
            pe.matmul(m.bank[1][0:NB, 0:1], row[:, 3, 1:NB + 1], m.ones[0:1, 0:1], start=True, stop=True)
            pe.matmul(m.bank[1][0:NB, 1:2], row[:, 5, 0:NB], m.ones[0:1, 0:1], start=True, stop=True).then_inc(cols, 1)
            pe.wait_ge(past_made, 1)
            pe.matmul(m.bank[2][0:1, 0:UNITS], m.ones[0:NB, 0:1], past[:, 0:T:GU], start=True, stop=True)
            for h in range(4):
                pe.matmul(m.bank[3][0:UQ, h:h + 1], past[:, h * UQ * GU:(h + 1) * UQ * GU:GU], col[:, 1:2],
                          start=True, stop=True)
            for k in range(TB):
                n = min(P, T - k * P)
                mm = pe.matmul(m.bank[4][0:n, k:k + 1], past[:, k * P:k * P + n], m.ones[0:NB, 0:1], start=True, stop=True)
            if T % P:
                mm = pe.matmul(m.bank[4][T % P:P, TB - 1:TB], past[:, 0:P - T % P], m.ones[0:NB, 0:1], start=True, stop=True)
            mm.then_inc(units, 1)
            pe.wait_ge(floated, 1)
            for a in range(3):
                if a == 2:
                    pe.wait_ge(taken, 1)
                for k in range(TB):
                    n = min(P, T - k * P)
                    at = m.bank[4 * (a % 2) + k // 4][:, k % 4 * P:k % 4 * P + n]
                    mm = pe.transpose(at, nat_f[a][0:n, k, :], m.ident[0:n, 0:n])
                mm.then_inc(turned, 1)
            pe.wait_ge(dl_made, 1)
            pe.wait_ge(cuts_made, 1)
            pe.matmul(m.bank[6][0:4, 0:CH], m.ones[0:1, 0:4], m.dl[0:1, 0:T:TC], start=True, stop=True)
            for k in range(2):
                for c in range(CH):
                    at = m.bank[2 * k + c // 8][0:4, c % 8 * TC:(c % 8 + 1) * TC]
                    mm = pe.transpose(at, rcw[:, k, c, :], m.ident[0:TC, 0:TC])
            mm.then_inc(cuts_turned, 1)


def prep0(nc, io, m):
    c = CONVS[0]
    with ExitStack() as ctx:
        sb = lambda n, s, dt=F32: ctx.enter_context(nc.sbuf_tensor("p0_" + n, s, dt))
        sem = m.stage_sems()
        w = sb("w", [P, 2, D])
        tb = sb("tb", [P, NB, c.W])
        prod = sb("prod", [P, NB, D])
        w_in, step_sem, made, out_sem = sem("w_in"), sem("step"), sem("made"), sem("out")
        block = ctx.enter_context(nc.Block())

        @block.sync
        def _(sp):
            sp.dma_start(w[:, :, :], io["wij"].rearrange("(o k) d -> o k d", o=1).to_broadcast([P, 2, D])).then_inc(w_in, 16)
            sp.wait_ge(made, 1)
            sp.dma_start(rows(m.table[0], c.W), tb[:, :, :]).then_inc(out_sem, 16)
            sp.wait_ge(out_sem, 16)

        @block.vector
        def _(dve):
            step = Steps(dve, step_sem)
            step(dve.memset(m.spread[:, :, 0:1], 0.0))
            step(dve.tensor_copy(tb[:, :, 0:D], m.x[:, :, :]))
            step(dve.memset(tb[:, :, D:D + 1], 1.0))
            dve.wait_ge(w_in, 16)
            for k, out in enumerate((m.spread[:, 0:NB, 0:1], tb[:, :, D + 1:D + 2])):
                step(dve.tensor_tensor(prod[:, :, :], m.x[:, :, :], w[:, k:k + 1, :].to_broadcast([P, NB, D]), ALU.mult))
                step(dve.tensor_reduce(out, prod[:, :, :], AX.X, ALU.add))
            dve.nop(nofuse=True).then_inc(made, 1)


def prep_linear(nc, io, m, l):
    c = CONVS[l]
    inp = m.skip if l == 2 else m.x
    with ExitStack() as ctx:
        sb = lambda n, s, dt=F32: ctx.enter_context(nc.sbuf_tensor(f"pl{l}_" + n, s, dt))
        sem = m.stage_sems()
        w = sb("w", [D + 1, 4 * D])
        xt = sb("xt", [D + 1, 2, P])
        tb = sb("tb", [P, NB, c.W])
        w_in, ready, turned, moved = sem("w_in"), sem("ready"), sem("turned"), sem("moved")
        product, taken_d, taken_a, out_sem = sem("product"), sem("taken_d"), sem("taken_a"), sem("out")
        block = ctx.enter_context(nc.Block())
        vb = D // c.H
        payload = tb[:, :, 0:c.PW].rearrange("p b (h v) -> p b h v", h=c.H)

        @block.sync
        def _(sp):
            sp.dma_start(w[:, :], io[f"W{l}"]).then_inc(w_in, 16)
            sp.wait_ge(taken_d, NB)
            sp.wait_ge(taken_a, NB)
            sp.dma_start(rows(m.table[l], c.W), tb[:, :, :]).then_inc(out_sem, 16)
            sp.wait_ge(out_sem, 16)

        @block.gpsimd
        def _(pool):
            step = Steps(pool, ready)
            step(pool.memset(xt[D:D + 1, :, :], 1.0))
            step(pool.memset(payload[:, :, :, vb:vb + 1], 1.0))
            step(pool.memset(m.spread[:, NB:NB + 1, :], 0.0))

        @block.tensor
        def _(pe):
            pe.wait_ge(w_in, 16)
            pe.wait_ge(ready, 3)
            for b in range(NB + 1):
                if b < NB:
                    if b >= 2:
                        pe.wait_ge(moved, b - 1)
                    pe.transpose(m.bank[b % 2][0:D, 0:P], inp[:, b, :], m.ident[:, :]).then_inc(turned, 1)
                if b >= 1:
                    k = b - 1
                    pe.wait_ge(moved, k + 1)
                    if k >= 2:
                        pe.wait_ge(taken_d, k - 1)
                        pe.wait_ge(taken_a, k - 1)
                    pe.matmul(m.bank[2 + k % 2][:, 0:4 * D], xt[:, k % 2, :], w[:, :], start=True, stop=True)\
                        .then_inc(product, 1)

        @block.scalar
        def _(act):
            for b in range(NB + 1):
                if b < NB:
                    act.wait_ge(turned, b + 1)
                    if b >= 2:
                        act.wait_ge(product, b - 1)
                    act.copy(xt[0:D, b % 2, :], m.bank[b % 2][0:D, 0:P]).then_inc(moved, 1)
                if b >= 1:
                    k = b - 1
                    act.wait_ge(product, k + 1)
                    act.copy(payload[:, k, :, 0:vb],
                             m.bank[2 + k % 2][:, 2 * D:3 * D].rearrange("p (h v) -> p h v", h=c.H)).then_inc(taken_a, 1)

        @block.vector
        def _(dve):
            dve.wait_ge(ready, 3)
            for b in range(NB):
                dve.wait_ge(taken_a, b + 1)
                bank = m.bank[2 + b % 2]
                dve.tensor_copy(m.spread[:, b, 0:D], bank[:, 0:D])
                dve.tensor_copy(tb[:, b, c.PW:c.W], bank[:, D:2 * D])
                dve.tensor_copy(m.skip[:, b, :], bank[:, 3 * D:4 * D]).then_inc(taken_d, 1)


def conv(nc, io, m, l):
    c_ = CONVS[l]
    W, Q, R, H, B, PW, X, HP, NS = c_.W, c_.Q, c_.R, c_.H, c_.B, c_.PW, c_.X, c_.HP, c_.NS
    AW = PW + X
    HPP = HP * TC
    scale = {0: 1.0, 1: float(D) ** -0.5, 2: float(D) ** -0.5, 3: float(D // 8) ** -0.5, 4: 1.0}[l]
    idx = m.s8_t if l == 4 else m.src_t
    G, RING = c_.G, c_.ring
    KV, U = TC // G, G // GU
    VE, QV = G * P, 2
    PART = RING * G
    PARTS = KV // RING
    UPB = min(U, 512 // AW)
    SLOTS, AHEAD = 4, 3
    HALF = (NB + 2) // 2
    with ExitStack() as ctx:
        sb = lambda n, s, dt=F32: ctx.enter_context(nc.sbuf_tensor(f"c{l}_" + n, s, dt))
        sem = m.stage_sems()
        stage = sb("stage", [P, 2, PART], I32)
        g = sb("g", [P, RING, G, W])
        keep = sb("keep", [P, KV, G, PW])
        dlw = sb("dlw", [P, 2, QV * VE], BF16)
        oh_n = sb("oh_n", [P, SLOTS, VE], BF16)
        parts = sb("parts", [P, NB + 1, 3, Q], BF16)
        raw = sb("raw", [P, R, TC])
        if l == 4:
            free, at = m.spread[:, :, :].rearrange("p b q -> p (b q)"), [0]

            def over(n, s):
                size = s[1] * s[2]
                at[0] += size
                return free[0:s[0], at[0] - size:at[0]].rearrange("p (a b) -> p a b", a=s[1])
            dl_c = over("dl_c", [P, 1, TC])
            tmp, score, prod2 = over("tmp", [P, 10, TC]), over("score", [P, H, TC]), over("prod2", [P, G, R_ * H3])
        else:
            over, score = sb, raw
        prod = over("prod", [P, G, D])
        S = over("S", [HPP, NS, P])
        f, b = over("f", [HPP, NS, P]), over("b", [HPP, NS, P])
        ex = over("ex", [HPP, NS, P])
        lrow = sb("lrow", [NS, 2, HP, TC])
        crow = sb("crow", [NS, 2, HP, TC + 1])
        cin = sb("cin", [NS, 2, HP, TC])
        rho, dm = sb("rho", [NS, HP]), sb("dm", [NS, HP])
        rho_b = sb("rho_b", [NS, NS, HP])
        first = sb("first", [NS, P])
        carry = sb("carry", [HPP, 2, NS])
        fac = sb("fac", [P, H])
        wt = sb("wt", [P, H, TC])
        if X:
            ends = sb("ends", [TC, 2, P])
            ext = sb("ext", [P, X, TC])
        if l == 4:
            oh_e = m.skip[:, :, :].rearrange("p b d -> p (b d)")[:, 0:2 * G * P].rearrange("p (s g n) -> p s g n", s=2, g=G)
        else:
            oh_e = sb("oh_e", [P, 2, G, P])
        wp = sb("wp", [P, 2, G, AW])

        gathered = m.gathered[l]
        staged, split, onehot, spread, scored = (sem(n) for n in ("staged", "split", "onehot", "spread", "scored"))
        kept, dl_in = [sem(f"kept{s}") for s in range(RING)], [sem("dl_in0"), sem("dl_in1")]
        visit_step, soft_step, sides_a, sides_b = sem("visit_step"), sem("soft_step"), sem("sides_a"), sem("sides_b")
        weighted, summed, added, cleared = sem("weighted"), sem("summed"), sem("added"), sem("cleared")
        final, scans, carries, rescale = sem("final"), sem("scans"), sem("carries"), sem("rescale")
        s_in, rho_in, wt_in = sem("s_in"), sem("rho_in"), sem("wt_in")
        to_scan, to_rows, to_cols, to_nodes, to_tiles = (sem(n) for n in ("to_scan", "to_rows", "to_cols",
                                                                          "to_nodes", "to_tiles"))
        shifted, expd = sem("shifted"), sem("expd")
        ask, answered = sem("ask"), sem("answered")
        dl_set, apart, selected = sem("dl_set"), sem("apart"), sem("selected")
        block = ctx.enter_context(nc.Block())

        def gathers(c, k):
            return (c * (KV // RING) + k // RING + 1) * (16 * G)

        def copies(c, k):
            return (c * (KV // RING) + k // RING + 1) * 16

        SPLIT_STEPS = 10

        def sums(k, u):
            return m.bank[4 + 2 * (k % 2) + u // UPB][:, u % UPB * AW:(u % UPB + 1) * AW]

        @block.gpsimd
        def _(pool):
            pool.memset(m.acc[:, :, 0:AW], 0.0).then_inc(cleared, 1)

            def chunk(c, first_chunk):
                for k in range(KV):
                    s = k % RING
                    if s == 0:
                        pool.wait_ge(staged, c * (KV // RING) + k // RING + 1)
                        pool.nop(nofuse=True)
                    if not (first_chunk and k < RING):
                        pool.wait_ge(scored, c * KV + (k + 1 - RING))
                        pool.nop(nofuse=True)
                        if l == 4:
                            pool.wait_ge(sides_a, c * KV + (k + 1 - RING))
                            pool.nop(nofuse=True)
                        pool.wait_ge(kept[s], (c * (KV // RING) + k // RING) * 16)
                        pool.nop(nofuse=True)
                    for j in range(G):
                        at = s * G + j
                        pool.indirect_dma_start(g[:, s, j, :], None, m.table[l],
                                                bass.IndirectOffsetOnAxis(ap=stage[:, k // RING % 2, at:at + 1], axis=0))\
                            .then_inc(gathered[s], 16)
            chunk(0, True)
            with pool.Fori(1, CH) as c:
                chunk(c, False)

        @block.sync
        def _(sp):
            NQ = KV // QV

            def load_dl(q, slot):
                sp.dma_start(dlw[:, slot, :], m.flat_dl[bass.ds(q * (QV * VE), QV * VE)].rearrange("(o w) -> o w", o=1)
                             .to_broadcast([P, QV * VE])).then_inc(dl_in[slot], 16)

            def chunk(c, first_chunk, last_chunk):
                for k in range(KV):
                    s = k % RING
                    sp.wait_ge(gathered[s], gathers(c, k))
                    sp.nop(nofuse=True)
                    if not first_chunk:
                        sp.wait_ge(weighted, (c - 1) * KV + k + 1)
                    sp.dma_start(keep[:, k, :, :], g[:, s, :, 0:PW]).then_inc(kept[s], 16)
                    q = k // QV
                    if k % QV == QV - 1 and not (last_chunk and q >= NQ - 2):
                        sp.wait_ge(onehot, c * KV + k + 1)
                        sp.nop(nofuse=True)
                        load_dl(c * NQ + (q + 2), q % 2)
            load_dl(0, 0)
            load_dl(1, 1)
            chunk(0, True, False)
            with sp.Fori(1, CH - 1) as c:
                chunk(c, False, False)
            chunk(CH - 1, False, True)

        @block.tensor
        def _(pe):
            def buckets(eng, c, k):
                return [eng.value_load(m.unit_bucket[0:1, bass.ds(c * UC + (U * k + u), 1)], min_val=0, max_val=NB)
                        for u in range(U)]

            def do_spread(c, k, early):
                bs = buckets(pe, c, k)
                pe.wait_ge(onehot, c * KV + (k + 1))
                if not (early and k < 2):
                    pe.wait_ge(scored, c * KV + (k - 1))
                    if l == 4:
                        pe.wait_ge(sides_a, c * KV + (k - 1))
                for j in range(G):
                    for part in range(3):
                        mm = pe.matmul(m.bank[k % 2][:, j * Q:(j + 1) * Q], oh_n[:, k % SLOTS, j * P:(j + 1) * P],
                                       parts[:, bass.ds(bs[j // GU], 1), part, :], start=(part == 0), stop=(part == 2))
                mm.then_inc(spread, 1)

            def do_sum(c, k, early):
                pe.wait_ge(weighted, c * KV + (k + 1))
                if X:
                    pe.wait_ge(sides_b, c * KV + (k + 1))
                if l == 4:
                    pe.wait_ge(selected, c * KV + (k + 1))
                if not (early and k < 2):
                    pe.wait_ge(added, (c * KV + (k - 1)) * U)
                for j in range(G):
                    mm = pe.matmul(sums(k, j // GU), oh_e[:, k % 2, j, :], wp[:, k % 2, j, :],
                                   start=(j % GU == 0), stop=(j % GU == GU - 1))
                mm.then_inc(summed, 1)

            def do_soft(c):
                if l in (0, 4):
                    pe.wait_ge(final, c + 1)
                    pe.nop(nofuse=True)
                else:
                    pe.wait_ge(scored, (c + 1) * KV)
                    pe.nop(nofuse=True)
                for n in range(NS):
                    mm = pe.transpose(m.bank[2][0:HPP, n * P:(n + 1) * P],
                                      score[:, n * HP:(n + 1) * HP, :].rearrange("p h t -> p (h t)"), m.ident[:, :])
                mm.then_inc(to_scan, 1)
                pe.wait_ge(scans, c + 1)
                pe.nop(nofuse=True)
                pe.transpose(m.bank[3][0:NS, 0:HPP], f[:, :, P - 1], m.ident[0:HPP, 0:HPP])
                pe.transpose(m.bank[3][0:NS, HPP:2 * HPP], b[:, :, 0], m.ident[0:HPP, 0:HPP]).then_inc(to_rows, 1)
                pe.wait_ge(carries, c + 1)
                pe.nop(nofuse=True)
                for k in range(2):
                    mm = pe.transpose(m.bank[4][0:HPP, k * NS:(k + 1) * NS],
                                      cin[:, k, :, :].rearrange("s h t -> s (h t)"), m.ident[0:NS, 0:NS])
                mm.then_inc(to_cols, 1)
                pe.wait_ge(rescale, c + 1)
                pe.nop(nofuse=True)
                pe.matmul(m.bank[5][:, 0:H], first[:, :], rho_b[:, :, :].rearrange("s n h -> s (n h)"),
                          start=True, stop=True).then_inc(to_nodes, 1)
                for n in range(NS):
                    pe.wait_ge(expd, c * NS + (n + 1))
                    pe.nop(nofuse=True)
                    mm = pe.transpose(m.bank[6][:, n * HPP:(n + 1) * HPP], ex[:, n, :], m.ident[0:HPP, 0:HPP])
                for n in range(X):
                    if n == 0:
                        pe.wait_ge(ask, c + 1)
                        pe.nop(nofuse=True)
                    mm = pe.transpose(m.bank[6][:, (H + n) * TC:(H + n + 1) * TC], ends[:, n, :], m.ident[0:TC, 0:TC])
                mm.then_inc(to_tiles, 1)
                pe.wait_ge(wt_in, c + 1)
                pe.nop(nofuse=True)

            def turn(c, first_chunk, last_chunk):
                if not last_chunk:
                    do_spread(c + 1, 0, False)
                do_soft(c)
                for k in range(KV):
                    if not last_chunk and k < KV - 1:
                        do_spread(c + 1, k + 1, False)
                    do_sum(c, k, first_chunk)

            pe.wait_ge(split, SPLIT_STEPS)
            for k in range(KV):
                do_spread(0, k, True)
            turn(0, True, False)
            with pe.Fori(1, CH - 1) as c:
                turn(c, False, False)
            turn(CH - 1, False, True)

        @block.scalar
        def _(act):
            def take_sides(c, k):
                act.wait_ge(scored, c * KV + (k + 1))
                bank = m.bank[k % 2][:, 0:G * Q].rearrange("p (g q) -> p g q", q=Q)
                out = raw[:, :, k * G:(k + 1) * G].rearrange("p r g -> p g r")
                act.copy(out[:, :, 1:2], bank[:, :, Q - 1:Q])
                act.copy(out[:, :, 6:11], g[:, k % RING, :, PW + D:PW + D + 5]).then_inc(sides_a, 1)

            def select_edges(c, k):
                if k >= 2:
                    act.wait_ge(summed, c * KV + (k - 1))
                for j in range(G):
                    act.activation(oh_e[:, k % 2, j, :], m.iota_f[:, :], ACT.Abs, bias=dl_c[:, 0, k * G + j:k * G + j + 1],
                                   scale=-1.0).then_inc(apart, 1)
                act.wait_ge(apart, (c * KV + (k + 1)) * G)
                act.activation(oh_e[:, k % 2, :, :], oh_e[:, k % 2, :, :], ACT.Relu, bias=1.0, scale=-1.0)\
                    .then_inc(selected, 1)

            def copy_ends(c, k, early):
                if not (early and k < 2):
                    act.wait_ge(summed, c * KV + (k - 1))
                act.copy(wp[:, k % 2, :, PW:AW], ext[:, :, k * G:(k + 1) * G].rearrange("p x g -> p g x"))\
                    .then_inc(sides_b, 1)

            def turn(c, first_chunk, last_chunk):
                if l == 4:
                    act.wait_ge(ask, 2 * c + 1)
                    act.activation(tmp[:, 4, :], tmp[:, 3, :], ACT.Sqrt).then_inc(answered, 1)
                    act.wait_ge(ask, 2 * c + 2)
                    act.activation(tmp[:, 5, :], tmp[:, 4, :], ACT.Ln, bias=1.0)
                    act.activation(tmp[:, 6, :], tmp[:, 4, :], ACT.Ln, bias=1.0, scale=-1.0).then_inc(answered, 1)
                act.wait_ge(to_scan, c + 1)
                act.copy(S[:, :, :].rearrange("p n e -> p (n e)"), m.bank[2][0:HPP, 0:NS * P]).then_inc(s_in, 1)
                act.wait_ge(carries, c + 1)
                act.activation(rho[:, :], dm[:, :], ACT.Exp, scale=scale).then_inc(rho_in, 1)
                for n in range(NS):
                    act.wait_ge(shifted, c * NS + (n + 1))
                    act.activation(ex[:, n, :], S[:, n, :], ACT.Exp, scale=scale).then_inc(expd, 1)
                act.wait_ge(to_tiles, c + 1)
                if X:
                    act.copy(ext[:, :, :].rearrange("p x t -> p (x t)"), m.bank[6][:, H * TC:(H + X) * TC])
                act.copy(wt[:, :, :].rearrange("p h t -> p (h t)"), m.bank[6][:, 0:H * TC]).then_inc(wt_in, 1)
                if X:
                    act.wait_ge(wt_in, c + 1)
                if l == 4:
                    act.wait_ge(dl_set, c + 1)
                    select_edges(c, 0)
                for k in range(KV):
                    if l == 4 and k < KV - 1:
                        select_edges(c, k + 1)
                    if l == 4 and not last_chunk:
                        take_sides(c + 1, k)
                    if X:
                        copy_ends(c, k, first_chunk)
            if l == 4:
                for k in range(KV):
                    take_sides(0, k)
            turn(0, True, False)
            with act.Fori(1, CH - 1) as c:
                turn(c, False, False)
            turn(CH - 1, False, True)

        @block.vector
        def _(dve):
            s_step = Steps(dve, soft_step)

            def stage_part(j, slot):
                dve.tensor_copy(stage[:, slot, :], idx[:, bass.ds(j * PART, PART)]).then_inc(staged, 1)

            def restage(c, k, is_last):
                part = k // RING
                if k % RING == RING - 1 and not (is_last and part >= PARTS - 2):
                    stage_part(c * PARTS + (part + 2), part % 2)

            def split_rows():
                step = Steps(dve, split)
                for lo in (0, HALF):
                    n = min(HALF, NB + 1 - lo)
                    rest = wp[:, :, :, :].rearrange("p s g w -> p (s g w)")[:, 0:n * Q].rearrange("p (b q) -> p b q", q=Q)
                    row, left = m.spread[:, lo:lo + n, 0:Q], parts[:, lo:lo + n, :, :]
                    step(dve.tensor_copy(left[:, :, 0, :], row))
                    step(dve.tensor_tensor(rest, row, left[:, :, 0, :], ALU.subtract))
                    step(dve.tensor_copy(left[:, :, 1, :], rest))
                    step(dve.tensor_tensor(rest, rest, left[:, :, 1, :], ALU.subtract))
                    step(dve.tensor_copy(left[:, :, 2, :], rest))
                assert step.n == SPLIT_STEPS

            def compare(c, k):
                if k >= KV:
                    c, k = c + 1, k - KV
                q = k // QV
                if k % QV == 0:
                    dve.wait_ge(dl_in[q % 2], (c * (KV // QV // 2) + q // 2 + 1) * 16)
                dve.tensor_scalar(oh_n[:, k % SLOTS, :], dlw[:, q % 2, k % QV * VE:(k % QV + 1) * VE],
                                  m.iota_p[:, 0:1], None, ALU.is_equal).then_inc(onehot, 1)

            def score_products(c, k, early):
                s = k % RING
                dve.wait_ge(spread, c * KV + (k + 1))
                dve.wait_ge(gathered[s], gathers(c, k))
                bank = m.bank[k % 2][:, 0:G * Q].rearrange("p (g q) -> p g q", q=Q)
                out = raw[:, :, k * G:(k + 1) * G].rearrange("p r g -> p g r")
                if l == 0:
                    dve.tensor_tensor(out, bank, g[:, s, :, W - 1:W], ALU.add).then_inc(scored, 1)
                    return
                if not (early and k == 0):
                    dve.wait_ge(scored, c * KV + k)
                if l == 4:
                    dve.tensor_tensor(prod2[:, :, :].rearrange("p g (r h) -> p g r h", h=H3),
                                      bank[:, :, D:D + R_ * H3].rearrange("p g (r h) -> p g r h", h=H3),
                                      g[:, s, :, W - R_:W].unsqueeze(3).to_broadcast([P, G, R_, H3]), ALU.mult).then_inc(visit_step, 1)
                dve.tensor_tensor(prod[:, :, :], bank[:, :, 0:D], g[:, s, :, PW:PW + D], ALU.mult).then_inc(visit_step, 1)

            def score_sums(c, k):
                out = raw[:, :, k * G:(k + 1) * G].rearrange("p r g -> p g r")
                if l == 0:
                    return
                dve.wait_ge(visit_step, (c * KV + (k + 1)) * (2 if l == 4 else 1))
                if l == 4:
                    dve.tensor_reduce(out[:, :, 2:6], prod2[:, :, :].rearrange("p g (r h) -> p g h r", h=H3),
                                      AX.X, ALU.add)
                if l == 3:
                    dve.tensor_reduce(out, prod[:, :, :].rearrange("p g (h c) -> p g h c", h=H), AX.X, ALU.add)\
                        .then_inc(scored, 1)
                else:
                    dve.tensor_reduce(out[:, :, 0:1], prod[:, :, :], AX.X, ALU.add).then_inc(scored, 1)

            def select_edges(c, k):
                dve.tensor_tensor(oh_e[:, k % 2, :, :], m.iota_f[:, :].unsqueeze(1).to_broadcast([P, G, P]),
                                  m.dl[:, bass.ds(c * TC + k * G, G)].unsqueeze(2).to_broadcast([P, G, P]),
                                  ALU.is_equal)

            def weigh(c, k):
                dve.wait_ge(kept[k % RING], copies(c, k))
                w = wt[:, :, k * G:(k + 1) * G].rearrange("p h g -> p g h").unsqueeze(3).to_broadcast([P, G, H, B])
                dve.tensor_tensor(wp[:, k % 2, :, 0:PW].rearrange("p g (h b) -> p g h b", b=B),
                                  keep[:, k, :, :].rearrange("p g (h b) -> p g h b", b=B), w, ALU.mult)\
                    .then_inc(weighted, 1)

            def add(c, k, u, bucket):
                if u == 0:
                    dve.wait_ge(summed, c * KV + (k + 1))
                acc = m.acc[:, bass.ds(bucket, 1), 0:AW]
                dve.tensor_tensor(acc, acc, sums(k, u).unsqueeze(1), ALU.add).then_inc(added, 1)

            def unit(c, k, u):
                return dve.value_load(m.unit_bucket[0:1, bass.ds(c * UC + (U * k + u), 1)], min_val=0, max_val=NB)

            def final_scores(c, step):
                dve.wait_ge(scored, (c + 1) * KV)
                if l == 0:
                    step(dve.scalar_tensor_tensor(raw[:, 0, :], raw[:, 0, :], 0.01, raw[:, 0, :], ALU.mult, ALU.max))
                elif l == 4:
                    dve.wait_ge(sides_a, (c + 1) * KV)
                    dve.tensor_copy(dl_c[:, :, :], m.dl[:, bass.ds(c * TC, TC)].unsqueeze(1)).then_inc(dl_set, 1)
                    score4(dve, step, raw, tmp, score, ask, answered, c)
                dve.nop(nofuse=True).then_inc(final, 1)

            def do_soft(c, step):
                step.begin(c, {0: 3, 4: SCORE4_STEPS}.get(l, 0) + 6 * NS + 2 * HP + 12)
                if l in (0, 4):
                    final_scores(c, step)
                dve.wait_ge(s_in, c + 1)
                cuts = [cut[0:HPP, bass.ds(c, 1), :].rearrange("p o e -> p (o e)") for cut in (m.cut_f, m.cut_b)]
                for n in range(NS):
                    step(dve.tensor_tensor_scan(f[:, n, :], cuts[0], S[:, n, :], -BIG, ALU.add, ALU.max))
                    step(dve.tensor_tensor_scan(b[:, n, ::-1], cuts[1], S[:, n, ::-1], -BIG, ALU.add, ALU.max))
                dve.nop(nofuse=True).then_inc(scans, 1)
                dve.wait_ge(to_rows, c + 1)
                step(dve.tensor_copy(lrow[:, :, :, :], m.bank[3][0:NS, 0:2 * HPP].rearrange("s (k h t) -> s k h t", k=2, h=HP)))
                step(dve.tensor_copy(crow[:, 0, :, 0], crow[:, 0, :, TC]))
                row_cuts = [m.row_cut[0:NS, k, bass.ds(c, 1), :].rearrange("s o t -> s (o t)") for k in range(2)]
                for h in range(HP):
                    step(dve.tensor_tensor_scan(crow[:, 0, h, 1:TC + 1], row_cuts[0], lrow[:, 0, h, :],
                                                crow[:, 0, h, 0:1], ALU.add, ALU.max))
                    step(dve.tensor_tensor_scan(crow[:, 1, h, TC - 1::-1], row_cuts[1], lrow[:, 1, h, ::-1], -BIG,
                                                ALU.add, ALU.max))
                step(dve.tensor_copy(cin[:, 0, :, :], crow[:, 0, :, 0:TC]))
                step(dve.tensor_copy(cin[:, 1, :, :], crow[:, 1, :, 1:TC + 1]))
                step(dve.tensor_tensor(dm[:, :], crow[:, 0, :, 0], crow[:, 1, :, 0], ALU.max))
                step(dve.tensor_tensor(dm[:, :], crow[:, 0, :, 0], dm[:, :], ALU.subtract))
                step(dve.tensor_scalar(dm[:, :], dm[:, :], -3000.0, None, ALU.max))
                dve.nop(nofuse=True).then_inc(carries, 1)
                step(dve.tensor_scalar(first[:, :], m.iota_f[0:NS, :], m.dl0[0:NS, bass.ds(c, 1)], None, ALU.is_equal))
                dve.wait_ge(rho_in, c + 1)
                step(dve.scalar_tensor_tensor(rho_b[:, :, :], rho[:, :].unsqueeze(1).to_broadcast([NS, NS, HP]), -1.0,
                                              m.eye4[0:NS, 0:NS, 0:HP], ALU.add, ALU.mult))
                dve.nop(nofuse=True).then_inc(rescale, 1)
                dve.wait_ge(to_cols, c + 1)
                step(dve.tensor_copy(carry[:, :, :], m.bank[4][0:HPP, 0:2 * NS].rearrange("p (k n) -> p k n", k=2)))
                for n in range(NS):
                    step(dve.tensor_tensor_scan(f[:, n, :], cuts[0], S[:, n, :], carry[:, 0, n:n + 1], ALU.add, ALU.max))
                    step(dve.tensor_tensor_scan(b[:, n, ::-1], cuts[1], S[:, n, ::-1], carry[:, 1, n:n + 1],
                                                ALU.add, ALU.max))
                    step(dve.tensor_tensor(f[:, n, :], f[:, n, :], b[:, n, :], ALU.max))
                    step(dve.tensor_tensor(S[:, n, :], S[:, n, :], f[:, n, :], ALU.subtract))
                    dve.nop(nofuse=True).then_inc(shifted, 1)
                if X:
                    step(dve.tensor_scalar(ends[:, 1, ::-1], cuts[1], 0.0, None, ALU.is_lt))
                    step(dve.tensor_tensor(ends[:, 0, :], ends[:, 1, :], f[:, 0, :], ALU.mult))
                    dve.nop(nofuse=True).then_inc(ask, 1)
                dve.wait_ge(to_nodes, c + 1)
                step(dve.tensor_scalar(fac[:, :], m.bank[5][:, 0:H], 1.0, None, ALU.add))
                bucket = unit(c, 0, 0)
                acc = m.acc[:, bass.ds(bucket, 1), 0:PW].rearrange("p o (h b) -> p (o h) b", h=H)
                step(dve.tensor_tensor(acc, acc, fac[:, :].unsqueeze(2).to_broadcast([P, H, B]), ALU.mult))
                dve.wait_ge(wt_in, c + 1)

            def turn(c, last_chunk, compares):
                do_soft(c, s_step)
                if l != 4:
                    select_edges(c, 0)
                weigh(c, 0)
                for k in range(KV):
                    if not last_chunk:
                        score_products(c + 1, k, False)
                    if l != 4 and k < KV - 1:
                        select_edges(c, k + 1)
                    early = 0 if l == 4 else 2
                    at = [unit(c, k, u) for u in range(early)]
                    if not last_chunk:
                        score_sums(c + 1, k)
                        restage(c + 1, k, compares < KV)
                    if k < KV - 1:
                        weigh(c, k + 1)
                    at += [unit(c, k, u) for u in range(early, U)]
                    add(c, k, 0, at[0])
                    if k < compares:
                        compare(c + 1, k + AHEAD)
                    for u in range(1, U + 1):
                        dve.wait_ge(added, (c * KV + k) * U + u)
                        if u < U:
                            add(c, k, u, at[u])

            stage_part(0, 0)
            stage_part(1, 1)
            for h in range(2):
                dve.memset(crow[:, h, :, :], -BIG).then_inc(cleared, 1)
            dve.wait_ge(cleared, 3)
            split_rows()
            for k in range(AHEAD):
                compare(0, k)
            for k in range(KV):
                score_products(0, k, True)
                score_sums(0, k)
                restage(0, k, False)
                compare(0, k + AHEAD)
            turn(0, False, KV)
            with dve.Fori(1, CH - 2) as c:
                turn(c, False, KV)
            turn(CH - 2, False, KV - AHEAD)
            turn(CH - 1, True, 0)


SCORE4_STEPS = 41


def score4(dve, step, raw, tmp, score, ask, answered, c):
    dot, y2, x2 = raw[:, 0, :], raw[:, 1, :], raw[:, 6, :]
    A, B, den, n2, t, up, lo, u, poly, f = (tmp[:, k, :] for k in range(10))
    stt, ts, tt = dve.scalar_tensor_tensor, dve.tensor_scalar, dve.tensor_tensor
    step(ts(f, dot, -2.0 * CURV, 1.0, ALU.mult, ALU.add))
    step(stt(A, y2, CURV, f, ALU.mult, ALU.add))
    step(ts(B, x2, -CURV, 1.0, ALU.mult, ALU.add))
    step(stt(den, x2, CURV * CURV, y2, ALU.mult, ALU.mult))
    step(tt(den, den, f, ALU.add))
    step(ts(den, den, MIN_NORM, None, ALU.max))
    step(dve.reciprocal(den, den))
    step(tt(tmp[:, 0:2, :], tmp[:, 0:2, :], den.unsqueeze(1).to_broadcast([P, 2, TC]), ALU.mult))
    step(tt(n2, A, A, ALU.mult))
    step(tt(n2, n2, x2, ALU.mult))
    step(tt(u, A, B, ALU.mult))
    step(stt(u, u, -2.0, dot, ALU.mult, ALU.mult))
    step(tt(n2, n2, u, ALU.add))
    step(tt(u, B, B, ALU.mult))
    step(tt(u, u, y2, ALU.mult))
    step(tt(n2, n2, u, ALU.add))
    step(ts(n2, n2, 1e-30, None, ALU.max))
    dve.nop(nofuse=True).then_inc(ask, 1)
    dve.wait_ge(answered, 2 * c + 1)
    step(ts(t, t, MIN_NORM, ROOT_C, ALU.max, ALU.mult))
    step(ts(t, t, MIN_NORM, TOP, ALU.max, ALU.min))
    atanh_ratio(dve, step, t, lo, up, u, poly, f, ask, (answered, 2 * c + 2))
    step(tt(tmp[:, 0:2, :], tmp[:, 0:2, :], f.unsqueeze(1).to_broadcast([P, 2, TC]), ALU.mult))
    heads = lambda k: k.unsqueeze(1).to_broadcast([P, H3, TC])
    us, ud = tmp[:, 2:2 + H3, :], raw[:, 2:2 + H3, :]
    step(tt(us, raw[:, 7:7 + H3, :], heads(A), ALU.mult))
    step(tt(ud, ud, heads(B), ALU.mult))
    step(tt(us, us, ud, ALU.subtract))
    step(stt(score[:, :, :], us, 0.2, us, ALU.mult, ALU.max))


def layer_norm(dve, step, m, y, sq, st, ask, answered):
    mean, var, rstd = (st[:, k, :].unsqueeze(2) for k in range(3))
    step(dve.tensor_reduce(mean, y[:, :, :], AX.X, ALU.add))
    step(dve.tensor_scalar(mean, mean, 1.0 / D, None, ALU.mult))
    step(dve.tensor_tensor(y[:, :, :], y[:, :, :], mean.to_broadcast([P, NB, D]), ALU.subtract))
    step(dve.tensor_tensor(sq[:, :, :], y[:, :, :], y[:, :, :], ALU.mult))
    step(dve.tensor_reduce(var, sq[:, :, :], AX.X, ALU.add))
    step(dve.tensor_scalar(var, var, 1.0 / D, EPS, ALU.mult, ALU.add))
    dve.nop(nofuse=True).then_inc(ask, 1)
    dve.wait_ge(*answered)
    step(dve.reciprocal(rstd, var))
    step(dve.tensor_tensor(m.x[:, :, :], y[:, :, :], rstd.to_broadcast([P, NB, D]), ALU.mult))


def finish0(nc, io, m):
    with ExitStack() as ctx:
        sb = lambda n, s, dt=F32: ctx.enter_context(nc.sbuf_tensor("f0_" + n, s, dt))
        sem = m.stage_sems()
        y, sq = sb("y", [P, NB, D]), sb("sq", [P, NB, D])
        w, sj, pr = sb("w", [P, D]), sb("sj", [P, NB]), sb("pr", [P, NB, D])
        st = sb("st", [P, 12, NB])
        w_in, step_sem, ask, ans = sem("w_in"), sem("step"), sem("ask"), sem("answered")
        block = ctx.enter_context(nc.Block())

        @block.sync
        def _(sp):
            sp.dma_start(w[:, :], io["wij"][1:2, :].to_broadcast([P, D])).then_inc(w_in, 16)

        @block.scalar
        def _(act):
            act.wait_ge(ask, 1)
            act.activation(st[:, 6:8, :], st[:, 4:6, :], ACT.Exp).then_inc(ans, 1)
            act.wait_ge(ask, 2)
            act.activation(st[:, 1, :], st[:, 1, :], ACT.Sqrt).then_inc(ans, 1)

        @block.vector
        def _(dve):
            step = Steps(dve, step_sem)
            dve.wait_ge(w_in, 16)
            acc = m.acc[:, 0:NB, :]
            own, most, top = st[:, 8, :], st[:, 9, :], st[:, 10, :]
            step(dve.tensor_tensor(pr[:, :, :], m.x[:, :, :], w[:, :].unsqueeze(1).to_broadcast([P, NB, D]), ALU.mult))
            step(dve.tensor_reduce(own.unsqueeze(2), pr[:, :, :], AX.X, ALU.add))
            step(dve.tensor_tensor(own, own, m.spread[:, 0:NB, 0], ALU.add))
            step(dve.scalar_tensor_tensor(own, own, 0.01, own, ALU.mult, ALU.max))
            step(dve.tensor_scalar(most, acc[:, :, D + 2], BIG, -BIG, ALU.mult, ALU.add))
            step(dve.tensor_tensor(most, most, acc[:, :, D + 1], ALU.add))
            step(dve.tensor_tensor(top, most, own, ALU.max))
            step(dve.tensor_tensor(st[:, 4, :], most, top, ALU.subtract))
            step(dve.tensor_tensor(st[:, 5, :], own, top, ALU.subtract))
            step(dve.tensor_scalar(st[:, 4:6, :], st[:, 4:6, :], -200.0, None, ALU.max))
            dve.nop(nofuse=True).then_inc(ask, 1)
            dve.wait_ge(ans, 1)
            fac, one = st[:, 6, :], st[:, 7, :]
            den = st[:, 11, :]
            step(dve.tensor_tensor(den, acc[:, :, D], fac, ALU.mult))
            step(dve.tensor_tensor(den, den, one, ALU.add))
            step(dve.reciprocal(den, den))
            step(dve.tensor_tensor(fac, fac, den, ALU.mult))
            step(dve.tensor_tensor(one, one, den, ALU.mult))
            step(dve.tensor_tensor(y[:, :, :], acc[:, :, 0:D], fac.unsqueeze(2).to_broadcast([P, NB, D]), ALU.mult))
            step(dve.tensor_tensor(sq[:, :, :], m.x[:, :, :], one.unsqueeze(2).to_broadcast([P, NB, D]), ALU.mult))
            step(dve.tensor_tensor(y[:, :, :], y[:, :, :], sq[:, :, :], ALU.add))
            step(dve.scalar_tensor_tensor(y[:, :, :], y[:, :, :], 0.0, m.x[:, :, :], ALU.max, ALU.add))
            layer_norm(dve, step, m, y, sq, st, ask, (ans, 2))


def finish_linear(nc, io, m, l):
    c = CONVS[l]
    H, B = c.H, c.B
    with ExitStack() as ctx:
        sb = lambda n, s, dt=F32: ctx.enter_context(nc.sbuf_tensor(f"f{l}_" + n, s, dt))
        sem = m.stage_sems()
        y, sq = sb("y", [P, NB, D]), sb("sq", [P, NB, D])
        st, den = sb("st", [P, 3, NB]), sb("den", [P, NB, H])
        step_sem, ask, ans = sem("step"), sem("ask"), sem("answered")
        block = ctx.enter_context(nc.Block())

        @block.scalar
        def _(act):
            if l != 1:
                act.wait_ge(ask, 1)
                act.activation(st[:, 1, :], st[:, 1, :], ACT.Sqrt).then_inc(ans, 1)

        @block.vector
        def _(dve):
            step = Steps(dve, step_sem)
            acc = m.acc[:, 0:NB, 0:c.PW].rearrange("p n (h b) -> p n h b", h=H)
            step(dve.tensor_scalar(den[:, :, :], acc[:, :, :, B - 1], 1.0e-20, None, ALU.max))
            step(dve.reciprocal(den[:, :, :], den[:, :, :]))
            step(dve.tensor_tensor(y[:, :, :].rearrange("p n (h b) -> p n h b", h=H), acc[:, :, :, 0:B - 1],
                                   den[:, :, :].unsqueeze(3).to_broadcast([P, NB, H, B - 1]), ALU.mult))
            step(dve.tensor_tensor(y[:, :, :], y[:, :, :], m.skip[:, :, :], ALU.add))
            if l == 1:
                step(dve.tensor_scalar(m.skip[:, :, :], y[:, :, :], 0.0, None, ALU.max))
                return
            step(dve.tensor_tensor(y[:, :, :], y[:, :, :], m.x[:, :, :], ALU.add))
            layer_norm(dve, step, m, y, sq, st, ask, (ans, 1))


ATANH_TERMS = [1.0 / (2 * k + 1) for k in range(9)]


def atanh_ratio(dve, step, t, lo, up, u, poly, out, ask, answered):
    dve.nop(nofuse=True).then_inc(ask, 1)
    step(dve.tensor_tensor(u, t, t, ALU.mult))
    step(dve.tensor_scalar(poly, u, ATANH_TERMS[-1], None, ALU.mult))
    for a in ATANH_TERMS[-2:0:-1]:
        step(dve.scalar_tensor_tensor(poly, poly, a, u, ALU.add, ALU.mult))
    step(dve.tensor_scalar(poly, poly, ATANH_TERMS[0], None, ALU.add))
    dve.wait_ge(*answered)
    step(dve.tensor_tensor(up, up, lo, ALU.subtract))
    step(dve.reciprocal(lo, t))
    step(dve.scalar_tensor_tensor(up, up, 0.5, lo, ALU.mult, ALU.mult))
    step(dve.tensor_scalar(u, t, 0.25, None, ALU.is_lt))
    step(dve.tensor_tensor(poly, poly, up, ALU.subtract))
    step(dve.tensor_tensor(poly, poly, u, ALU.mult))
    step(dve.tensor_tensor(out, up, poly, ALU.add))


CURV, MIN_NORM, TOP = 0.01, 1e-10, 1.0 - 1e-5
ROOT_C = 0.1


def prep4(nc, io, m):
    c = CONVS[4]
    W, PW = c.W, c.PW
    RH = R_ * H3
    with ExitStack() as ctx:
        sb = lambda n, s, dt=F32: ctx.enter_context(nc.sbuf_tensor("p4_" + n, s, dt))
        sem = m.stage_sems()
        w, av = sb("w", [D, RH * D]), sb("av", [D, RH])
        ht = sb("ht", [P, NB, D])
        st = sb("st", [P, 8, NB])
        xt = sb("xt", [D, 2, P])
        rb = sb("rb", [P, 2, R_, W])
        sq = sb("sq", [P, 4, 512])
        ms = sb("ms", [P, 8, RH])
        ohr = sb("ohr", [P, R_ * R_], I32)
        w_in, step_sem, ask, ans, ready = sem("w_in"), sem("step"), sem("ask"), sem("answered"), sem("ready")
        turned, moved, product, row_out = sem("turned"), sem("moved"), sem("product"), [sem("row_out0"), sem("row_out1")]
        rowed, squared, tanhed = sem("rowed"), sem("squared"), sem("tanhed")
        normed, made = sem("normed"), sem("made")
        block = ctx.enter_context(nc.Block())

        @block.sync
        def _(sp):
            sp.dma_start(w[:, :], io["Wrel"]).then_inc(w_in, 16)
            sp.dma_start(av[:, :], io["AV"]).then_inc(w_in, 16)
            tab = m.table[4].rearrange("(b p r) w -> b p (r w)", p=P, r=R_)
            for b in range(NB):
                sp.wait_ge(rowed, b + 1)
                sp.dma_start(tab[b], rb[:, b % 2, :, :].rearrange("p r w -> p (r w)")).then_inc(row_out[b % 2], 16)
            sp.wait_ge(row_out[0], 16 * ((NB + 1) // 2))
            sp.wait_ge(row_out[1], 16 * (NB // 2))

        @block.gpsimd
        def _(pool):
            step = Steps(pool, ready)
            step(pool.iota(ohr[:, :], [[-1, R_], [1, R_]], base=0, channel_multiplier=0))
            step(pool.memset(m.spread[:, NB:NB + 1, :], 0.0))

        @block.scalar
        def _(act):
            act.wait_ge(ask, 1)
            act.activation(st[:, 1, :], st[:, 0, :], ACT.Sqrt).then_inc(ans, 1)
            act.wait_ge(ask, 2)
            act.activation(st[:, 3, :], st[:, 2, :], ACT.Ln, bias=1.0)
            act.activation(st[:, 4, :], st[:, 2, :], ACT.Ln, bias=1.0, scale=-1.0).then_inc(ans, 1)
            for b in range(NB):
                act.wait_ge(turned, b + 1)
                act.copy(xt[:, 0, :], m.bank[0][0:D, 0:P])
                act.copy(xt[:, 1, :], m.bank[0][0:D, P:2 * P]).then_inc(moved, 1)
                act.wait_ge(product, b + 1)
                if b:
                    act.wait_ge(made, 2 * b - 1)
                for k in range(4):
                    ins = act.activation(sq[:, k, :], m.bank[2 + k][:, :], ACT.Square)
                ins.then_inc(squared, 1)
                act.wait_ge(made, 2 * b + 1)
                act.activation(ms[:, 1, :], ms[:, 0, :], ACT.Sqrt).then_inc(normed, 1)
                act.wait_ge(made, 2 * b + 2)
                act.activation(ms[:, 3, :], ms[:, 2, :], ACT.Tanh).then_inc(tanhed, 1)

        @block.tensor
        def _(pe):
            pe.wait_ge(w_in, 32)
            pe.wait_ge(ask, 3)
            for b in range(NB):
                if b:
                    pe.wait_ge(moved, b)
                pe.transpose(m.bank[0][0:D, 0:P], ht[:, b, :], m.ident[:, :])
                pe.transpose(m.bank[0][0:D, P:2 * P], m.x[:, b, :], m.ident[:, :]).then_inc(turned, 1)
                pe.wait_ge(moved, b + 1)
                if b:
                    pe.wait_ge(rowed, b)
                for k in range(4):
                    pe.matmul(m.bank[2 + k][:, :], xt[:, 0, :], w[:, k * 512:(k + 1) * 512], start=True, stop=True)
                pe.matmul(m.bank[1][:, 0:RH], xt[:, 1, :], av[:, :], start=True, stop=True).then_inc(product, 1)

        @block.vector
        def _(dve):
            step = Steps(dve, step_sem)
            n2, nrm, t, up, lo, u, poly, ratio = (st[:, k, :] for k in range(8))
            step(dve.tensor_tensor(ht[:, :, :], m.x[:, :, :], m.x[:, :, :], ALU.mult))
            step(dve.tensor_reduce(n2.unsqueeze(2), ht[:, :, :], AX.X, ALU.add))
            step(dve.tensor_copy(m.spread[:, 0:NB, D + RH], n2))
            step(dve.tensor_copy(m.spread[:, 0:NB, 0:D], m.x[:, :, :]))
            step(dve.tensor_scalar(n2, n2, 1e-30, None, ALU.max))
            dve.nop(nofuse=True).then_inc(ask, 1)
            dve.wait_ge(ans, 1)
            step(dve.tensor_scalar(nrm, nrm, MIN_NORM, None, ALU.max))
            step(dve.tensor_scalar(t, nrm, ROOT_C, MIN_NORM, ALU.mult, ALU.max))
            step(dve.tensor_scalar(t, t, TOP, None, ALU.min))
            atanh_ratio(dve, step, t, lo, up, u, poly, ratio, ask, (ans, 2))
            step(dve.tensor_tensor(ht[:, :, :], m.x[:, :, :], ratio.unsqueeze(2).to_broadcast([P, NB, D]), ALU.mult))
            dve.nop(nofuse=True).then_inc(ask, 1)
            dve.wait_ge(ready, 2)
            for s in range(2):
                step(dve.tensor_scalar(rb[:, s, :, W - R_:W], ohr[:, :].rearrange("p (r k) -> p r k", r=R_), 0.0, None,
                                       ALU.is_equal))
                blocks = rb[:, s, :, 0:PW].rearrange("p r (h k) -> p r h k", h=H3)
                step(dve.memset(blocks[:, :, :, B3 - 1:B3], 1.0))
            a = [ms[:, k, :] for k in range(8)]
            for b in range(NB):
                s = b % 2
                if b >= 2:
                    dve.wait_ge(row_out[s], 16 * (b // 2))
                blocks = rb[:, s, :, 0:PW].rearrange("p r (h k) -> p r h k", h=H3)
                step(dve.tensor_copy(rb[:, s, :, PW:PW + D], m.x[:, b:b + 1, :].to_broadcast([P, R_, D])))
                step(dve.tensor_copy(rb[:, s, :, PW + D:PW + D + 1],
                                     m.spread[:, b:b + 1, D + RH:D + RH + 1].to_broadcast([P, R_, 1])))
                dve.wait_ge(squared, b + 1)
                step(dve.tensor_reduce(a[0].unsqueeze(2), sq[:, :, :].rearrange("p k (q o) -> p (k q) o", o=D), AX.X, ALU.add))
                step(dve.tensor_scalar(a[7], a[0], 1e-30, None, ALU.max))
                step(dve.tensor_copy(a[0], a[7]))
                dve.nop(nofuse=True).then_inc(made, 1)
                step(dve.tensor_copy(m.spread[:, b, D:D + RH], m.bank[1][:, 0:RH]))
                step(dve.tensor_copy(rb[:, s, :, PW + D + 1:PW + D + 1 + H3],
                                     m.bank[1][:, 0:RH].rearrange("p (r h) -> p r h", h=H3)))
                dve.wait_ge(normed, b + 1)
                step(dve.tensor_scalar(a[2], a[1], MIN_NORM, ROOT_C, ALU.max, ALU.mult))
                dve.nop(nofuse=True).then_inc(made, 1)
                step(dve.reciprocal(a[4], a[2]))
                dve.wait_ge(tanhed, b + 1)
                step(dve.tensor_tensor(a[4], a[3], a[4], ALU.mult))
                step(dve.tensor_tensor(a[5], a[4], a[4], ALU.mult))
                step(dve.tensor_tensor(a[5], a[5], a[0], ALU.mult))
                step(dve.tensor_scalar(a[5], a[5], -CURV, 1.0, ALU.mult, ALU.add))
                step(dve.tensor_scalar(a[5], a[5], 1e-6, 0.5, ALU.add, ALU.mult))
                step(dve.reciprocal(a[6], a[5]))
                step(dve.tensor_tensor(a[4], a[4], a[6], ALU.mult))
                step(dve.tensor_copy(blocks[:, :, :, D], a[6].rearrange("p (r h) -> p r h", h=H3)))
                for k in range(4):
                    fac = a[4].rearrange("p (r h) -> p r h", h=H3)[:, 2 * k:2 * k + 2, :]
                    step(dve.tensor_tensor(blocks[:, 2 * k:2 * k + 2, :, 0:D],
                                           m.bank[2 + k][:, :].rearrange("p (r h o) -> p r h o", r=2, h=H3),
                                           fac.unsqueeze(3).to_broadcast([P, 2, H3, D]), ALU.mult))
                dve.nop(nofuse=True).then_inc(rowed, 1)


def finish4(nc, io, m):
    NH = NB * H3
    with ExitStack() as ctx:
        sb = lambda n, s, dt=F32: ctx.enter_context(nc.sbuf_tensor("f4_" + n, s, dt))
        sem = m.stage_sems()
        y, sq, st = sb("y", [P, NB, D]), sb("sq", [P, NB, D]), sb("st", [P, 8, NB])
        mid, mq, a = sb("mid", [P, NH, D]), sb("mq", [P, NH, D]), sb("a", [P, 11, NH])
        step_sem, ask, ans, out_sem = sem("step"), sem("ask"), sem("answered"), sem("out")
        block = ctx.enter_context(nc.Block())

        @block.scalar
        def _(act):
            act.wait_ge(ask, 1)
            act.activation(a[:, 3, :], a[:, 2, :], ACT.Sqrt).then_inc(ans, 1)
            act.wait_ge(ask, 2)
            act.activation(a[:, 6, :], a[:, 5, :], ACT.Ln, bias=1.0)
            act.activation(a[:, 7, :], a[:, 5, :], ACT.Ln, bias=1.0, scale=-1.0).then_inc(ans, 1)
            act.wait_ge(ask, 3)
            act.activation(st[:, 1, :], st[:, 0, :], ACT.Sqrt).then_inc(ans, 1)
            act.wait_ge(ask, 4)
            act.activation(st[:, 3, :], st[:, 2, :], ACT.Tanh).then_inc(ans, 1)
            act.wait_ge(ask, 5)
            act.activation(st[:, 1, :], st[:, 1, :], ACT.Sqrt).then_inc(ans, 1)

        @block.vector
        def _(dve):
            step = Steps(dve, step_sem)
            ts, tt = dve.tensor_scalar, dve.tensor_tensor
            acc = m.acc[:, 0:NB, :].rearrange("p n (h b) -> p (n h) b", h=H3)
            rz, den, n2, nrm, p, t, up, lo, u, poly, f = (a[:, k, :] for k in range(11))
            wide = lambda k: k.unsqueeze(2).to_broadcast([P, NH, D])
            step(ts(rz, acc[:, :, D + 1], 1e-20, None, ALU.max))
            step(dve.reciprocal(rz, rz))
            step(tt(den, acc[:, :, D], rz, ALU.mult))
            step(ts(den, den, 1e-6, None, ALU.add))
            step(dve.reciprocal(den, den))
            step(tt(rz, rz, den, ALU.mult))
            step(tt(mid[:, :, :], acc[:, :, 0:D], wide(rz), ALU.mult))
            step(tt(mq[:, :, :], mid[:, :, :], mid[:, :, :], ALU.mult))
            step(dve.tensor_reduce(n2.unsqueeze(2), mq[:, :, :], AX.X, ALU.add))
            step(ts(n2, n2, 1e-30, None, ALU.max))
            dve.nop(nofuse=True).then_inc(ask, 1)
            dve.wait_ge(ans, 1)
            step(ts(nrm, nrm, MIN_NORM, None, ALU.max))
            step(dve.reciprocal(p, nrm))
            step(ts(p, p, TOP / ROOT_C, 1.0, ALU.mult, ALU.min))
            step(tt(t, nrm, p, ALU.mult))
            step(ts(t, t, MIN_NORM, ROOT_C, ALU.max, ALU.mult))
            step(ts(t, t, MIN_NORM, TOP, ALU.max, ALU.min))
            atanh_ratio(dve, step, t, lo, up, u, poly, f, ask, (ans, 2))
            step(tt(f, f, p, ALU.mult))
            step(ts(f, f, 1.0 / H3, None, ALU.mult))
            step(tt(mid[:, :, :], mid[:, :, :], wide(f), ALU.mult))
            step(dve.tensor_reduce(y[:, :, :], mid[:, :, :].rearrange("p (n h) d -> p n d h", h=H3), AX.X, ALU.add))
            n2, nrm, t, th, f = (st[:, k, :] for k in range(5))
            step(tt(sq[:, :, :], y[:, :, :], y[:, :, :], ALU.mult))
            step(dve.tensor_reduce(n2.unsqueeze(2), sq[:, :, :], AX.X, ALU.add))
            step(ts(n2, n2, 1e-30, None, ALU.max))
            dve.nop(nofuse=True).then_inc(ask, 1)
            dve.wait_ge(ans, 3)
            step(ts(t, nrm, MIN_NORM, ROOT_C, ALU.max, ALU.mult))
            dve.nop(nofuse=True).then_inc(ask, 1)
            step(dve.reciprocal(f, t))
            dve.wait_ge(ans, 4)
            step(tt(f, th, f, ALU.mult))
            step(tt(y[:, :, :], y[:, :, :], f.unsqueeze(2).to_broadcast([P, NB, D]), ALU.mult))
            step(tt(y[:, :, :], y[:, :, :], m.x[:, :, :], ALU.add))
            layer_norm(dve, step, m, y, sq, st, ask, (ans, 5))
            dve.nop(nofuse=True).then_inc(ask, 1)

        @block.sync
        def _(sp):
            sp.wait_ge(ask, 6)
            out = io["out"]
            sp.dma_start(out[0:NFULL * P, :].rearrange("(b p) d -> p b d", p=P), m.x[:, 0:NFULL, :]).then_inc(out_sem, 16)
            sp.dma_start(out[NFULL * P:N, :], m.x[0:NREST, NFULL, :]).then_inc(out_sem, 16)
            sp.wait_ge(out_sem, 32)


def kernel(**inputs):
    import numpy as _np
    import concourse.bacc as _bacc
    from concourse import mybir as _mybir
    from concourse.bass_utils import run_bass_kernel_spmd as _run

    i = {k: _np.asarray(v) for k, v in inputs.items()}
    cat = _np.concatenate

    def packed(prefix, suffix, turned):
        w = [i[f"{prefix}_W{n}{suffix}"] for n in "qkvs"]
        b = [i[f"{prefix}_b{n}{suffix}"] for n in "qkvs"]
        return cat([cat([k.T if turned else k for k in w], axis=1), cat(b)[None, :]], axis=0)

    arrays = {
        "x": i["x"], "src": i["src"], "dst": i["dst"], "edge_type_8": i["edge_type_8"],
        "wij": _np.stack([i["L0_gnn_w_i"], i["L0_gnn_w_j"]]),
        "W1": packed("L1_gnn", "1", True), "W2": packed("L1_gnn", "2", True), "W3": packed("L2_gnn", "", False),
        "Wrel": i["L3_gnn_rel_weight"].transpose(2, 0, 1, 3).reshape(64, -1),
        "AV": i["L3_gnn_attn_vec"].transpose(2, 0, 1).reshape(64, -1),
    }
    arrays = {f"in_{k}": _np.ascontiguousarray(v) for k, v in arrays.items()}
    nc = _bacc.Bacc("TRN2", target_bir_lowering=False, num_devices=1)
    io = {k[3:]: nc.dram_tensor(k, v.shape, _mybir.dt.from_np(v.dtype), kind="ExternalInput").ap()
          for k, v in arrays.items()}
    io["out"] = nc.dram_tensor("out_x", (3125, 64), _mybir.dt.float32, kind="ExternalOutput").ap()
    build(nc, io)
    r = _run(nc, [arrays], core_ids=[0])
    return r.results[0]["out_x"]
```

```python
from contextlib import ExitStack

import numpy as np
import concourse.bass as bass
from concourse import mybir

F32 = mybir.dt.float32
BF16 = mybir.dt.bfloat16
I32 = mybir.dt.int32
ALU = mybir.AluOpType
ACT = mybir.ActivationFunctionType
AX = mybir.AxisListType

P = 128
N, D, E = 3125, 64, 100000
NB = -(-N // P)
NFULL = N // P
NREST = N - NFULL * P
NPAD = NB * P
GU = 2
UE = GU * P
TC = 64
UC = TC // GU
CH = -(-((E + NB * (UE - 1)) // UE) // UC)
UNITS = CH * UC
T = CH * TC
TB = -(-T // P)
EC, ER = E // P, E % P
BIG = 1.0e30
EPS = 1e-5


class Steps:

    def __init__(self, eng, sem):
        self.eng, self.sem, self.n, self.base, self.per = eng, sem, 0, 0, None

    def __call__(self, ins):
        ins.then_inc(self.sem, 1)
        self.n += 1
        self.eng.wait_ge(self.sem, self.base + self.n)

    def begin(self, i, per):
        assert self.per is None or self.n == self.per, (self.n, self.per)
        self.resume(i, per, 0)

    def resume(self, i, per, n):
        self.base, self.n, self.per = i * per, n, per


def rows(dram, width):
    return dram.rearrange("(b p) w -> p b w", p=P)


def build(nc, io):
    ctx = ExitStack()
    with ctx:
        m = Memory(nc, ctx)
        setup(nc, io, m)
        prep0(nc, io, m)
        conv(nc, io, m, 0)
        finish0(nc, io, m)
        for l in (1, 2, 3):
            prep_linear(nc, io, m, l)
            conv(nc, io, m, l)
            finish_linear(nc, io, m, l)
        prep4(nc, io, m)
        conv(nc, io, m, 4)
        finish4(nc, io, m)


class Conv:

    def __init__(self, heads, block, row, spread, raw, extra=0, tiles=8, ring=4):
        self.G, self.ring = tiles, ring
        self.H, self.B, self.W, self.Q, self.R, self.X = heads, block, row, spread, raw, extra
        self.PW = heads * block
        self.HP = min(heads, 2)
        self.NS = heads // self.HP


R_, H3 = 8, 4
B3 = D + 2
CONVS = [Conv(1, D + 1, D + 2, 1, 1, extra=2),
         Conv(1, D + 1, 2 * D + 1, D, 1),
         Conv(1, D + 1, 2 * D + 1, D, 1),
         Conv(8, D // 8 + 1, 8 * 9 + D, D, 8),
         Conv(H3, B3, H3 * B3 + D + 1 + H3 + R_, D + R_ * H3 + 1, 11, tiles=4, ring=4)]


class Memory:

    def __init__(self, nc, ctx):
        def sb(name, shape, dt=F32):
            return ctx.enter_context(nc.sbuf_tensor(name, shape, dt))

        def dram(name, shape, dt=F32):
            return nc.dram_tensor(name, shape, dt, kind="Internal").ap()

        self.nc = nc
        self.sems = [[ctx.enter_context(nc.semaphore(f"bank{k}_{j}")) for j in range(40)] for k in range(2)]
        self.stages = 0
        self.gathered = [[ctx.enter_context(nc.semaphore(f"gathered{l}_{s}")) for s in range(CONVS[l].ring)] for l in range(5)]
        self.bank = [ctx.enter_context(nc.psum_tensor(f"bank{i}", [P, 512], F32)) for i in range(8)]
        self.ident = sb("ident", [P, P])
        self.ones = sb("ones", [P, P])
        self.iota_p = sb("iota_p", [P, 1])
        self.iota_f = sb("iota_f", [P, P])
        self.eye4 = sb("eye4", [4, 4, 2])
        self.unit_bucket = sb("unit_bucket", [1, UNITS], I32)
        self.dl = sb("dl", [P, T])
        self.src_t = sb("src_t", [P, T], I32)
        self.s8_t = sb("s8_t", [P, T], I32)
        self.cut_f = sb("cut_f", [P, CH, P])
        self.cut_b = sb("cut_b", [P, CH, P])
        self.row_cut = sb("row_cut", [4, 2, CH, TC])
        self.dl0 = sb("dl0", [4, CH])
        self.x = sb("x", [P, NB, D])
        self.skip = sb("skip", [P, NB, D])
        self.acc = sb("acc", [P, NB + 1, H3 * B3])
        self.spread = sb("spread", [P, NB + 1, D + R_ * H3 + 1])
        self.flat_dl = dram("flat_dl", [T * P], BF16)
        self.table = [dram(f"table{l}", [NPAD * (R_ if l == 4 else 1), c.W]) for l, c in enumerate(CONVS)]

    def stage_sems(self):
        mine, other = self.sems[self.stages % 2], self.sems[1 - self.stages % 2]
        if self.stages:
            lo = min(s.num for s in other)
            assert max(s.num for s in other) == lo + len(other) - 1
            self.nc.sync.sem_clear(range(lo, lo + len(other)))
        self.stages += 1
        left = list(mine)
        return lambda name: left.pop(0)


def setup(nc, io, m):
    ctx = ExitStack()
    with ctx:
        def sb(name, shape, dt=F32):
            return ctx.enter_context(nc.sbuf_tensor("st_" + name, shape, dt))

        sem = m.stage_sems()

        def dram(name, shape, dt=F32):
            return nc.dram_tensor(name, shape, dt, kind="Internal").ap()

        UQ = UNITS // 4
        dst_i, src_i, typ_i = (sb(n, [P, EC + 1], I32) for n in ("dst_i", "src_i", "typ_i"))
        dst_f, junk = sb("dst_f", [P, EC + 1]), sb("junk", [P, EC + 1])
        s8_i = sb("s8_i", [P, EC + 1], I32)
        cnt = sb("cnt", [P, NB + 1])
        row = sb("row", [1, 6, NB + 1])
        rowi = sb("rowi", [1, 2, NB + 1], I32)
        col = sb("col", [NB, 2])
        iota_i = sb("iota_i", [P, T], I32)
        iota_pi = sb("iota_pi", [P, 1], I32)
        iota_t = sb("iota_t", [NB, T])
        past = sb("past", [NB, T])
        e0 = sb("e0", [UQ, 12])
        e0_i = sb("e0_i", [UQ, 4], I32)
        bvt = sb("bvt", [P, TB])
        pad = sb("pad", [1, 3, UE], I32)
        gat = [[sb(f"gat{a}{h}", [UQ, UE], I32) for h in range(4)] for a in range(3)]
        nat_i = [sb(f"nat_i{a}", [P, TB, P], I32) for a in range(3)]
        nat_f = [sb(f"nat_f{a}", [P, TB, P]) for a in range(3)]
        ok, key = sb("ok", [P, TB, P]), sb("key", [P, TB, P])
        dl_b = sb("dl_b", [P, TB, P], BF16)
        own, prev, nxt = (sb(n, [P, CH, P]) for n in ("own", "prev", "nxt"))
        edge2 = sb("edge2", [1, 2])
        rc = sb("rc", [TC, 2, CH])
        rcw = sb("rcw", [TC, 2, CH, 4])
        lin = [dram(f"lin{a}", [E + UE], I32) for a in range(3)]
        flat = [dram(f"flat{a}", [T * P], I32) for a in range(3)]
        flat_key = dram("flat_key", [T * P + 2])

        loaded, x_in, pool_step, consts = sem("loaded"), sem("x_in"), sem("pool_step"), sem("consts")
        dve_step, stored, flat_out, flat_in = sem("dve_step"), sem("stored"), sem("flat_out"), sem("flat_in")
        key_out, key_in = sem("key_out"), sem("key_in")
        gathered = ctx.enter_context(nc.semaphore("gathered"))
        (x_zero, s8_made, e0_made, key_made, counted, rowed, past_made, floated, dl_made, cuts_made) = (
            sem(n) for n in ("x_zero", "s8_made", "e0_made", "key_made", "counted", "rowed", "past_made",
                             "floated", "dl_made", "cuts_made"))
        starts, cols, units, turned, cuts_turned = (sem(n) for n in ("starts", "cols", "units", "turned",
                                                                     "cuts_turned"))
        taken = sem("taken")
        block = ctx.enter_context(nc.Block())

        def edges(a):
            return a[0:P * EC].rearrange("(p c) -> p c", p=P), a[P * EC:E].rearrange("(p c) -> p c", c=1)

        def blocks(flat_array):
            full = T // P
            yield flat_array[0:full * P * P].rearrange("(k i e) -> i k e", i=P, e=P), P, slice(0, full)
            if T % P:
                yield flat_array[full * P * P:T * P].rearrange("(k i e) -> i k e", k=1, e=P), T % P, slice(full, full + 1)

        NPARTS = 1 + (T % P > 0)

        @block.sync
        def _(sp):
            for tile, name in ((dst_i, "dst"), (src_i, "src"), (typ_i, "edge_type_8")):
                body, rest = edges(io[name])
                sp.dma_start(tile[:, 0:EC], body).then_inc(loaded, 16)
                sp.dma_start(tile[0:ER, EC:EC + 1], rest).then_inc(loaded, 16)
            xin = io["x"]
            sp.wait_ge(x_zero, 1)
            sp.dma_start(m.x[:, 0:NFULL, :], xin[0:NFULL * P, :].rearrange("(b p) d -> p b d", p=P)).then_inc(x_in, 16)
            sp.dma_start(m.x[0:NREST, NFULL, :], xin[NFULL * P:N, :]).then_inc(x_in, 16)
            sp.wait_ge(s8_made, 1)
            for a, tile in enumerate((dst_i, src_i, s8_i)):
                body, rest = edges(lin[a][0:E])
                sp.dma_start(body, tile[:, 0:EC]).then_inc(stored, 16)
                sp.dma_start(rest, tile[0:ER, EC:EC + 1]).then_inc(stored, 16)
                sp.dma_start(lin[a][E:E + UE].rearrange("(o w) -> o w", o=1), pad[:, a, :]).then_inc(stored, 16)
            sp.wait_ge(gathered, 16 * 12)
            for a in range(3):
                for h in range(4):
                    sp.dma_start(flat[a][h * UQ * UE:(h + 1) * UQ * UE].rearrange("(v e) -> v e", e=UE),
                                 gat[a][h][:, :]).then_inc(flat_out, 16)
            sp.wait_ge(flat_out, 16 * 12)
            for a in range(3):
                for src, n, ks in blocks(flat[a]):
                    sp.dma_start(nat_i[a][0:n, ks, :], src).then_inc(flat_in, 16)
            sp.wait_ge(key_made, 1)
            for tile, array in ((key, flat_key[1:1 + T * P]), (dl_b, m.flat_dl)):
                for out, n, ks in blocks(array):
                    sp.dma_start(out, tile[0:n, ks, :]).then_inc(key_out, 16)
            sp.dma_start(flat_key[0:1].rearrange("(o w) -> o w", o=1), edge2[:, 0:1]).then_inc(key_out, 16)
            sp.dma_start(flat_key[T * P + 1:T * P + 2].rearrange("(o w) -> o w", o=1), edge2[:, 1:2]).then_inc(key_out, 16)
            sp.wait_ge(key_out, 16 * (2 * NPARTS + 2))
            for at, tile in enumerate((prev, own, nxt)):
                for half in range(2):
                    sp.dma_start(tile[half * TC:(half + 1) * TC, :, :],
                                 flat_key[at:at + T * P].rearrange("(c t e) -> t c e", t=TC, e=P)).then_inc(key_in, 16)

        @block.gpsimd
        def _(pool):
            step = Steps(pool, pool_step)
            step(pool.memset(m.ident[:, :], 0.0))
            step(pool.affine_select(out=m.ident[:, :], in_=m.ident[:, :], compare_op=ALU.not_equal, fill=1.0,
                                    base=0, pattern=[[-1, P]], channel_multiplier=1))
            step(pool.memset(m.eye4[:, :, :], 0.0))
            step(pool.affine_select(out=m.eye4[:, :, :], in_=m.eye4[:, :, :], compare_op=ALU.not_equal, fill=1.0,
                                    base=0, pattern=[[-1, 4], [0, 2]], channel_multiplier=1))
            step(pool.iota(iota_i[:, :], [[1, T]], base=0, channel_multiplier=0))
            pool.memset(m.ones[:, :], 1.0).then_inc(consts, 1)
            pool.iota(iota_pi[:, :], [[0, 1]], base=0, channel_multiplier=1).then_inc(consts, 1)
            pool.wait_ge(e0_made, 1)
            pool.wait_ge(stored, 16 * 9)
            for a in range(3):
                for h in range(4):
                    pool.indirect_dma_start(gat[a][h][:, :], None, lin[a].rearrange("(n o) -> n o", o=1),
                                            bass.IndirectOffsetOnAxis(ap=e0_i[:, h:h + 1], axis=0)).then_inc(gathered, 16)

        @block.vector
        def _(dve):
            step = Steps(dve, dve_step)

            def tell(sem):
                dve.nop(nofuse=True).then_inc(sem, 1)

            step(dve.memset(m.x[:, :, :], 0.0))
            tell(x_zero)
            step(dve.memset(pad[:, 0, :], NPAD))
            step(dve.memset(pad[:, 1:3, :], 0))
            step(dve.memset(edge2[:, :], -1000.0))
            step(dve.memset(cnt[:, :], 0.0))
            step(dve.memset(dst_f[:, :], 1.0e9))
            dve.wait_ge(loaded, 16 * 6)
            step(dve.tensor_scalar(s8_i[:, 0:EC], src_i[:, 0:EC], float(R_), None, ALU.mult))
            step(dve.tensor_scalar(s8_i[0:ER, EC:EC + 1], src_i[0:ER, EC:EC + 1], float(R_), None, ALU.mult))
            step(dve.tensor_tensor(s8_i[:, 0:EC], s8_i[:, 0:EC], typ_i[:, 0:EC], ALU.add))
            step(dve.tensor_tensor(s8_i[0:ER, EC:EC + 1], s8_i[0:ER, EC:EC + 1], typ_i[0:ER, EC:EC + 1], ALU.add))
            tell(s8_made)
            step(dve.tensor_copy(dst_f[:, 0:EC], dst_i[:, 0:EC]))
            step(dve.tensor_copy(dst_f[0:ER, EC:EC + 1], dst_i[0:ER, EC:EC + 1]))
            for b in range(1, NB + 1):
                step(dve.tensor_scalar(junk[:, :], dst_f[:, :], float(P * b), 0.0, ALU.is_lt, ALU.add,
                                       accum_out=cnt[:, b:b + 1]))
            dve.wait_ge(consts, 2)
            step(dve.tensor_copy(m.iota_p[:, :], iota_pi[:, :]))
            step(dve.tensor_copy(m.iota_f[:, :], iota_i[:, 0:P]))
            step(dve.tensor_copy(iota_t[:, :], iota_i[0:NB, :]))
            tell(counted)
            dve.wait_ge(starts, 1)
            start, n, nu, us, g, dg = (row[:, k, :] for k in range(6))
            step(dve.tensor_copy(start, m.bank[0][0:1, 0:NB + 1]))
            step(dve.tensor_tensor(n[:, 0:NB], start[:, 1:NB + 1], start[:, 0:NB], ALU.subtract))
            step(dve.tensor_scalar(rowi[:, 0, 0:NB], n[:, 0:NB], float(UE - 1), None, ALU.add))
            step(dve.tensor_scalar(rowi[:, 1, 0:NB], rowi[:, 0, 0:NB], UE.bit_length() - 1, None, ALU.arith_shift_right))
            step(dve.tensor_copy(nu[:, 0:NB], rowi[:, 1, 0:NB]))
            step(dve.memset(us[:, 0:1], 0.0))
            step(dve.tensor_tensor_scan(us[:, 1:NB + 1], m.ones[0:1, 0:NB], nu[:, 0:NB], 0.0, ALU.mult, ALU.add))
            step(dve.scalar_tensor_tensor(g, us, float(-UE), start, ALU.mult, ALU.add))
            step(dve.tensor_tensor(dg[:, 0:NB], g[:, 1:NB + 1], g[:, 0:NB], ALU.subtract))
            step(dve.tensor_scalar(us, us, float(GU), None, ALU.mult))
            tell(rowed)
            dve.wait_ge(cols, 1)
            step(dve.tensor_copy(col[:, :], m.bank[1][0:NB, 0:2]))
            step(dve.tensor_scalar(past[:, :], iota_t[:, :], col[:, 0:1], None, ALU.is_ge))
            tell(past_made)
            dve.wait_ge(units, 1)
            step(dve.tensor_copy(m.unit_bucket[:, :], m.bank[2][0:1, 0:UNITS]))
            step(dve.tensor_copy(e0[:, 0:4], m.bank[3][0:UQ, 0:4]))
            for h in range(4):
                step(dve.tensor_scalar(e0[:, 4 + h:5 + h], m.iota_p[0:UQ, :], float(h * UQ), float(UE), ALU.add, ALU.mult))
            step(dve.tensor_tensor(e0[:, 8:12], e0[:, 0:4], e0[:, 4:8], ALU.add))
            step(dve.tensor_scalar(e0_i[:, :], e0[:, 8:12], float(E), 0.0, ALU.min, ALU.max))
            tell(e0_made)
            step(dve.tensor_copy(bvt[:, :], m.bank[4][:, 0:TB]))
            if T % P:
                for a in range(3):
                    step(dve.memset(nat_f[a][:, TB - 1, :], 0.0))
            dve.wait_ge(flat_in, 16 * 3 * NPARTS)
            for a in range(3):
                for _, n, ks in blocks(flat[a]):
                    step(dve.tensor_copy(nat_f[a][0:n, ks, :], nat_i[a][0:n, ks, :]))
            dst_n = nat_f[0][:, :, :]
            wide = bvt[:, :].unsqueeze(2).to_broadcast([P, TB, P])
            step(dve.scalar_tensor_tensor(dst_n, wide, float(-P), dst_n, ALU.mult, ALU.add))
            step(dve.tensor_scalar(ok[:, :, :], dst_n, float(P), None, ALU.is_lt))
            step(dve.scalar_tensor_tensor(dst_n, dst_n, 1.0, ok[:, :, :], ALU.add, ALU.mult))
            step(dve.tensor_scalar(dst_n, dst_n, -1.0, None, ALU.add))
            tell(floated)
            step(dve.scalar_tensor_tensor(key[:, :, :], wide, float(P + 2), dst_n, ALU.mult, ALU.add))
            step(dve.tensor_copy(dl_b[:, :, :], dst_n))
            tell(key_made)
            outs = (m.dl, m.src_t, m.s8_t)
            for a in range(3):
                dve.wait_ge(turned, a + 1)
                at = 4 * (a % 2)
                step(dve.tensor_copy(outs[a][:, 0:512], m.bank[at][:, :]))
                step(dve.tensor_copy(outs[a][:, 512:T], m.bank[at + 1][:, 0:T - 512]))
                tell(taken)
            tell(dl_made)
            dve.wait_ge(key_in, 16 * 6)
            for k, (cut, other) in enumerate(((m.cut_f, prev), (m.cut_b, nxt))):
                out = cut[:, :, ::-1] if k else cut[:, :, :]
                step(dve.tensor_tensor(out, own[:, :, :], other[:, :, :], ALU.not_equal))
                step(dve.tensor_scalar(cut[:, :, :], cut[:, :, :], -BIG, None, ALU.mult))
                step(dve.tensor_reduce(rc[:, k, :].unsqueeze(2), cut[0:TC, :, :], AX.X, ALU.min))
            step(dve.tensor_copy(rcw[:, :, :, :], rc[:, :, :].unsqueeze(3).to_broadcast([TC, 2, CH, 4])))
            tell(cuts_made)
            dve.wait_ge(cuts_turned, 1)
            step(dve.tensor_copy(m.dl0[:, :], m.bank[6][0:4, 0:CH]))
            for k in range(2):
                for h in range(2):
                    n = min(8, CH - 8 * h)
                    step(dve.tensor_copy(m.row_cut[:, k, 8 * h:8 * h + n, ::(-1 if k else 1)],
                                         m.bank[2 * k + h][0:4, 0:n * TC].rearrange("s (c t) -> s c t", t=TC)))
            dve.wait_ge(x_in, 32)

        @block.tensor
        def _(pe):
            pe.wait_ge(counted, 1)
            pe.matmul(m.bank[0][0:1, 0:NB + 1], m.ones[:, 0:1], cnt[:, :], start=True, stop=True).then_inc(starts, 1)
            pe.wait_ge(rowed, 1)
            pe.matmul(m.bank[1][0:NB, 0:1], row[:, 3, 1:NB + 1], m.ones[0:1, 0:1], start=True, stop=True)
            pe.matmul(m.bank[1][0:NB, 1:2], row[:, 5, 0:NB], m.ones[0:1, 0:1], start=True, stop=True).then_inc(cols, 1)
            pe.wait_ge(past_made, 1)
            pe.matmul(m.bank[2][0:1, 0:UNITS], m.ones[0:NB, 0:1], past[:, 0:T:GU], start=True, stop=True)
            for h in range(4):
                pe.matmul(m.bank[3][0:UQ, h:h + 1], past[:, h * UQ * GU:(h + 1) * UQ * GU:GU], col[:, 1:2],
                          start=True, stop=True)
            for k in range(TB):
                n = min(P, T - k * P)
                mm = pe.matmul(m.bank[4][0:n, k:k + 1], past[:, k * P:k * P + n], m.ones[0:NB, 0:1], start=True, stop=True)
            if T % P:
                mm = pe.matmul(m.bank[4][T % P:P, TB - 1:TB], past[:, 0:P - T % P], m.ones[0:NB, 0:1], start=True, stop=True)
            mm.then_inc(units, 1)
            pe.wait_ge(floated, 1)
            for a in range(3):
                if a == 2:
                    pe.wait_ge(taken, 1)
                for k in range(TB):
                    n = min(P, T - k * P)
                    at = m.bank[4 * (a % 2) + k // 4][:, k % 4 * P:k % 4 * P + n]
                    mm = pe.transpose(at, nat_f[a][0:n, k, :], m.ident[0:n, 0:n])
                mm.then_inc(turned, 1)
            pe.wait_ge(dl_made, 1)
            pe.wait_ge(cuts_made, 1)
            pe.matmul(m.bank[6][0:4, 0:CH], m.ones[0:1, 0:4], m.dl[0:1, 0:T:TC], start=True, stop=True)
            for k in range(2):
                for c in range(CH):
                    at = m.bank[2 * k + c // 8][0:4, c % 8 * TC:(c % 8 + 1) * TC]
                    mm = pe.transpose(at, rcw[:, k, c, :], m.ident[0:TC, 0:TC])
            mm.then_inc(cuts_turned, 1)


def prep0(nc, io, m):
    c = CONVS[0]
    with ExitStack() as ctx:
        sb = lambda n, s, dt=F32: ctx.enter_context(nc.sbuf_tensor("p0_" + n, s, dt))
        sem = m.stage_sems()
        w = sb("w", [P, 2, D])
        tb = sb("tb", [P, NB, c.W])
        prod = sb("prod", [P, NB, D])
        w_in, step_sem, made, out_sem = sem("w_in"), sem("step"), sem("made"), sem("out")
        block = ctx.enter_context(nc.Block())

        @block.sync
        def _(sp):
            sp.dma_start(w[:, :, :], io["wij"].rearrange("(o k) d -> o k d", o=1).to_broadcast([P, 2, D])).then_inc(w_in, 16)
            sp.wait_ge(made, 1)
            sp.dma_start(rows(m.table[0], c.W), tb[:, :, :]).then_inc(out_sem, 16)
            sp.wait_ge(out_sem, 16)

        @block.vector
        def _(dve):
            step = Steps(dve, step_sem)
            step(dve.memset(m.spread[:, :, 0:1], 0.0))
            step(dve.tensor_copy(tb[:, :, 0:D], m.x[:, :, :]))
            step(dve.memset(tb[:, :, D:D + 1], 1.0))
            dve.wait_ge(w_in, 16)
            for k, out in enumerate((m.spread[:, 0:NB, 0:1], tb[:, :, D + 1:D + 2])):
                step(dve.tensor_tensor(prod[:, :, :], m.x[:, :, :], w[:, k:k + 1, :].to_broadcast([P, NB, D]), ALU.mult))
                step(dve.tensor_reduce(out, prod[:, :, :], AX.X, ALU.add))
            dve.nop(nofuse=True).then_inc(made, 1)


def prep_linear(nc, io, m, l):
    c = CONVS[l]
    inp = m.skip if l == 2 else m.x
    with ExitStack() as ctx:
        sb = lambda n, s, dt=F32: ctx.enter_context(nc.sbuf_tensor(f"pl{l}_" + n, s, dt))
        sem = m.stage_sems()
        w = sb("w", [D + 1, 4 * D])
        xt = sb("xt", [D + 1, 2, P])
        tb = sb("tb", [P, NB, c.W])
        w_in, ready, turned, moved = sem("w_in"), sem("ready"), sem("turned"), sem("moved")
        product, taken_d, taken_a, out_sem = sem("product"), sem("taken_d"), sem("taken_a"), sem("out")
        block = ctx.enter_context(nc.Block())
        vb = D // c.H
        payload = tb[:, :, 0:c.PW].rearrange("p b (h v) -> p b h v", h=c.H)

        @block.sync
        def _(sp):
            sp.dma_start(w[:, :], io[f"W{l}"]).then_inc(w_in, 16)
            sp.wait_ge(taken_d, NB)
            sp.wait_ge(taken_a, NB)
            sp.dma_start(rows(m.table[l], c.W), tb[:, :, :]).then_inc(out_sem, 16)
            sp.wait_ge(out_sem, 16)

        @block.gpsimd
        def _(pool):
            step = Steps(pool, ready)
            step(pool.memset(xt[D:D + 1, :, :], 1.0))
            step(pool.memset(payload[:, :, :, vb:vb + 1], 1.0))
            step(pool.memset(m.spread[:, NB:NB + 1, :], 0.0))

        @block.tensor
        def _(pe):
            pe.wait_ge(w_in, 16)
            pe.wait_ge(ready, 3)
            for b in range(NB + 1):
                if b < NB:
                    if b >= 2:
                        pe.wait_ge(moved, b - 1)
                    pe.transpose(m.bank[b % 2][0:D, 0:P], inp[:, b, :], m.ident[:, :]).then_inc(turned, 1)
                if b >= 1:
                    k = b - 1
                    pe.wait_ge(moved, k + 1)
                    if k >= 2:
                        pe.wait_ge(taken_d, k - 1)
                        pe.wait_ge(taken_a, k - 1)
                    pe.matmul(m.bank[2 + k % 2][:, 0:4 * D], xt[:, k % 2, :], w[:, :], start=True, stop=True)\
                        .then_inc(product, 1)

        @block.scalar
        def _(act):
            for b in range(NB + 1):
                if b < NB:
                    act.wait_ge(turned, b + 1)
                    if b >= 2:
                        act.wait_ge(product, b - 1)
                    act.copy(xt[0:D, b % 2, :], m.bank[b % 2][0:D, 0:P]).then_inc(moved, 1)
                if b >= 1:
                    k = b - 1
                    act.wait_ge(product, k + 1)
                    act.copy(payload[:, k, :, 0:vb],
                             m.bank[2 + k % 2][:, 2 * D:3 * D].rearrange("p (h v) -> p h v", h=c.H)).then_inc(taken_a, 1)

        @block.vector
        def _(dve):
            dve.wait_ge(ready, 3)
            for b in range(NB):
                dve.wait_ge(taken_a, b + 1)
                bank = m.bank[2 + b % 2]
                dve.tensor_copy(m.spread[:, b, 0:D], bank[:, 0:D])
                dve.tensor_copy(tb[:, b, c.PW:c.W], bank[:, D:2 * D])
                dve.tensor_copy(m.skip[:, b, :], bank[:, 3 * D:4 * D]).then_inc(taken_d, 1)


def conv(nc, io, m, l):
    c_ = CONVS[l]
    W, Q, R, H, B, PW, X, HP, NS = c_.W, c_.Q, c_.R, c_.H, c_.B, c_.PW, c_.X, c_.HP, c_.NS
    AW = PW + X
    HPP = HP * TC
    scale = {0: 1.0, 1: float(D) ** -0.5, 2: float(D) ** -0.5, 3: float(D // 8) ** -0.5, 4: 1.0}[l]
    idx = m.s8_t if l == 4 else m.src_t
    G, RING = c_.G, c_.ring
    KV, U = TC // G, G // GU
    VE, QV = G * P, 2
    PART = RING * G
    PARTS = KV // RING
    UPB = min(U, 512 // AW)
    SLOTS, AHEAD = 4, 3
    HALF = (NB + 2) // 2
    with ExitStack() as ctx:
        sb = lambda n, s, dt=F32: ctx.enter_context(nc.sbuf_tensor(f"c{l}_" + n, s, dt))
        sem = m.stage_sems()
        stage = sb("stage", [P, 2, PART], I32)
        g = sb("g", [P, RING, G, W])
        keep = sb("keep", [P, KV, G, PW])
        dlw = sb("dlw", [P, 2, QV * VE], BF16)
        oh_n = sb("oh_n", [P, SLOTS, VE], BF16)
        parts = sb("parts", [P, NB + 1, 3, Q], BF16)
        raw = sb("raw", [P, R, TC])
        if l == 4:
            free, at = m.spread[:, :, :].rearrange("p b q -> p (b q)"), [0]

            def over(n, s):
                size = s[1] * s[2]
                at[0] += size
                return free[0:s[0], at[0] - size:at[0]].rearrange("p (a b) -> p a b", a=s[1])
            dl_c = over("dl_c", [P, 1, TC])
            tmp, score, prod2 = over("tmp", [P, 10, TC]), over("score", [P, H, TC]), over("prod2", [P, G, R_ * H3])
        else:
            over, score = sb, raw
        prod = over("prod", [P, G, D])
        S = over("S", [HPP, NS, P])
        f, b = over("f", [HPP, NS, P]), over("b", [HPP, NS, P])
        ex = over("ex", [HPP, NS, P])
        lrow = sb("lrow", [NS, 2, HP, TC])
        crow = sb("crow", [NS, 2, HP, TC + 1])
        cin = sb("cin", [NS, 2, HP, TC])
        rho, dm = sb("rho", [NS, HP]), sb("dm", [NS, HP])
        rho_b = sb("rho_b", [NS, NS, HP])
        first = sb("first", [NS, P])
        carry = sb("carry", [HPP, 2, NS])
        fac = sb("fac", [P, H])
        wt = sb("wt", [P, H, TC])
        if X:
            ends = sb("ends", [TC, 2, P])
            ext = sb("ext", [P, X, TC])
        if l == 4:
            oh_e = m.skip[:, :, :].rearrange("p b d -> p (b d)")[:, 0:2 * G * P].rearrange("p (s g n) -> p s g n", s=2, g=G)
        else:
            oh_e = sb("oh_e", [P, 2, G, P])
        wp = sb("wp", [P, 2, G, AW])

        gathered = m.gathered[l]
        staged, split, onehot, spread, scored = (sem(n) for n in ("staged", "split", "onehot", "spread", "scored"))
        kept, dl_in = [sem(f"kept{s}") for s in range(RING)], [sem("dl_in0"), sem("dl_in1")]
        visit_step, soft_step, sides_a, sides_b = sem("visit_step"), sem("soft_step"), sem("sides_a"), sem("sides_b")
        weighted, summed, added, cleared = sem("weighted"), sem("summed"), sem("added"), sem("cleared")
        final, scans, carries, rescale = sem("final"), sem("scans"), sem("carries"), sem("rescale")
        s_in, rho_in, wt_in = sem("s_in"), sem("rho_in"), sem("wt_in")
        to_scan, to_rows, to_cols, to_nodes, to_tiles = (sem(n) for n in ("to_scan", "to_rows", "to_cols",
                                                                          "to_nodes", "to_tiles"))
        shifted, expd = sem("shifted"), sem("expd")
        ask, answered = sem("ask"), sem("answered")
        dl_set, apart, selected = sem("dl_set"), sem("apart"), sem("selected")
        block = ctx.enter_context(nc.Block())

        def gathers(c, k):
            return (c * (KV // RING) + k // RING + 1) * (16 * G)

        def copies(c, k):
            return (c * (KV // RING) + k // RING + 1) * 16

        SPLIT_STEPS = 10
        FINAL_STEPS = {0: 1, 4: SCORE4_STEPS}.get(l, 0)
        SOFT_STEPS = FINAL_STEPS + (2 if X else 0) + 6 * NS + 2 * HP + 12

        def sums(k, u):
            return m.bank[4 + 2 * (k % 2) + u // UPB][:, u % UPB * AW:(u % UPB + 1) * AW]

        @block.gpsimd
        def _(pool):
            pool.memset(m.acc[:, :, 0:AW], 0.0).then_inc(cleared, 1)

            def chunk(c, first_chunk):
                for k in range(KV):
                    s = k % RING
                    if s == 0:
                        pool.wait_ge(staged, c * (KV // RING) + k // RING + 1)
                        pool.nop(nofuse=True)
                    if not (first_chunk and k < RING):
                        pool.wait_ge(scored, c * KV + (k + 1 - RING))
                        pool.nop(nofuse=True)
                        if l == 4:
                            pool.wait_ge(sides_a, c * KV + (k + 1 - RING))
                            pool.nop(nofuse=True)
                        pool.wait_ge(kept[s], (c * (KV // RING) + k // RING) * 16)
                        pool.nop(nofuse=True)
                    for j in range(G):
                        at = s * G + j
                        pool.indirect_dma_start(g[:, s, j, :], None, m.table[l],
                                                bass.IndirectOffsetOnAxis(ap=stage[:, k // RING % 2, at:at + 1], axis=0))\
                            .then_inc(gathered[s], 16)
            chunk(0, True)
            with pool.Fori(1, CH) as c:
                chunk(c, False)

        @block.sync
        def _(sp):
            NQ = KV // QV

            def load_dl(q, slot):
                sp.dma_start(dlw[:, slot, :], m.flat_dl[bass.ds(q * (QV * VE), QV * VE)].rearrange("(o w) -> o w", o=1)
                             .to_broadcast([P, QV * VE])).then_inc(dl_in[slot], 16)

            def chunk(c, first_chunk, last_chunk):
                for k in range(KV):
                    s = k % RING
                    sp.wait_ge(gathered[s], gathers(c, k))
                    sp.nop(nofuse=True)
                    if not first_chunk:
                        sp.wait_ge(weighted, (c - 1) * KV + k + 1)
                    sp.dma_start(keep[:, k, :, :], g[:, s, :, 0:PW]).then_inc(kept[s], 16)
                    q = k // QV
                    if k % QV == QV - 1 and not (last_chunk and q >= NQ - 3):
                        sp.wait_ge(onehot, c * KV + QV * (q + 2))
                        sp.nop(nofuse=True)
                        load_dl(c * NQ + (q + 3), (q + 3) % 2)
            load_dl(0, 0)
            load_dl(1, 1)
            sp.wait_ge(onehot, QV)
            load_dl(2, 0)
            chunk(0, True, False)
            with sp.Fori(1, CH - 1) as c:
                chunk(c, False, False)
            chunk(CH - 1, False, True)

        @block.tensor
        def _(pe):
            def buckets(eng, c, k):
                return [eng.value_load(m.unit_bucket[0:1, bass.ds(c * UC + (U * k + u), 1)], min_val=0, max_val=NB)
                        for u in range(U)]

            def do_spread(c, k, early):
                bs = buckets(pe, c, k)
                pe.wait_ge(onehot, c * KV + (k + 1))
                if not (early and k < 2):
                    pe.wait_ge(scored, c * KV + (k - 1))
                    if l == 4:
                        pe.wait_ge(sides_a, c * KV + (k - 1))
                for j in range(G):
                    for part in range(3):
                        mm = pe.matmul(m.bank[k % 2][:, j * Q:(j + 1) * Q], oh_n[:, k % SLOTS, j * P:(j + 1) * P],
                                       parts[:, bass.ds(bs[j // GU], 1), part, :], start=(part == 0), stop=(part == 2))
                mm.then_inc(spread, 1)

            def do_sum(c, k, early):
                pe.wait_ge(weighted, c * KV + (k + 1))
                if X:
                    pe.wait_ge(sides_b, c * KV + (k + 1))
                if l == 4:
                    pe.wait_ge(selected, c * KV + (k + 1))
                if not (early and k < 2):
                    pe.wait_ge(added, (c * KV + (k - 1)) * U)
                for j in range(G):
                    mm = pe.matmul(sums(k, j // GU), oh_e[:, k % 2, j, :], wp[:, k % 2, j, :],
                                   start=(j % GU == 0), stop=(j % GU == GU - 1))
                mm.then_inc(summed, 1)

            def do_soft(c):
                if l in (0, 4):
                    pe.wait_ge(final, c + 1)
                    pe.nop(nofuse=True)
                else:
                    pe.wait_ge(scored, (c + 1) * KV)
                    pe.nop(nofuse=True)
                for n in range(NS):
                    mm = pe.transpose(m.bank[2][0:HPP, n * P:(n + 1) * P],
                                      score[:, n * HP:(n + 1) * HP, :].rearrange("p h t -> p (h t)"), m.ident[:, :])
                mm.then_inc(to_scan, 1)
                pe.wait_ge(scans, c + 1)
                pe.nop(nofuse=True)
                pe.transpose(m.bank[3][0:NS, 0:HPP], f[:, :, P - 1], m.ident[0:HPP, 0:HPP])
                pe.transpose(m.bank[3][0:NS, HPP:2 * HPP], b[:, :, 0], m.ident[0:HPP, 0:HPP]).then_inc(to_rows, 1)
                pe.wait_ge(carries, c + 1)
                pe.nop(nofuse=True)
                for k in range(2):
                    mm = pe.transpose(m.bank[4][0:HPP, k * NS:(k + 1) * NS],
                                      cin[:, k, :, :].rearrange("s h t -> s (h t)"), m.ident[0:NS, 0:NS])
                mm.then_inc(to_cols, 1)
                pe.wait_ge(rescale, c + 1)
                pe.nop(nofuse=True)
                pe.matmul(m.bank[5][:, 0:H], first[:, :], rho_b[:, :, :].rearrange("s n h -> s (n h)"),
                          start=True, stop=True).then_inc(to_nodes, 1)
                for n in range(NS):
                    pe.wait_ge(expd, c * NS + (n + 1))
                    pe.nop(nofuse=True)
                    mm = pe.transpose(m.bank[6][:, n * HPP:(n + 1) * HPP], ex[:, n, :], m.ident[0:HPP, 0:HPP])
                for n in range(X):
                    if n == 0:
                        pe.wait_ge(ask, c + 1)
                        pe.nop(nofuse=True)
                    mm = pe.transpose(m.bank[6][:, (H + n) * TC:(H + n + 1) * TC], ends[:, n, :], m.ident[0:TC, 0:TC])
                mm.then_inc(to_tiles, 1)
                pe.wait_ge(wt_in, c + 1)
                pe.nop(nofuse=True)

            def turn(c, first_chunk, last_chunk):
                if not last_chunk:
                    do_spread(c + 1, 0, False)
                do_soft(c)
                for k in range(KV):
                    if not last_chunk and k < KV - 1:
                        do_spread(c + 1, k + 1, False)
                    do_sum(c, k, first_chunk)

            pe.wait_ge(split, SPLIT_STEPS)
            for k in range(KV):
                do_spread(0, k, True)
            turn(0, True, False)
            with pe.Fori(1, CH - 1) as c:
                turn(c, False, False)
            turn(CH - 1, False, True)

        @block.scalar
        def _(act):
            def take_sides(c, k):
                act.wait_ge(scored, c * KV + (k + 1))
                bank = m.bank[k % 2][:, 0:G * Q].rearrange("p (g q) -> p g q", q=Q)
                out = raw[:, :, k * G:(k + 1) * G].rearrange("p r g -> p g r")
                act.copy(out[:, :, 1:2], bank[:, :, Q - 1:Q])
                act.copy(out[:, :, 6:11], g[:, k % RING, :, PW + D:PW + D + 5]).then_inc(sides_a, 1)

            def select_edges(c, k):
                if k >= 2:
                    act.wait_ge(summed, c * KV + (k - 1))
                for j in range(G):
                    act.activation(oh_e[:, k % 2, j, :], m.iota_f[:, :], ACT.Abs, bias=dl_c[:, 0, k * G + j:k * G + j + 1],
                                   scale=-1.0).then_inc(apart, 1)
                act.wait_ge(apart, (c * KV + (k + 1)) * G)
                act.activation(oh_e[:, k % 2, :, :], oh_e[:, k % 2, :, :], ACT.Relu, bias=1.0, scale=-1.0)\
                    .then_inc(selected, 1)

            def copy_ends(c, k, early):
                if not (early and k < 2):
                    act.wait_ge(summed, c * KV + (k - 1))
                act.copy(wp[:, k % 2, :, PW:AW], ext[:, :, k * G:(k + 1) * G].rearrange("p x g -> p g x"))\
                    .then_inc(sides_b, 1)

            def turn(c, first_chunk, last_chunk):
                if l == 4:
                    act.wait_ge(ask, 2 * c + 1)
                    act.activation(tmp[:, 4, :], tmp[:, 3, :], ACT.Sqrt, scale=CURV).then_inc(answered, 1)
                    act.wait_ge(ask, 2 * c + 2)
                    act.activation(tmp[:, 5, :], tmp[:, 4, :], ACT.Ln, bias=1.0)
                    act.activation(tmp[:, 6, :], tmp[:, 4, :], ACT.Ln, bias=1.0, scale=-1.0).then_inc(answered, 1)
                act.wait_ge(to_scan, c + 1)
                act.copy(S[:, :, :].rearrange("p n e -> p (n e)"), m.bank[2][0:HPP, 0:NS * P]).then_inc(s_in, 1)
                act.wait_ge(carries, c + 1)
                act.activation(rho[:, :], dm[:, :], ACT.Exp, scale=scale).then_inc(rho_in, 1)
                for n in range(NS):
                    act.wait_ge(shifted, c * NS + (n + 1))
                    act.activation(ex[:, n, :], S[:, n, :], ACT.Exp, scale=scale).then_inc(expd, 1)
                act.wait_ge(to_tiles, c + 1)
                if X:
                    act.copy(ext[:, :, :].rearrange("p x t -> p (x t)"), m.bank[6][:, H * TC:(H + X) * TC])
                act.copy(wt[:, :, :].rearrange("p h t -> p (h t)"), m.bank[6][:, 0:H * TC]).then_inc(wt_in, 1)
                if X:
                    act.wait_ge(wt_in, c + 1)
                if l == 4:
                    act.wait_ge(dl_set, c + 1)
                    select_edges(c, 0)
                for k in range(KV):
                    if l == 4 and k < KV - 1:
                        select_edges(c, k + 1)
                    if l == 4 and not last_chunk:
                        take_sides(c + 1, k)
                    if X:
                        copy_ends(c, k, first_chunk)
            if l == 4:
                for k in range(KV):
                    take_sides(0, k)
            turn(0, True, False)
            with act.Fori(1, CH - 1) as c:
                turn(c, False, False)
            turn(CH - 1, False, True)

        @block.vector
        def _(dve):
            s_step = Steps(dve, soft_step)

            def stage_part(j, slot):
                dve.tensor_copy(stage[:, slot, :], idx[:, bass.ds(j * PART, PART)]).then_inc(staged, 1)

            def restage(c, k, is_last):
                part = k // RING
                if k % RING == RING - 1 and not (is_last and part >= PARTS - 2):
                    stage_part(c * PARTS + (part + 2), part % 2)

            def split_rows():
                step = Steps(dve, split)
                for lo in (0, HALF):
                    n = min(HALF, NB + 1 - lo)
                    rest = wp[:, :, :, :].rearrange("p s g w -> p (s g w)")[:, 0:n * Q].rearrange("p (b q) -> p b q", q=Q)
                    row, left = m.spread[:, lo:lo + n, 0:Q], parts[:, lo:lo + n, :, :]
                    step(dve.tensor_copy(left[:, :, 0, :], row))
                    step(dve.tensor_tensor(rest, row, left[:, :, 0, :], ALU.subtract))
                    step(dve.tensor_copy(left[:, :, 1, :], rest))
                    step(dve.tensor_tensor(rest, rest, left[:, :, 1, :], ALU.subtract))
                    step(dve.tensor_copy(left[:, :, 2, :], rest))
                assert step.n == SPLIT_STEPS

            def compare(c, k):
                if k >= KV:
                    c, k = c + 1, k - KV
                q = k // QV
                if k % QV == 0:
                    dve.wait_ge(dl_in[q % 2], (c * (KV // QV // 2) + q // 2 + 1) * 16)
                dve.tensor_scalar(oh_n[:, k % SLOTS, :], dlw[:, q % 2, k % QV * VE:(k % QV + 1) * VE],
                                  m.iota_p[:, 0:1], None, ALU.is_equal).then_inc(onehot, 1)

            def score_products(c, k, early):
                s = k % RING
                dve.wait_ge(spread, c * KV + (k + 1))
                dve.wait_ge(gathered[s], gathers(c, k))
                bank = m.bank[k % 2][:, 0:G * Q].rearrange("p (g q) -> p g q", q=Q)
                out = raw[:, :, k * G:(k + 1) * G].rearrange("p r g -> p g r")
                if l == 0:
                    dve.tensor_tensor(out, bank, g[:, s, :, W - 1:W], ALU.add).then_inc(scored, 1)
                    return
                if not (early and k == 0):
                    dve.wait_ge(scored, c * KV + k)
                if l == 4:
                    dve.tensor_tensor(prod2[:, :, :].rearrange("p g (r h) -> p g r h", h=H3),
                                      bank[:, :, D:D + R_ * H3].rearrange("p g (r h) -> p g r h", h=H3),
                                      g[:, s, :, W - R_:W].unsqueeze(3).to_broadcast([P, G, R_, H3]), ALU.mult).then_inc(visit_step, 1)
                dve.tensor_tensor(prod[:, :, :], bank[:, :, 0:D], g[:, s, :, PW:PW + D], ALU.mult).then_inc(visit_step, 1)

            def score_sums(c, k):
                out = raw[:, :, k * G:(k + 1) * G].rearrange("p r g -> p g r")
                if l == 0:
                    return
                dve.wait_ge(visit_step, (c * KV + (k + 1)) * (2 if l == 4 else 1))
                if l == 4:
                    dve.tensor_reduce(out[:, :, 2:6], prod2[:, :, :].rearrange("p g (r h) -> p g h r", h=H3),
                                      AX.X, ALU.add)
                if l == 3:
                    dve.tensor_reduce(out, prod[:, :, :].rearrange("p g (h c) -> p g h c", h=H), AX.X, ALU.add)\
                        .then_inc(scored, 1)
                else:
                    dve.tensor_reduce(out[:, :, 0:1], prod[:, :, :], AX.X, ALU.add).then_inc(scored, 1)

            def select_edges(c, k):
                dve.tensor_tensor(oh_e[:, k % 2, :, :], m.iota_f[:, :].unsqueeze(1).to_broadcast([P, G, P]),
                                  m.dl[:, bass.ds(c * TC + k * G, G)].unsqueeze(2).to_broadcast([P, G, P]),
                                  ALU.is_equal)

            def weigh(c, k):
                dve.wait_ge(kept[k % RING], copies(c, k))
                w = wt[:, :, k * G:(k + 1) * G].rearrange("p h g -> p g h").unsqueeze(3).to_broadcast([P, G, H, B])
                dve.tensor_tensor(wp[:, k % 2, :, 0:PW].rearrange("p g (h b) -> p g h b", b=B),
                                  keep[:, k, :, :].rearrange("p g (h b) -> p g h b", b=B), w, ALU.mult)\
                    .then_inc(weighted, 1)

            def add(c, k, u, bucket):
                if u == 0:
                    dve.wait_ge(summed, c * KV + (k + 1))
                acc = m.acc[:, bass.ds(bucket, 1), 0:AW]
                dve.tensor_tensor(acc, acc, sums(k, u).unsqueeze(1), ALU.add).then_inc(added, 1)

            def unit(c, k, u):
                return dve.value_load(m.unit_bucket[0:1, bass.ds(c * UC + (U * k + u), 1)], min_val=0, max_val=NB)

            def final_scores(c, step):
                step.begin(c, SOFT_STEPS)
                if l not in (0, 4):
                    return
                dve.wait_ge(scored, (c + 1) * KV)
                if l == 0:
                    step(dve.scalar_tensor_tensor(raw[:, 0, :], raw[:, 0, :], 0.01, raw[:, 0, :], ALU.mult, ALU.max))
                elif l == 4:
                    dve.wait_ge(sides_a, (c + 1) * KV)
                    score4(dve, step, raw, tmp, score, ask, answered, c)
                dve.nop(nofuse=True).then_inc(final, 1)

            def do_soft(c, step):
                step.resume(c, SOFT_STEPS, FINAL_STEPS)
                if l == 4:
                    dve.tensor_copy(dl_c[:, :, :], m.dl[:, bass.ds(c * TC, TC)].unsqueeze(1)).then_inc(dl_set, 1)
                dve.wait_ge(s_in, c + 1)
                cuts = [cut[0:HPP, bass.ds(c, 1), :].rearrange("p o e -> p (o e)") for cut in (m.cut_f, m.cut_b)]
                for n in range(NS):
                    step(dve.tensor_tensor_scan(f[:, n, :], cuts[0], S[:, n, :], -BIG, ALU.add, ALU.max))
                    step(dve.tensor_tensor_scan(b[:, n, ::-1], cuts[1], S[:, n, ::-1], -BIG, ALU.add, ALU.max))
                dve.nop(nofuse=True).then_inc(scans, 1)
                dve.wait_ge(to_rows, c + 1)
                step(dve.tensor_copy(lrow[:, :, :, :], m.bank[3][0:NS, 0:2 * HPP].rearrange("s (k h t) -> s k h t", k=2, h=HP)))
                step(dve.tensor_copy(crow[:, 0, :, 0], crow[:, 0, :, TC]))
                row_cuts = [m.row_cut[0:NS, k, bass.ds(c, 1), :].rearrange("s o t -> s (o t)") for k in range(2)]
                for h in range(HP):
                    step(dve.tensor_tensor_scan(crow[:, 0, h, 1:TC + 1], row_cuts[0], lrow[:, 0, h, :],
                                                crow[:, 0, h, 0:1], ALU.add, ALU.max))
                    step(dve.tensor_tensor_scan(crow[:, 1, h, TC - 1::-1], row_cuts[1], lrow[:, 1, h, ::-1], -BIG,
                                                ALU.add, ALU.max))
                step(dve.tensor_copy(cin[:, 0, :, :], crow[:, 0, :, 0:TC]))
                step(dve.tensor_copy(cin[:, 1, :, :], crow[:, 1, :, 1:TC + 1]))
                step(dve.tensor_tensor(dm[:, :], crow[:, 0, :, 0], crow[:, 1, :, 0], ALU.max))
                step(dve.tensor_tensor(dm[:, :], crow[:, 0, :, 0], dm[:, :], ALU.subtract))
                step(dve.tensor_scalar(dm[:, :], dm[:, :], -3000.0, None, ALU.max))
                dve.nop(nofuse=True).then_inc(carries, 1)
                step(dve.tensor_scalar(first[:, :], m.iota_f[0:NS, :], m.dl0[0:NS, bass.ds(c, 1)], None, ALU.is_equal))
                dve.wait_ge(rho_in, c + 1)
                step(dve.scalar_tensor_tensor(rho_b[:, :, :], rho[:, :].unsqueeze(1).to_broadcast([NS, NS, HP]), -1.0,
                                              m.eye4[0:NS, 0:NS, 0:HP], ALU.add, ALU.mult))
                dve.nop(nofuse=True).then_inc(rescale, 1)
                dve.wait_ge(to_cols, c + 1)
                step(dve.tensor_copy(carry[:, :, :], m.bank[4][0:HPP, 0:2 * NS].rearrange("p (k n) -> p k n", k=2)))
                for n in range(NS):
                    step(dve.tensor_tensor_scan(f[:, n, :], cuts[0], S[:, n, :], carry[:, 0, n:n + 1], ALU.add, ALU.max))
                    step(dve.tensor_tensor_scan(b[:, n, ::-1], cuts[1], S[:, n, ::-1], carry[:, 1, n:n + 1],
                                                ALU.add, ALU.max))
                    step(dve.tensor_tensor(f[:, n, :], f[:, n, :], b[:, n, :], ALU.max))
                    step(dve.tensor_tensor(S[:, n, :], S[:, n, :], f[:, n, :], ALU.subtract))
                    dve.nop(nofuse=True).then_inc(shifted, 1)
                if X:
                    step(dve.tensor_scalar(ends[:, 1, ::-1], cuts[1], 0.0, None, ALU.is_lt))
                    step(dve.tensor_tensor(ends[:, 0, :], ends[:, 1, :], f[:, 0, :], ALU.mult))
                    dve.nop(nofuse=True).then_inc(ask, 1)
                dve.wait_ge(to_nodes, c + 1)
                step(dve.tensor_scalar(fac[:, :], m.bank[5][:, 0:H], 1.0, None, ALU.add))
                bucket = unit(c, 0, 0)
                acc = m.acc[:, bass.ds(bucket, 1), 0:PW].rearrange("p o (h b) -> p (o h) b", h=H)
                step(dve.tensor_tensor(acc, acc, fac[:, :].unsqueeze(2).to_broadcast([P, H, B]), ALU.mult))
                dve.wait_ge(wt_in, c + 1)

            def turn(c, last_chunk, compares):
                do_soft(c, s_step)
                if l != 4:
                    select_edges(c, 0)
                weigh(c, 0)
                for k in range(KV):
                    if not last_chunk:
                        score_products(c + 1, k, False)
                    if l != 4 and k < KV - 1:
                        select_edges(c, k + 1)
                    early = U // 2
                    at = [unit(c, k, u) for u in range(early)]
                    if not last_chunk:
                        score_sums(c + 1, k)
                        restage(c + 1, k, compares < KV)
                    if k < KV - 1:
                        weigh(c, k + 1)
                    at += [unit(c, k, u) for u in range(early, U)]
                    if k == KV - 1 and not last_chunk:
                        final_scores(c + 1, s_step)
                    if k:
                        dve.wait_ge(added, (c * KV + k) * U)
                    add(c, k, 0, at[0])
                    if k < compares:
                        compare(c + 1, k + AHEAD)
                    for u in range(1, U):
                        dve.wait_ge(added, (c * KV + k) * U + u)
                        add(c, k, u, at[u])
                dve.wait_ge(added, (c + 1) * (KV * U))
                assert s_step.n == (SOFT_STEPS if last_chunk else FINAL_STEPS)

            stage_part(0, 0)
            stage_part(1, 1)
            for h in range(2):
                dve.memset(crow[:, h, :, :], -BIG).then_inc(cleared, 1)
            dve.wait_ge(cleared, 3)
            split_rows()
            for k in range(AHEAD):
                compare(0, k)
            for k in range(KV):
                score_products(0, k, True)
                score_sums(0, k)
                restage(0, k, False)
                compare(0, k + AHEAD)
            final_scores(0, s_step)
            turn(0, False, KV)
            with dve.Fori(1, CH - 2) as c:
                turn(c, False, KV)
            turn(CH - 2, False, KV - AHEAD)
            turn(CH - 1, True, 0)


SCORE4_STEPS = 38


def score4(dve, step, raw, tmp, score, ask, answered, c):
    dot, y2, x2 = raw[:, 0, :], raw[:, 1, :], raw[:, 6, :]
    B, A, den, n2, t, up, lo, u, poly, f = (tmp[:, k, :] for k in range(10))
    stt, ts, tt = dve.scalar_tensor_tensor, dve.tensor_scalar, dve.tensor_tensor
    step(ts(f, dot, -2.0 * CURV, 1.0, ALU.mult, ALU.add))
    step(stt(A, y2, CURV, f, ALU.mult, ALU.add))
    step(ts(B, x2, -CURV, 1.0, ALU.mult, ALU.add))
    step(stt(den, x2, CURV * CURV, y2, ALU.mult, ALU.mult))
    step(tt(den, den, f, ALU.add))
    step(ts(den, den, MIN_NORM, None, ALU.max))
    step(dve.reciprocal(den, den))
    step(tt(tmp[:, 0:2, :], tmp[:, 0:2, :], den.unsqueeze(1).to_broadcast([P, 2, TC]), ALU.mult))
    step(tt(u, A, B, ALU.mult))
    step(stt(u, u, -2.0, dot, ALU.mult, ALU.mult))
    step(tt(tmp[:, 8:10, :], tmp[:, 0:2, :], tmp[:, 0:2, :], ALU.mult))
    step(tt(tmp[:, 8:10, :], tmp[:, 8:10, :], raw[:, 1:7:5, :], ALU.mult))
    step(tt(n2, poly, f, ALU.add))
    step(tt(n2, n2, u, ALU.add))
    step(ts(n2, n2, MIN_NORM * MIN_NORM, None, ALU.max))
    dve.nop(nofuse=True).then_inc(ask, 1)
    dve.wait_ge(answered, 2 * c + 1)
    step(ts(t, t, MIN_NORM, TOP, ALU.max, ALU.min))
    atanh_ratio(dve, step, t, lo, up, u, poly, f, ask, (answered, 2 * c + 2))
    step(tt(tmp[:, 0:2, :], tmp[:, 0:2, :], f.unsqueeze(1).to_broadcast([P, 2, TC]), ALU.mult))
    heads = lambda k: k.unsqueeze(1).to_broadcast([P, H3, TC])
    us, ud = tmp[:, 2:2 + H3, :], raw[:, 2:2 + H3, :]
    step(tt(us, raw[:, 7:7 + H3, :], heads(A), ALU.mult))
    step(tt(ud, ud, heads(B), ALU.mult))
    step(tt(us, us, ud, ALU.subtract))
    step(stt(score[:, :, :], us, 0.2, us, ALU.mult, ALU.max))


def layer_norm(dve, step, m, y, sq, st, ask, answered):
    mean, var, rstd = (st[:, k, :].unsqueeze(2) for k in range(3))
    step(dve.tensor_reduce(mean, y[:, :, :], AX.X, ALU.add))
    step(dve.tensor_scalar(mean, mean, 1.0 / D, None, ALU.mult))
    step(dve.tensor_tensor(y[:, :, :], y[:, :, :], mean.to_broadcast([P, NB, D]), ALU.subtract))
    step(dve.tensor_tensor(sq[:, :, :], y[:, :, :], y[:, :, :], ALU.mult))
    step(dve.tensor_reduce(var, sq[:, :, :], AX.X, ALU.add))
    step(dve.tensor_scalar(var, var, 1.0 / D, EPS, ALU.mult, ALU.add))
    dve.nop(nofuse=True).then_inc(ask, 1)
    dve.wait_ge(*answered)
    step(dve.reciprocal(rstd, var))
    step(dve.tensor_tensor(m.x[:, :, :], y[:, :, :], rstd.to_broadcast([P, NB, D]), ALU.mult))


def finish0(nc, io, m):
    with ExitStack() as ctx:
        sb = lambda n, s, dt=F32: ctx.enter_context(nc.sbuf_tensor("f0_" + n, s, dt))
        sem = m.stage_sems()
        y, sq = sb("y", [P, NB, D]), sb("sq", [P, NB, D])
        w, sj, pr = sb("w", [P, D]), sb("sj", [P, NB]), sb("pr", [P, NB, D])
        st = sb("st", [P, 12, NB])
        w_in, step_sem, ask, ans = sem("w_in"), sem("step"), sem("ask"), sem("answered")
        block = ctx.enter_context(nc.Block())

        @block.sync
        def _(sp):
            sp.dma_start(w[:, :], io["wij"][1:2, :].to_broadcast([P, D])).then_inc(w_in, 16)

        @block.scalar
        def _(act):
            act.wait_ge(ask, 1)
            act.activation(st[:, 6:8, :], st[:, 4:6, :], ACT.Exp).then_inc(ans, 1)
            act.wait_ge(ask, 2)
            act.activation(st[:, 1, :], st[:, 1, :], ACT.Sqrt).then_inc(ans, 1)

        @block.vector
        def _(dve):
            step = Steps(dve, step_sem)
            dve.wait_ge(w_in, 16)
            acc = m.acc[:, 0:NB, :]
            own, most, top = st[:, 8, :], st[:, 9, :], st[:, 10, :]
            step(dve.tensor_tensor(pr[:, :, :], m.x[:, :, :], w[:, :].unsqueeze(1).to_broadcast([P, NB, D]), ALU.mult))
            step(dve.tensor_reduce(own.unsqueeze(2), pr[:, :, :], AX.X, ALU.add))
            step(dve.tensor_tensor(own, own, m.spread[:, 0:NB, 0], ALU.add))
            step(dve.scalar_tensor_tensor(own, own, 0.01, own, ALU.mult, ALU.max))
            step(dve.tensor_scalar(most, acc[:, :, D + 2], BIG, -BIG, ALU.mult, ALU.add))
            step(dve.tensor_tensor(most, most, acc[:, :, D + 1], ALU.add))
            step(dve.tensor_tensor(top, most, own, ALU.max))
            step(dve.tensor_tensor(st[:, 4, :], most, top, ALU.subtract))
            step(dve.tensor_tensor(st[:, 5, :], own, top, ALU.subtract))
            step(dve.tensor_scalar(st[:, 4:6, :], st[:, 4:6, :], -200.0, None, ALU.max))
            dve.nop(nofuse=True).then_inc(ask, 1)
            dve.wait_ge(ans, 1)
            fac, one = st[:, 6, :], st[:, 7, :]
            den = st[:, 11, :]
            step(dve.tensor_tensor(den, acc[:, :, D], fac, ALU.mult))
            step(dve.tensor_tensor(den, den, one, ALU.add))
            step(dve.reciprocal(den, den))
            step(dve.tensor_tensor(fac, fac, den, ALU.mult))
            step(dve.tensor_tensor(one, one, den, ALU.mult))
            step(dve.tensor_tensor(y[:, :, :], acc[:, :, 0:D], fac.unsqueeze(2).to_broadcast([P, NB, D]), ALU.mult))
            step(dve.tensor_tensor(sq[:, :, :], m.x[:, :, :], one.unsqueeze(2).to_broadcast([P, NB, D]), ALU.mult))
            step(dve.tensor_tensor(y[:, :, :], y[:, :, :], sq[:, :, :], ALU.add))
            step(dve.scalar_tensor_tensor(y[:, :, :], y[:, :, :], 0.0, m.x[:, :, :], ALU.max, ALU.add))
            layer_norm(dve, step, m, y, sq, st, ask, (ans, 2))


def finish_linear(nc, io, m, l):
    c = CONVS[l]
    H, B = c.H, c.B
    with ExitStack() as ctx:
        sb = lambda n, s, dt=F32: ctx.enter_context(nc.sbuf_tensor(f"f{l}_" + n, s, dt))
        sem = m.stage_sems()
        y, sq = sb("y", [P, NB, D]), sb("sq", [P, NB, D])
        st, den = sb("st", [P, 3, NB]), sb("den", [P, NB, H])
        step_sem, ask, ans = sem("step"), sem("ask"), sem("answered")
        block = ctx.enter_context(nc.Block())

        @block.scalar
        def _(act):
            if l != 1:
                act.wait_ge(ask, 1)
                act.activation(st[:, 1, :], st[:, 1, :], ACT.Sqrt).then_inc(ans, 1)

        @block.vector
        def _(dve):
            step = Steps(dve, step_sem)
            acc = m.acc[:, 0:NB, 0:c.PW].rearrange("p n (h b) -> p n h b", h=H)
            step(dve.tensor_scalar(den[:, :, :], acc[:, :, :, B - 1], 1.0e-20, None, ALU.max))
            step(dve.reciprocal(den[:, :, :], den[:, :, :]))
            step(dve.tensor_tensor(y[:, :, :].rearrange("p n (h b) -> p n h b", h=H), acc[:, :, :, 0:B - 1],
                                   den[:, :, :].unsqueeze(3).to_broadcast([P, NB, H, B - 1]), ALU.mult))
            step(dve.tensor_tensor(y[:, :, :], y[:, :, :], m.skip[:, :, :], ALU.add))
            if l == 1:
                step(dve.tensor_scalar(m.skip[:, :, :], y[:, :, :], 0.0, None, ALU.max))
                return
            step(dve.tensor_tensor(y[:, :, :], y[:, :, :], m.x[:, :, :], ALU.add))
            layer_norm(dve, step, m, y, sq, st, ask, (ans, 1))


ATANH_TERMS = [1.0 / (2 * k + 1) for k in range(9)]


def atanh_ratio(dve, step, t, lo, up, u, poly, out, ask, answered):
    dve.nop(nofuse=True).then_inc(ask, 1)
    step(dve.tensor_tensor(u, t, t, ALU.mult))
    step(dve.tensor_scalar(poly, u, ATANH_TERMS[-1], None, ALU.mult))
    for a in ATANH_TERMS[-2:0:-1]:
        step(dve.scalar_tensor_tensor(poly, poly, a, u, ALU.add, ALU.mult))
    step(dve.tensor_scalar(poly, poly, ATANH_TERMS[0], None, ALU.add))
    dve.wait_ge(*answered)
    step(dve.tensor_tensor(up, up, lo, ALU.subtract))
    step(dve.reciprocal(lo, t))
    step(dve.scalar_tensor_tensor(up, up, 0.5, lo, ALU.mult, ALU.mult))
    step(dve.tensor_scalar(u, t, 0.25, None, ALU.is_lt))
    step(dve.tensor_tensor(poly, poly, up, ALU.subtract))
    step(dve.tensor_tensor(poly, poly, u, ALU.mult))
    step(dve.tensor_tensor(out, up, poly, ALU.add))


CURV, MIN_NORM, TOP = 0.01, 1e-10, 1.0 - 1e-5
ROOT_C = 0.1


def prep4(nc, io, m):
    c = CONVS[4]
    W, PW = c.W, c.PW
    RH, RP = R_ * H3, R_ // 2
    M = RP * H3
    PIECES = 2 * NB
    with ExitStack() as ctx:
        sb = lambda n, s, dt=F32: ctx.enter_context(nc.sbuf_tensor("p4_" + n, s, dt))
        sem = m.stage_sems()
        w, rest_w, av = sb("w", [2 * D, RH * D]), sb("rest_w", [2 * D, RH * D]), sb("av", [D, RH])
        wp = sb("wp", [2 * D, 3, RH * D], BF16)
        ht, rest = sb("ht", [P, NB, D]), sb("rest", [P, NB, D])
        hp = sb("hp", [P, NB, 2, 2, D], BF16)
        ident_b = sb("ident_b", [P, P], BF16)
        st = sb("st", [P, 8, NB])
        hts = sb("hts", [2 * D, NB, 2, P], BF16)
        xts = sb("xts", [D, 2, P])
        rb = sb("rb", [P, 2, R_, W])
        sq = sb("sq", [P, 2, M * D])
        msg_n2, norms, ths, lams, facs = (sb(n, [P, NB * RH]) for n in ("msg_n2", "norms", "ths", "lams", "facs"))
        ohr = sb("ohr", [P, R_ * R_], I32)
        w_in, step_sem, ask, ans, ready = sem("w_in"), sem("step"), sem("ask"), sem("answered"), sem("ready")
        turned, moved, scores, copied = sem("turned"), sem("moved"), sem("scores"), sem("copied")
        product, squared, summed = sem("product"), sem("squared"), sem("summed")
        factored, scaled, filled, framed = sem("factored"), sem("scaled"), sem("filled"), sem("framed")
        row_out = [sem("row_out0"), sem("row_out1")]
        block = ctx.enter_context(nc.Block())

        def bank(i, k):
            return m.bank[2 + 2 * (i % 3) + k]

        @block.sync
        def _(sp):
            for k in range(2):
                sp.dma_start(w[k * D:(k + 1) * D, :], io["Wrel"]).then_inc(w_in, 16)
            sp.dma_start(av[:, :], io["AV"]).then_inc(w_in, 16)
            tab = m.table[4].rearrange("(b p r) w -> b p (r w)", p=P, r=R_)
            for b in range(NB):
                sp.wait_ge(scaled, 2 * b + 2)
                sp.wait_ge(filled, b + 1)
                sp.dma_start(tab[b], rb[:, b % 2, :, :].rearrange("p r w -> p (r w)")).then_inc(row_out[b % 2], 16)
            sp.wait_ge(row_out[0], 16 * ((NB + 1) // 2))
            sp.wait_ge(row_out[1], 16 * (NB // 2))

        @block.gpsimd
        def _(pool):
            step = Steps(pool, ready)
            step(pool.iota(ohr[:, :], [[-1, R_], [1, R_]], base=0, channel_multiplier=0))
            step(pool.memset(m.spread[:, NB:NB + 1, :], 0.0))
            pool.wait_ge(w_in, 48)
            step(pool.tensor_copy(wp[:, 0, :], w[:, :]))
            step(pool.tensor_tensor(rest_w[:, :], w[:, :], wp[:, 0, :], ALU.subtract))
            step(pool.tensor_copy(wp[:, 1, :], rest_w[:, :]))
            step(pool.tensor_tensor(rest_w[0:D, :], rest_w[0:D, :], wp[0:D, 1, :], ALU.subtract))
            step(pool.tensor_copy(wp[0:D, 2, :], rest_w[0:D, :]))
            step(pool.tensor_copy(wp[D:2 * D, 2, :], w[D:2 * D, :]))
            pool.wait_ge(framed, 1)
            pool.wait_ge(factored, 1)
            for b in range(NB):
                row = rb[:, b % 2, :, :]
                if b >= 2:
                    pool.wait_ge(row_out[b % 2], 16 * (b // 2))
                pool.wait_ge(copied, b + 1)
                pool.tensor_copy(row[:, :, PW:PW + D], m.x[:, b:b + 1, :].to_broadcast([P, R_, D]))
                pool.tensor_copy(row[:, :, PW + D:PW + D + 1], m.spread[:, b:b + 1, D + RH:D + RH + 1].to_broadcast([P, R_, 1]))
                pool.tensor_copy(row[:, :, PW + D + 1:PW + D + 1 + H3],
                                 m.spread[:, b, D:D + RH].rearrange("p (r h) -> p r h", h=H3))
                pool.tensor_copy(row[:, :, 0:PW].rearrange("p r (h k) -> p r h k", h=H3)[:, :, :, D],
                                 lams[:, b * RH:(b + 1) * RH].rearrange("p (r h) -> p r h", h=H3)).then_inc(filled, 1)

        @block.scalar
        def _(act):
            act.wait_ge(ask, 1)
            act.activation(st[:, 1, :], st[:, 0, :], ACT.Sqrt).then_inc(ans, 1)
            act.wait_ge(ask, 2)
            act.activation(st[:, 3, :], st[:, 2, :], ACT.Ln, bias=1.0)
            act.activation(st[:, 4, :], st[:, 2, :], ACT.Ln, bias=1.0, scale=-1.0).then_inc(ans, 1)

            def move(b):
                act.wait_ge(turned, b + 1)
                if b >= 2:
                    act.wait_ge(scores, b - 1)
                act.copy(hts[:, b, :, :].rearrange("d k p -> d (k p)"), m.bank[0][:, 0:2 * P])
                act.copy(xts[:, b % 2, :], m.bank[0][0:D, 2 * P:3 * P]).then_inc(moved, 1)
            move(0)
            for i in range(PIECES):
                b = i // 2
                if i % 2 == 0:
                    if b < NB - 1:
                        move(b + 1)
                    act.wait_ge(scores, b + 1)
                    act.copy(m.spread[:, b, D:D + RH], m.bank[1][:, 0:RH]).then_inc(copied, 1)
                act.wait_ge(product, i + 1)
                if i >= 2:
                    act.wait_ge(summed, i - 1)
                for k in range(2):
                    ins = act.activation(sq[:, i % 2, k * 512:(k + 1) * 512], bank(i, k)[:, :], ACT.Square)
                ins.then_inc(squared, 1)
            act.wait_ge(ask, 4)
            act.activation(norms[:, :], msg_n2[:, :], ACT.Sqrt).then_inc(ans, 1)
            act.wait_ge(ask, 5)
            act.activation(ths[:, :], norms[:, :], ACT.Tanh).then_inc(ans, 1)

        @block.tensor
        def _(pe):
            def turn_bucket(b):
                if b:
                    pe.wait_ge(moved, b)
                for k in range(2):
                    pe.matmul(m.bank[0][:, k * P:(k + 1) * P], hp[:, b, k, :, :].rearrange("p k d -> p (k d)"),
                              ident_b[:, :], start=True, stop=True)
                pe.transpose(m.bank[0][0:D, 2 * P:3 * P], m.x[:, b, :], m.ident[:, :]).then_inc(turned, 1)

            def messages(i):
                if 3 <= i < PIECES + 3:
                    pe.wait_ge(squared, i - 2)
                if i >= PIECES + 3:
                    pe.wait_ge(scaled, i - PIECES - 2)
                for k in range(2):
                    at = (i % 2 * 2 + k) * 512
                    for part in range(3):
                        mm = pe.matmul(bank(i, k)[:, :], hts[:, i % PIECES // 2, part // 2, :], wp[:, part, at:at + 512],
                                       start=(part == 0), stop=(part == 2))
                mm.then_inc(product, 1)
            pe.wait_ge(w_in, 48)
            pe.wait_ge(ready, 8)
            pe.wait_ge(ask, 3)
            turn_bucket(0)
            for b in range(NB):
                if b < NB - 1:
                    turn_bucket(b + 1)
                pe.wait_ge(moved, b + 1)
                if b:
                    pe.wait_ge(copied, b)
                pe.matmul(m.bank[1][:, 0:RH], xts[:, b % 2, :], av[:, :], start=True, stop=True).then_inc(scores, 1)
                messages(2 * b)
                messages(2 * b + 1)
            for i in range(PIECES):
                messages(PIECES + i)

        @block.vector
        def _(dve):
            step = Steps(dve, step_sem)
            n2, nrm, t, up, lo, u, poly, ratio = (st[:, k, :] for k in range(8))
            ts, tt = dve.tensor_scalar, dve.tensor_tensor
            step(tt(ht[:, :, :], m.x[:, :, :], m.x[:, :, :], ALU.mult))
            step(dve.tensor_reduce(n2.unsqueeze(2), ht[:, :, :], AX.X, ALU.add))
            step(dve.tensor_copy(m.spread[:, 0:NB, D + RH], n2))
            step(ts(n2, n2, 1e-30, None, ALU.max))
            dve.nop(nofuse=True).then_inc(ask, 1)
            step(dve.tensor_copy(m.spread[:, 0:NB, 0:D], m.x[:, :, :]))
            dve.wait_ge(ans, 1)
            step(ts(nrm, nrm, MIN_NORM, None, ALU.max))
            step(ts(t, nrm, ROOT_C, MIN_NORM, ALU.mult, ALU.max))
            step(ts(t, t, TOP, None, ALU.min))
            atanh_ratio(dve, step, t, lo, up, u, poly, ratio, ask, (ans, 2))
            step(tt(ht[:, :, :], m.x[:, :, :], ratio.unsqueeze(2).to_broadcast([P, NB, D]), ALU.mult))
            step(dve.tensor_copy(ident_b[:, :], m.ident[:, :]))
            step(dve.tensor_copy(hp[:, :, 0, 0, :], ht[:, :, :]))
            step(dve.tensor_copy(hp[:, :, 1, 0, :], ht[:, :, :]))
            step(tt(rest[:, :, :], ht[:, :, :], hp[:, :, 0, 0, :], ALU.subtract))
            step(dve.tensor_copy(hp[:, :, 0, 1, :], rest[:, :, :]))
            step(tt(rest[:, :, :], rest[:, :, :], hp[:, :, 0, 1, :], ALU.subtract))
            step(dve.tensor_copy(hp[:, :, 1, 1, :], rest[:, :, :]))
            dve.nop(nofuse=True).then_inc(ask, 1)
            dve.wait_ge(ready, 1)
            for s in range(2):
                step(ts(rb[:, s, :, W - R_:W], ohr[:, :].rearrange("p (r k) -> p r k", r=R_), 0.0, None, ALU.is_equal))
                ones = rb[:, s, :, 0:PW].rearrange("p r (h k) -> p r h k", h=H3)[:, :, :, B3 - 1:B3]
                step(dve.memset(ones, 1.0))
            dve.nop(nofuse=True).then_inc(framed, 1)
            for i in range(PIECES):
                dve.wait_ge(squared, i + 1)
                dve.tensor_reduce(msg_n2[:, i * M:(i + 1) * M].unsqueeze(2), sq[:, i % 2, :].rearrange("p (q o) -> p q o", o=D),
                                  AX.X, ALU.add).then_inc(summed, 1)
            dve.wait_ge(summed, PIECES)
            n2s, t, th, lam, fac = (k[:, :] for k in (msg_n2, norms, ths, lams, facs))
            step(ts(n2s, n2s, 1e-30, None, ALU.max))
            dve.nop(nofuse=True).then_inc(ask, 1)
            dve.wait_ge(ans, 3)
            step(ts(t, t, MIN_NORM, ROOT_C, ALU.max, ALU.mult))
            dve.nop(nofuse=True).then_inc(ask, 1)
            step(dve.reciprocal(fac, t))
            dve.wait_ge(ans, 4)
            step(tt(fac, th, fac, ALU.mult))
            step(tt(lam, fac, fac, ALU.mult))
            step(tt(lam, lam, n2s, ALU.mult))
            step(ts(lam, lam, -CURV, 1.0, ALU.mult, ALU.add))
            step(ts(lam, lam, 1e-6, 0.5, ALU.add, ALU.mult))
            step(dve.reciprocal(lam, lam))
            step(tt(fac, fac, lam, ALU.mult))
            dve.nop(nofuse=True).then_inc(factored, 1)
            for i in range(PIECES):
                dve.wait_ge(product, PIECES + i + 1)
                if i >= 4:
                    dve.wait_ge(row_out[i // 2 % 2], 16 * (i // 4))
                blocks = rb[:, i // 2 % 2, i % 2 * RP:(i % 2 + 1) * RP, 0:PW].rearrange("p r (h k) -> p r h k", h=H3)
                scale = fac[:, i * M:(i + 1) * M].rearrange("p (r h) -> p r h", h=H3)
                for k in range(2):
                    ins = tt(blocks[:, 2 * k:2 * k + 2, :, 0:D],
                             bank(PIECES + i, k)[:, :].rearrange("p (r h o) -> p r h o", r=2, h=H3),
                             scale[:, 2 * k:2 * k + 2, :].unsqueeze(3).to_broadcast([P, 2, H3, D]), ALU.mult)
                ins.then_inc(scaled, 1)


def finish4(nc, io, m):
    NH = NB * H3
    with ExitStack() as ctx:
        sb = lambda n, s, dt=F32: ctx.enter_context(nc.sbuf_tensor("f4_" + n, s, dt))
        sem = m.stage_sems()
        y, sq, st = sb("y", [P, NB, D]), sb("sq", [P, NB, D]), sb("st", [P, 8, NB])
        mid, mq, a = sb("mid", [P, NH, D]), sb("mq", [P, NH, D]), sb("a", [P, 11, NH])
        step_sem, ask, ans, out_sem = sem("step"), sem("ask"), sem("answered"), sem("out")
        block = ctx.enter_context(nc.Block())

        @block.scalar
        def _(act):
            act.wait_ge(ask, 1)
            act.activation(a[:, 3, :], a[:, 2, :], ACT.Sqrt).then_inc(ans, 1)
            act.wait_ge(ask, 2)
            act.activation(a[:, 6, :], a[:, 5, :], ACT.Ln, bias=1.0)
            act.activation(a[:, 7, :], a[:, 5, :], ACT.Ln, bias=1.0, scale=-1.0).then_inc(ans, 1)
            act.wait_ge(ask, 3)
            act.activation(st[:, 1, :], st[:, 0, :], ACT.Sqrt).then_inc(ans, 1)
            act.wait_ge(ask, 4)
            act.activation(st[:, 3, :], st[:, 2, :], ACT.Tanh).then_inc(ans, 1)
            act.wait_ge(ask, 5)
            act.activation(st[:, 1, :], st[:, 1, :], ACT.Sqrt).then_inc(ans, 1)

        @block.vector
        def _(dve):
            step = Steps(dve, step_sem)
            ts, tt = dve.tensor_scalar, dve.tensor_tensor
            acc = m.acc[:, 0:NB, :].rearrange("p n (h b) -> p (n h) b", h=H3)
            rz, den, n2, nrm, p, t, up, lo, u, poly, f = (a[:, k, :] for k in range(11))
            wide = lambda k: k.unsqueeze(2).to_broadcast([P, NH, D])
            step(ts(rz, acc[:, :, D + 1], 1e-20, None, ALU.max))
            step(dve.reciprocal(rz, rz))
            step(tt(den, acc[:, :, D], rz, ALU.mult))
            step(ts(den, den, 1e-6, None, ALU.add))
            step(dve.reciprocal(den, den))
            step(tt(rz, rz, den, ALU.mult))
            step(tt(mid[:, :, :], acc[:, :, 0:D], wide(rz), ALU.mult))
            step(tt(mq[:, :, :], mid[:, :, :], mid[:, :, :], ALU.mult))
            step(dve.tensor_reduce(n2.unsqueeze(2), mq[:, :, :], AX.X, ALU.add))
            step(ts(n2, n2, 1e-30, None, ALU.max))
            dve.nop(nofuse=True).then_inc(ask, 1)
            dve.wait_ge(ans, 1)
            step(ts(nrm, nrm, MIN_NORM, None, ALU.max))
            step(dve.reciprocal(p, nrm))
            step(ts(p, p, TOP / ROOT_C, 1.0, ALU.mult, ALU.min))
            step(tt(t, nrm, p, ALU.mult))
            step(ts(t, t, MIN_NORM, ROOT_C, ALU.max, ALU.mult))
            step(ts(t, t, MIN_NORM, TOP, ALU.max, ALU.min))
            atanh_ratio(dve, step, t, lo, up, u, poly, f, ask, (ans, 2))
            step(tt(f, f, p, ALU.mult))
            step(ts(f, f, 1.0 / H3, None, ALU.mult))
            step(tt(mid[:, :, :], mid[:, :, :], wide(f), ALU.mult))
            step(dve.tensor_reduce(y[:, :, :], mid[:, :, :].rearrange("p (n h) d -> p n d h", h=H3), AX.X, ALU.add))
            n2, nrm, t, th, f = (st[:, k, :] for k in range(5))
            step(tt(sq[:, :, :], y[:, :, :], y[:, :, :], ALU.mult))
            step(dve.tensor_reduce(n2.unsqueeze(2), sq[:, :, :], AX.X, ALU.add))
            step(ts(n2, n2, 1e-30, None, ALU.max))
            dve.nop(nofuse=True).then_inc(ask, 1)
            dve.wait_ge(ans, 3)
            step(ts(t, nrm, MIN_NORM, ROOT_C, ALU.max, ALU.mult))
            dve.nop(nofuse=True).then_inc(ask, 1)
            step(dve.reciprocal(f, t))
            dve.wait_ge(ans, 4)
            step(tt(f, th, f, ALU.mult))
            step(tt(y[:, :, :], y[:, :, :], f.unsqueeze(2).to_broadcast([P, NB, D]), ALU.mult))
            step(tt(y[:, :, :], y[:, :, :], m.x[:, :, :], ALU.add))
            layer_norm(dve, step, m, y, sq, st, ask, (ans, 5))
            dve.nop(nofuse=True).then_inc(ask, 1)

        @block.sync
        def _(sp):
            sp.wait_ge(ask, 6)
            out = io["out"]
            sp.dma_start(out[0:NFULL * P, :].rearrange("(b p) d -> p b d", p=P), m.x[:, 0:NFULL, :]).then_inc(out_sem, 16)
            sp.dma_start(out[NFULL * P:N, :], m.x[0:NREST, NFULL, :]).then_inc(out_sem, 16)
            sp.wait_ge(out_sem, 32)


def kernel(**inputs):
    import numpy as _np
    import concourse.bacc as _bacc
    from concourse import mybir as _mybir
    from concourse.bass_utils import run_bass_kernel_spmd as _run

    i = {k: _np.asarray(v) for k, v in inputs.items()}
    cat = _np.concatenate

    def packed(prefix, suffix, turned):
        w = [i[f"{prefix}_W{n}{suffix}"] for n in "qkvs"]
        b = [i[f"{prefix}_b{n}{suffix}"] for n in "qkvs"]
        return cat([cat([k.T if turned else k for k in w], axis=1), cat(b)[None, :]], axis=0)

    arrays = {
        "x": i["x"], "src": i["src"], "dst": i["dst"], "edge_type_8": i["edge_type_8"],
        "wij": _np.stack([i["L0_gnn_w_i"], i["L0_gnn_w_j"]]),
        "W1": packed("L1_gnn", "1", True), "W2": packed("L1_gnn", "2", True), "W3": packed("L2_gnn", "", False),
        "Wrel": i["L3_gnn_rel_weight"].transpose(2, 0, 1, 3).reshape(64, -1),
        "AV": i["L3_gnn_attn_vec"].transpose(2, 0, 1).reshape(64, -1),
    }
    arrays = {f"in_{k}": _np.ascontiguousarray(v) for k, v in arrays.items()}
    nc = _bacc.Bacc("TRN2", target_bir_lowering=False, num_devices=1)
    io = {k[3:]: nc.dram_tensor(k, v.shape, _mybir.dt.from_np(v.dtype), kind="ExternalInput").ap()
          for k, v in arrays.items()}
    io["out"] = nc.dram_tensor("out_x", (3125, 64), _mybir.dt.float32, kind="ExternalOutput").ap()
    build(nc, io)
    r = _run(nc, [arrays], core_ids=[0])
    return r.results[0]["out_x"]
```
